# Optimizing a Trainium2 kernel written in Bass

```python
import numpy as np
import jax
import jax.numpy as jnp

def _softmax(x, axis=-1):
    return jax.nn.softmax(x, axis=axis)

def _gelu(x):
    return jax.nn.gelu(x, approximate=True)

def _silu(x):
    return jax.nn.silu(x)

def _sigmoid(x):
    return jax.nn.sigmoid(x)

def _layernorm(x, axis=-1, eps=1e-05):
    m = jnp.mean(x, axis=axis, keepdims=True)
    v = jnp.var(x, axis=axis, keepdims=True)
    return (x - m) / jnp.sqrt(v + eps)

def _scatter_add(tgt, idx, src, axis=0):
    return tgt.at[idx].add(src)

def _segment_sum(src, seg, n):
    return jax.ops.segment_sum(src, seg, n)
kernel_name = 'mk_perceiver_d1_seqx_r2_de0d68'

def setup_inputs(seed: int=0):
    np.random.seed(seed)
    _w = jnp.asarray

    def _rec_inputs():
        import jax
        import jax.numpy as jnp
        _rk = jax.random.key(seed)
        x = 7.22e-05 + 1 * jax.random.normal(jax.random.fold_in(_rk, 1), (8, 128, 512), jnp.float32)
        _lenS = 128 - jax.random.randint(jax.random.fold_in(_rk, 7), (8,), 0, max(1, 128 // 4) + 1, jnp.int32)
        _lenS2 = 2048 - jax.random.randint(jax.random.fold_in(_rk, 8), (8,), 0, max(1, 2048 // 4) + 1, jnp.int32)
        _ctx_1024P = jax.random.normal(jax.random.fold_in(_rk, 11), (8, 16, 512), jnp.float32)
        _ctx_1024c = jax.random.dirichlet(jax.random.fold_in(_rk, 511), 0.3 * jnp.ones((16,), jnp.float32), (8, 2048))
        _ctx_1024t = jnp.einsum('bsk,bkd->bsd', _ctx_1024c, _ctx_1024P)
        _ctx_1024t = _ctx_1024t * jax.lax.rsqrt(jnp.mean(jnp.square(_ctx_1024t)) + 1e-12) * 0.953939
        ctx_1024 = 4.13588e-05 + 0.999923 * (_ctx_1024t + 0.3 * jax.random.normal(jax.random.fold_in(_rk, 611), (8, 2048, 512), jnp.float32))
        return (x, ctx_1024)
    x, ctx_1024 = _rec_inputs()

    def _L0_xattn_setup():
        import jax, jax.numpy as jnp
        import numpy as np
        D_MODEL = 512
        NUM_HEADS = 16
        HEAD_DIM = D_MODEL // NUM_HEADS
        key = jax.random.key(seed)
        ks = jax.random.split(key, 10)
        B, SQ, SKV = (4, 1024, 1024)
        s = 1.0 / np.sqrt(D_MODEL)
        return {'query': jax.random.normal(ks[0], (B, SQ, D_MODEL), jnp.float32), 'key_value': jax.random.normal(ks[1], (B, SKV, D_MODEL), jnp.float32), 'Wq': jax.random.normal(ks[2], (D_MODEL, D_MODEL), jnp.float32) * s, 'bq': jnp.zeros((D_MODEL,), jnp.float32), 'Wk': jax.random.normal(ks[3], (D_MODEL, D_MODEL), jnp.float32) * s, 'bk': jnp.zeros((D_MODEL,), jnp.float32), 'Wv': jax.random.normal(ks[4], (D_MODEL, D_MODEL), jnp.float32) * s, 'bv': jnp.zeros((D_MODEL,), jnp.float32), 'Wo': jax.random.normal(ks[5], (D_MODEL, D_MODEL), jnp.float32) * s, 'bo': jnp.zeros((D_MODEL,), jnp.float32)}
    _L0_xattn_all = _L0_xattn_setup()
    _L0_xattn_in = {k: v for k, v in _L0_xattn_all.items() if k in ('Wq', 'bq', 'Wk', 'bk', 'Wv', 'bv', 'Wo', 'bo')}
    del _L0_xattn_all

    def _L0_attn_setup():
        import jax, jax.numpy as jnp
        import numpy as np
        HID = 512
        DIN = 1024
        N = 16
        DTR = 64
        TW = 4

        def _causal_conv(xc, w_conv, b_conv):
            b, l, d = xc.shape
            xp = jnp.pad(xc, ((0, 0), (TW - 1, 0), (0, 0)))
            y = b_conv
            for k in range(TW):
                y = y + xp[:, k:k + l, :] * w_conv[k]
            return y

        def _forward(x, w_in, b_in, w_conv, b_conv, w_x, w_dt, A_log, D, w_out):
            b, l, _ = x.shape
            xr = x @ w_in + b_in
            xc, res = jnp.split(xr, 2, axis=-1)
            u = jax.nn.silu(_causal_conv(xc, w_conv, b_conv))
            A = -jnp.exp(A_log)
            x_dbl = u @ w_x
            dt, B, C = jnp.split(x_dbl, [DTR, DTR + N], axis=-1)
            delta = jax.nn.softplus(dt @ w_dt)
            deltaA = jnp.exp(delta[..., None] * A)
            deltaBu = delta[..., None] * B[:, :, None, :] * u[..., None]

            def step(h, ab):
                a, bu = ab
                h = a * h + bu
                return (h, h)
            a_t = jnp.moveaxis(deltaA, 1, 0)
            bu_t = jnp.moveaxis(deltaBu, 1, 0)
            h0 = jnp.zeros((b, DIN, N), dtype=x.dtype)
            _, hs = jax.lax.scan(step, h0, (a_t, bu_t))
            hs = jnp.moveaxis(hs, 0, 1)
            y = jnp.einsum('bldn,bln->bld', hs, C) + u * D
            return y * jax.nn.silu(res) @ w_out
        key = jax.random.key(seed)
        ks = jax.random.split(key, 10)
        s = lambda *shape: 1.0 / np.sqrt(shape[0])
        x = jax.random.normal(ks[0], (2, 1024, HID), dtype=jnp.float32)
        w_in = jax.random.normal(ks[1], (HID, 2 * DIN), dtype=jnp.float32) * s(HID)
        b_in = jax.random.normal(ks[2], (2 * DIN,), dtype=jnp.float32) * 0.02
        w_conv = jax.random.normal(ks[3], (TW, DIN), dtype=jnp.float32) * 0.5
        b_conv = jax.random.normal(ks[4], (DIN,), dtype=jnp.float32) * 0.02
        w_x = jax.random.normal(ks[5], (DIN, DTR + 2 * N), dtype=jnp.float32) * s(DIN)
        w_dt = jax.random.normal(ks[6], (DTR, DIN), dtype=jnp.float32) * s(DTR)
        A_log = jnp.log(jnp.broadcast_to(jnp.arange(1, N + 1, dtype=jnp.float32), (DIN, N)))
        D = jnp.ones((DIN,), dtype=jnp.float32)
        w_out = jax.random.normal(ks[7], (DIN, HID), dtype=jnp.float32) * s(DIN)
        return {'x': x, 'w_in': w_in, 'b_in': b_in, 'w_conv': w_conv, 'b_conv': b_conv, 'w_x': w_x, 'w_dt': w_dt, 'A_log': A_log, 'D': D, 'w_out': w_out}
    _L0_attn_all = _L0_attn_setup()
    _L0_attn_in = {k: v for k, v in _L0_attn_all.items() if k in ('w_in', 'b_in', 'w_conv', 'b_conv', 'w_x', 'w_dt', 'A_log', 'D', 'w_out')}
    del _L0_attn_all

    def _L0_ffn_setup():
        import jax, jax.numpy as jnp
        import numpy as np
        from jax import lax
        B, L, D = (4, 1024, 512)
        E, TOPK = (8, 2)
        K, DIL = (3, 1)
        HID = D // 4
        EPS = 1e-06

        def _rmsnorm(h, w):
            rms = jnp.sqrt(jnp.mean(h * h, axis=-1, keepdims=True) + EPS)
            return w * (h / rms)

        def _forward(x, dw_kernel, dw_bias, pw_w, pw_b, router_w, router_b, expert_w, expert_b, out_w, out_b, norm_w, ff_down_w, ff_down_b, ff_up_w, ff_up_b):
            pad = (K - 1) * DIL
            xc = jnp.transpose(x, (0, 2, 1))
            xc = lax.conv_general_dilated(xc, dw_kernel, window_strides=(1,), padding=((pad, 0),), rhs_dilation=(DIL,), dimension_numbers=('NCH', 'OIH', 'NCH'), feature_group_count=D) + dw_bias[None, :, None]
            xc = jax.nn.silu(jnp.einsum('bdl,ed->bel', xc, pw_w) + pw_b[None, :, None])
            x1 = x + jnp.transpose(xc, (0, 2, 1))
            logits = jnp.einsum('bsd,ed->bse', x1, router_w) + router_b
            top_v, top_i = lax.top_k(logits, TOPK)
            top_w = jax.nn.softmax(top_v, axis=-1)
            rw = jnp.sum(jax.nn.one_hot(top_i, E, dtype=x1.dtype) * top_w[..., None], axis=-2)
            ye = jax.nn.silu(jnp.einsum('bsd,eod->bseo', x1, expert_w) + expert_b)
            combined = jnp.einsum('bse,bseo->bso', rw, ye)
            moe_out = jnp.einsum('bsd,od->bso', combined, out_w) + out_b
            h = _rmsnorm(x1 + moe_out, norm_w)
            ff = jax.nn.gelu(jnp.einsum('bsd,hd->bsh', h, ff_down_w) + ff_down_b, approximate=False)
            ff = jnp.einsum('bsh,dh->bsd', ff, ff_up_w) + ff_up_b
            return h + ff
        key = jax.random.key(seed)
        ks = jax.random.split(key, 16)
        s = 0.02
        return {'x': jax.random.normal(ks[0], (B, L, D), dtype=jnp.float32), 'dw_kernel': jax.random.normal(ks[1], (D, 1, K), dtype=jnp.float32) * s, 'dw_bias': jnp.zeros((D,), dtype=jnp.float32), 'pw_w': jax.random.normal(ks[2], (D, D), dtype=jnp.float32) * s, 'pw_b': jnp.zeros((D,), dtype=jnp.float32), 'router_w': jax.random.normal(ks[3], (E, D), dtype=jnp.float32) * s, 'router_b': jnp.zeros((E,), dtype=jnp.float32), 'expert_w': jax.random.normal(ks[4], (E, D, D), dtype=jnp.float32) * s, 'expert_b': jnp.zeros((E, D), dtype=jnp.float32), 'out_w': jax.random.normal(ks[5], (D, D), dtype=jnp.float32) * s, 'out_b': jnp.zeros((D,), dtype=jnp.float32), 'norm_w': jnp.ones((D,), dtype=jnp.float32), 'ff_down_w': jax.random.normal(ks[6], (HID, D), dtype=jnp.float32) * s, 'ff_down_b': jnp.zeros((HID,), dtype=jnp.float32), 'ff_up_w': jax.random.normal(ks[7], (D, HID), dtype=jnp.float32) * s, 'ff_up_b': jnp.zeros((D,), dtype=jnp.float32)}
    _L0_ffn_all = _L0_ffn_setup()
    _L0_ffn_in = {k: v for k, v in _L0_ffn_all.items() if k in ('dw_kernel', 'dw_bias', 'pw_w', 'pw_b', 'router_w', 'router_b', 'expert_w', 'expert_b', 'out_w', 'out_b', 'norm_w', 'ff_down_w', 'ff_down_b', 'ff_up_w', 'ff_up_b')}
    del _L0_ffn_all
    return {'x': x, 'ctx_1024': ctx_1024, 'L0_xattn_Wq': _L0_xattn_in['Wq'], 'L0_xattn_bq': _L0_xattn_in['bq'], 'L0_xattn_Wk': _L0_xattn_in['Wk'], 'L0_xattn_bk': _L0_xattn_in['bk'], 'L0_xattn_Wv': _L0_xattn_in['Wv'], 'L0_xattn_bv': _L0_xattn_in['bv'], 'L0_xattn_Wo': _L0_xattn_in['Wo'], 'L0_xattn_bo': _L0_xattn_in['bo'], 'L0_attn_w_in': _L0_attn_in['w_in'], 'L0_attn_b_in': _L0_attn_in['b_in'], 'L0_attn_w_conv': _L0_attn_in['w_conv'], 'L0_attn_b_conv': _L0_attn_in['b_conv'], 'L0_attn_w_x': _L0_attn_in['w_x'], 'L0_attn_w_dt': _L0_attn_in['w_dt'], 'L0_attn_A_log': _L0_attn_in['A_log'], 'L0_attn_D': _L0_attn_in['D'], 'L0_attn_w_out': _L0_attn_in['w_out'], 'L0_ffn_dw_kernel': _L0_ffn_in['dw_kernel'], 'L0_ffn_dw_bias': _L0_ffn_in['dw_bias'], 'L0_ffn_pw_w': _L0_ffn_in['pw_w'], 'L0_ffn_pw_b': _L0_ffn_in['pw_b'], 'L0_ffn_router_w': _L0_ffn_in['router_w'], 'L0_ffn_router_b': _L0_ffn_in['router_b'], 'L0_ffn_expert_w': _L0_ffn_in['expert_w'], 'L0_ffn_expert_b': _L0_ffn_in['expert_b'], 'L0_ffn_out_w': _L0_ffn_in['out_w'], 'L0_ffn_out_b': _L0_ffn_in['out_b'], 'L0_ffn_norm_w': _L0_ffn_in['norm_w'], 'L0_ffn_ff_down_w': _L0_ffn_in['ff_down_w'], 'L0_ffn_ff_down_b': _L0_ffn_in['ff_down_b'], 'L0_ffn_ff_up_w': _L0_ffn_in['ff_up_w'], 'L0_ffn_ff_up_b': _L0_ffn_in['ff_up_b']}

def reference(x, ctx_1024, L0_xattn_Wq, L0_xattn_bq, L0_xattn_Wk, L0_xattn_bk, L0_xattn_Wv, L0_xattn_bv, L0_xattn_Wo, L0_xattn_bo, L0_attn_w_in, L0_attn_b_in, L0_attn_w_conv, L0_attn_b_conv, L0_attn_w_x, L0_attn_w_dt, L0_attn_A_log, L0_attn_D, L0_attn_w_out, L0_ffn_dw_kernel, L0_ffn_dw_bias, L0_ffn_pw_w, L0_ffn_pw_b, L0_ffn_router_w, L0_ffn_router_b, L0_ffn_expert_w, L0_ffn_expert_b, L0_ffn_out_w, L0_ffn_out_b, L0_ffn_norm_w, L0_ffn_ff_down_w, L0_ffn_ff_down_b, L0_ffn_ff_up_w, L0_ffn_ff_up_b):
    import jax
    import jax.numpy as jnp

    def _L0_xattn_ref(query, key_value, Wq, bq, Wk, bk, Wv, bv, Wo, bo):
        import jax, jax.numpy as jnp
        import numpy as np
        D_MODEL = 512
        NUM_HEADS = 16
        HEAD_DIM = D_MODEL // NUM_HEADS
        B, SQ, _ = query.shape
        SKV = key_value.shape[1]
        H, Dh = (NUM_HEADS, HEAD_DIM)
        Q = (query @ Wq.T + bq).reshape(B, SQ, H, Dh).transpose(0, 2, 1, 3)
        K = (key_value @ Wk.T + bk).reshape(B, SKV, H, Dh).transpose(0, 2, 1, 3)
        V = (key_value @ Wv.T + bv).reshape(B, SKV, H, Dh).transpose(0, 2, 1, 3)
        scale = jnp.asarray(np.sqrt(Dh), query.dtype)
        scores = jnp.einsum('bhqd,bhkd->bhqk', Q, K) / scale
        weights = jax.nn.softmax(scores, axis=-1)
        attn = jnp.einsum('bhqk,bhkd->bhqd', weights, V)
        attn = attn.transpose(0, 2, 1, 3).reshape(B, SQ, H * Dh)
        return attn @ Wo.T + bo

    def _L0_attn_ref(x, w_in, b_in, w_conv, b_conv, w_x, w_dt, A_log, D, w_out):
        import jax, jax.numpy as jnp
        import numpy as np
        HID = 512
        DIN = 1024
        N = 16
        DTR = 64
        TW = 4

        def _causal_conv(xc, w_conv, b_conv):
            b, l, d = xc.shape
            xp = jnp.pad(xc, ((0, 0), (TW - 1, 0), (0, 0)))
            y = b_conv
            for k in range(TW):
                y = y + xp[:, k:k + l, :] * w_conv[k]
            return y

        def _forward(x, w_in, b_in, w_conv, b_conv, w_x, w_dt, A_log, D, w_out):
            b, l, _ = x.shape
            xr = x @ w_in + b_in
            xc, res = jnp.split(xr, 2, axis=-1)
            u = jax.nn.silu(_causal_conv(xc, w_conv, b_conv))
            A = -jnp.exp(A_log)
            x_dbl = u @ w_x
            dt, B, C = jnp.split(x_dbl, [DTR, DTR + N], axis=-1)
            delta = jax.nn.softplus(dt @ w_dt)
            deltaA = jnp.exp(delta[..., None] * A)
            deltaBu = delta[..., None] * B[:, :, None, :] * u[..., None]

            def step(h, ab):
                a, bu = ab
                h = a * h + bu
                return (h, h)
            a_t = jnp.moveaxis(deltaA, 1, 0)
            bu_t = jnp.moveaxis(deltaBu, 1, 0)
            h0 = jnp.zeros((b, DIN, N), dtype=x.dtype)
            _, hs = jax.lax.scan(step, h0, (a_t, bu_t))
            hs = jnp.moveaxis(hs, 0, 1)
            y = jnp.einsum('bldn,bln->bld', hs, C) + u * D
            return y * jax.nn.silu(res) @ w_out
        return _forward(x, w_in, b_in, w_conv, b_conv, w_x, w_dt, A_log, D, w_out)

    def _L0_ffn_ref(x, dw_kernel, dw_bias, pw_w, pw_b, router_w, router_b, expert_w, expert_b, out_w, out_b, norm_w, ff_down_w, ff_down_b, ff_up_w, ff_up_b):
        import jax, jax.numpy as jnp
        import numpy as np
        from jax import lax
        B, L, D = (4, 1024, 512)
        E, TOPK = (8, 2)
        K, DIL = (3, 1)
        HID = D // 4
        EPS = 1e-06

        def _rmsnorm(h, w):
            rms = jnp.sqrt(jnp.mean(h * h, axis=-1, keepdims=True) + EPS)
            return w * (h / rms)

        def _forward(x, dw_kernel, dw_bias, pw_w, pw_b, router_w, router_b, expert_w, expert_b, out_w, out_b, norm_w, ff_down_w, ff_down_b, ff_up_w, ff_up_b):
            pad = (K - 1) * DIL
            xc = jnp.transpose(x, (0, 2, 1))
            xc = lax.conv_general_dilated(xc, dw_kernel, window_strides=(1,), padding=((pad, 0),), rhs_dilation=(DIL,), dimension_numbers=('NCH', 'OIH', 'NCH'), feature_group_count=D) + dw_bias[None, :, None]
            xc = jax.nn.silu(jnp.einsum('bdl,ed->bel', xc, pw_w) + pw_b[None, :, None])
            x1 = x + jnp.transpose(xc, (0, 2, 1))
            logits = jnp.einsum('bsd,ed->bse', x1, router_w) + router_b
            top_v, top_i = lax.top_k(logits, TOPK)
            top_w = jax.nn.softmax(top_v, axis=-1)
            rw = jnp.sum(jax.nn.one_hot(top_i, E, dtype=x1.dtype) * top_w[..., None], axis=-2)
            ye = jax.nn.silu(jnp.einsum('bsd,eod->bseo', x1, expert_w) + expert_b)
            combined = jnp.einsum('bse,bseo->bso', rw, ye)
            moe_out = jnp.einsum('bsd,od->bso', combined, out_w) + out_b
            h = _rmsnorm(x1 + moe_out, norm_w)
            ff = jax.nn.gelu(jnp.einsum('bsd,hd->bsh', h, ff_down_w) + ff_down_b, approximate=False)
            ff = jnp.einsum('bsh,dh->bsd', ff, ff_up_w) + ff_up_b
            return h + ff
        return _forward(x, dw_kernel, dw_bias, pw_w, pw_b, router_w, router_b, expert_w, expert_b, out_w, out_b, norm_w, ff_down_w, ff_down_b, ff_up_w, ff_up_b)
    x = x + _L0_xattn_ref(_layernorm(x, axis=-1), ctx_1024, L0_xattn_Wq, L0_xattn_bq, L0_xattn_Wk, L0_xattn_bk, L0_xattn_Wv, L0_xattn_bv, L0_xattn_Wo, L0_xattn_bo)
    x = x + _L0_attn_ref(_layernorm(x, axis=-1), L0_attn_w_in, L0_attn_b_in, L0_attn_w_conv, L0_attn_b_conv, L0_attn_w_x, L0_attn_w_dt, L0_attn_A_log, L0_attn_D, L0_attn_w_out)
    x = x + _L0_ffn_ref(_layernorm(x, axis=-1), L0_ffn_dw_kernel, L0_ffn_dw_bias, L0_ffn_pw_w, L0_ffn_pw_b, L0_ffn_router_w, L0_ffn_router_b, L0_ffn_expert_w, L0_ffn_expert_b, L0_ffn_out_w, L0_ffn_out_b, L0_ffn_norm_w, L0_ffn_ff_down_w, L0_ffn_ff_down_b, L0_ffn_ff_up_w, L0_ffn_ff_up_b)
    return x

_drawn_inputs = setup_inputs


def setup_inputs(seed=0):
    import zlib

    import numpy as np

    out = dict(_drawn_inputs(seed))
    spreads = {'L0_xattn_bq': (0.0, 0.369),
     'L0_xattn_bk': (0.0, 0.8),
     'L0_xattn_bv': (0.0, 0.1),
     'L0_xattn_bo': (0.0, 0.1),
     'L0_attn_D': (1.0, 0.2),
     'L0_ffn_dw_bias': (0.0, 0.7),
     'L0_ffn_pw_b': (0.0, 0.318),
     'L0_ffn_router_b': (0.0, 0.657),
     'L0_ffn_expert_b': (0.0, 0.8),
     'L0_ffn_out_b': (0.0, 0.1),
     'L0_ffn_norm_w': (1.0, 0.2),
     'L0_ffn_ff_down_b': (0.0, 0.8),
     'L0_ffn_ff_up_b': (0.0, 0.1)}
    factors = {'L0_attn_b_in': 3.681,
     'L0_attn_b_conv': 4.408,
     'L0_ffn_dw_kernel': 8.0,
     'L0_ffn_pw_w': 4.805}
    for name, (base, spread) in spreads.items():
        noise = np.random.default_rng([zlib.crc32(name.encode()), seed]).standard_normal(out[name].shape)
        drawn = base * np.exp(spread * noise) if base else spread * noise
        out[name] = jnp.asarray(drawn.astype(out[name].dtype))
    for name, factor in factors.items():
        out[name] = (out[name] * factor).astype(out[name].dtype)
    return out
```

```python
from contextlib import ExitStack

import concourse.bass as bass
from concourse import mybir

F32 = mybir.dt.float32
F32R = mybir.dt.float32r
U32 = mybir.dt.uint32
ALU = mybir.AluOpType
ACT = mybir.ActivationFunctionType
AX = mybir.AxisListType

P = 128
BANK = 512
B, L, D = 8, 128, 512
KC = D // P
T = B * L
SKV = 2048
H, DH = 16, 32
HG = P // DH
CH = SKV // BANK
KV = BANK // P
EPS = 1e-5


class Stage:

    def __init__(self, nc, ctx, prefix):
        self.nc, self.ctx, self.prefix = nc, ctx, prefix

    def sb(self, name, shape, dt=F32):
        return self.ctx.enter_context(self.nc.sbuf_tensor(f"{self.prefix}_{name}", shape, dt))

    def ps(self, name, shape):
        return self.ctx.enter_context(self.nc.psum_tensor(f"{self.prefix}_{name}", shape, F32))

    def sems(self, *names):
        return [self.ctx.enter_context(self.nc.semaphore(f"{self.prefix}_{n}")) for n in names]


def layer_norm_steps(eng, x, out, stats, mv, rstd, root_ready, var_ready, chain, done, b, base):
    eng.bn_stats(stats, x).then_inc(chain, 1)
    eng.wait_ge(chain, base + 1)
    eng.bn_aggr(mv, stats).then_inc(chain, 1)
    eng.wait_ge(chain, base + 2)
    eng.tensor_scalar(rstd, mv[:, 1:2], EPS, None, ALU.add).then_inc(var_ready, 1)
    eng.wait_ge(root_ready, b + 1)
    eng.reciprocal(rstd, rstd).then_inc(chain, 1)
    eng.wait_ge(chain, base + 3)
    eng.tensor_scalar(out, x, mv[:, 0:1], rstd, ALU.subtract, ALU.mult).then_inc(done, 1)


def queries(nc, x, wq_t, bq, ident_dram, q_scratch):
    with ExitStack() as ctx:
        st = Stage(nc, ctx, "q")
        xt = st.sb("x", [P, B, D])
        xn = st.sb("xn", [P, 2, D])
        xn_t = st.sb("xnT", [P, KC, T])
        w = st.sb("wq", [P, KC, D])
        bias = st.sb("bq", [P, KC])
        q_t = st.sb("qT", [P, B, KC, L])
        ident = st.sb("ident", [P, P])
        stats = st.sb("stats", [P, B, 6])
        mv = st.sb("mv", [P, B, 2])
        rstd = st.sb("rstd", [P, B])
        tp = st.ps("tp", [P, 2, BANK])
        qp = st.ps("qp", [P, 4, BANK])
        x_in, w_in, chain, var_ready, root_ready, normed, turned, copied, q_made, q_out, stored = st.sems(
            "x_in", "w_in", "chain", "var_ready", "root_ready", "normed", "turned", "copied", "q_made",
            "q_out", "stored")
        block = ctx.enter_context(nc.Block())

        @block.sync
        def _(sp):
            sp.dma_start(xt[:], x.rearrange("b l d -> l b d")).then_inc(x_in, 16)
            sp.dma_start(ident[:], ident_dram).then_inc(w_in, 16)
            sp.dma_start(w[:], wq_t).then_inc(w_in, 16)
            sp.dma_start(bias[:], bq).then_inc(w_in, 16)
            sp.wait_ge(q_out, 2 * KC)
            sp.dma_start(q_scratch.rearrange("b p m l -> p b m l"), q_t[:]).then_inc(stored, 16)
            sp.wait_ge(stored, 16)

        @block.scalar
        def _(act):
            for b in range(B):
                act.wait_ge(var_ready, b + 1)
                nc.scalar.activation(rstd[:, b:b + 1], rstd[:, b:b + 1], ACT.Sqrt).then_inc(root_ready, 1)

        @block.vector
        def _(dve):
            dve.wait_ge(x_in, 16)
            for b in range(B):
                if b >= 2:
                    dve.wait_ge(turned, b - 1)
                layer_norm_steps(dve, xt[:, b, :], xn[:, b % 2, :], stats[:, b, :], mv[:, b, :],
                                 rstd[:, b:b + 1], root_ready, var_ready, chain, normed, b, 3 * b)
                dve.wait_ge(turned, b + 1)
                dve.tensor_copy(xn_t[:, :, b * L:(b + 1) * L],
                                tp[:, b % 2, :].rearrange("p (k l) -> p k l", k=KC)).then_inc(copied, 1)
            dve.wait_ge(w_in, 48)
            for n in range(2 * KC):
                m, g = n // 2, n % 2
                dve.wait_ge(q_made, n + 1)
                dve.tensor_scalar(q_t[:, 4 * g:4 * g + 4, m, :],
                                  qp[:, n % 4, :].rearrange("p (b l) -> p b l", l=L),
                                  bias[:, m:m + 1], float(DH) ** -0.5, ALU.add, ALU.mult).then_inc(q_out, 1)

        @block.tensor
        def _(pe):
            pe.wait_ge(w_in, 48)
            for b in range(B):
                pe.wait_ge(normed, b + 1)
                if b >= 2:
                    pe.wait_ge(copied, b - 1)
                for k in range(KC):
                    mm = pe.transpose(tp[:, b % 2, k * L:(k + 1) * L], xn[:, b % 2, k * P:(k + 1) * P], ident[:])
                mm.then_inc(turned, 1)
            pe.wait_ge(copied, B)
            for n in range(2 * KC):
                m, g = n // 2, n % 2
                if n >= 4:
                    pe.wait_ge(q_out, n - 3)
                for k in range(KC):
                    mm = pe.matmul(qp[:, n % 4, :], w[:, k, m * P:(m + 1) * P], xn_t[:, k, g * BANK:(g + 1) * BANK],
                                   start=(k == 0), stop=(k == KC - 1))
                mm.then_inc(q_made, 1)


def attention(nc, ctx_t, wk_t, wv_t, bk, bv, ident_dram, q_scratch, a_scratch):
    with ExitStack() as ctx:
        st = Stage(nc, ctx, "a")
        raw = st.sb("raw", [P, KC, BANK])
        wk_hi, wk_lo = st.sb("wk_hi", [P, KC, D], F32R), st.sb("wk_lo", [P, KC, D], F32R)
        wv_hi, wv_lo = st.sb("wv_hi", [P, KC, D], F32R), st.sb("wv_lo", [P, KC, D], F32R)
        c_hi, c_lo = st.sb("c_hi", [P, 2, KC, BANK], F32R), st.sb("c_lo", [P, 2, KC, BANK], F32R)
        k_hi, k_lo = st.sb("k_hi", [P, KC, SKV], F32R), st.sb("k_lo", [P, KC, SKV], F32R)
        v = st.sb("v", [P, SKV // P, D])
        probs = st.sb("probs", [P, 2, SKV])
        pt = st.sb("pt", [P, 3, KV, L])
        q_t = st.sb("q_t", [P, KC, L])
        qb_hi, qb_lo = st.sb("qb_hi", [P, HG, L], F32R), st.sb("qb_lo", [P, HG, L], F32R)
        out_t = st.sb("out_t", [P, KC, L])
        ident = st.sb("ident", [P, P])
        bias_k, bias_v = st.sb("bias_k", [P, KC]), st.sb("bias_v", [P, KC])
        mx = st.sb("mx", [P, 2, CH])
        neg_max = st.sb("neg_max", [P, 2])
        sums = st.sb("sums", [P, H])
        inv = st.sb("inv", [P, HG])
        inv_wide = st.sb("inv_wide", [P, HG, DH])
        inv_t = st.sb("inv_t", [P, L])
        s_ps = st.ps("s", [P, CH, BANK])
        t_ps = st.ps("t", [P, 3, BANK])
        o_ps = st.ps("o", [P, BANK])
        (small_in, raw_in, split_hi, split_lo, projected, khi_out, klo_out, v_out, q_in, zeroed, qb_hi_set,
         qb_lo_set, scored, maxed, negated, exped, turned, pt_out, pv_done, inv_chain, inv_ready, inv_turned,
         inv_out, scaled, out_ready, stored) = st.sems(
            "small_in", "raw_in", "split_hi", "split_lo", "projected", "khi_out", "klo_out", "v_out", "q_in",
            "zeroed", "qb_hi_set", "qb_lo_set", "scored", "maxed", "negated", "exped", "turned", "pt_out",
            "pv_done", "inv_chain", "inv_ready", "inv_turned", "inv_out", "scaled", "out_ready", "stored")
        block = ctx.enter_context(nc.Block())
        AHEAD, FIRST = 2, 2
        hi_of = [wk_hi[:], wv_hi[:], c_hi[:, 0], c_hi[:, 1]]
        lo_of = [wk_lo[:], wv_lo[:], c_lo[:, 0], c_lo[:, 1]]
        PT_SLOT = [0, 1, 2, 0]

        @block.sync
        def _(sp):
            sp.dma_start(ident[:], ident_dram).then_inc(small_in, 16)
            sp.dma_start(bias_k[:], bk).then_inc(small_in, 16)
            sp.dma_start(bias_v[:], bv).then_inc(small_in, 16)
            sp.dma_start(q_t[:], q_scratch[0]).then_inc(q_in, 16)
            for n, src in enumerate([wk_t, wv_t, ctx_t[0, 0], ctx_t[0, 1]]):
                if n >= 1:
                    sp.wait_ge(split_lo, n)
                sp.dma_start(raw[:], src).then_inc(raw_in, 16)

            def batch(b, last):
                for c in range(CH):
                    if last and c >= CH - AHEAD:
                        continue
                    ahead = c + AHEAD
                    sp.wait_ge(split_lo, 4 * b + c + 4)
                    src = ctx_t[b, ahead] if ahead < CH else ctx_t[b + 1, ahead - CH]
                    sp.dma_start(raw[:], src).then_inc(raw_in, 16)
                sp.wait_ge(out_ready, KC * b + KC)
                sp.dma_start(a_scratch[b], out_t[:]).then_inc(stored, 16)
                sp.wait_ge(stored, 16 * b + 16)
                if not last:
                    sp.wait_ge(qb_lo_set, H * b + H)
                    sp.dma_start(q_t[:], q_scratch[b + 1]).then_inc(q_in, 16)

            with sp.Fori(0, B - 1) as b:
                batch(b, False)
            batch(B - 1, True)

        @block.gpsimd
        def _(pool):
            nc.gpsimd.memset(qb_hi[:].bitcast(F32), 0.0).then_inc(zeroed, 1)
            nc.gpsimd.memset(qb_lo[:].bitcast(F32), 0.0).then_inc(zeroed, 1)

            def split(n, slot):
                pool.wait_ge(split_hi, n + 1)
                nc.gpsimd.tensor_tensor(lo_of[slot], raw[:], hi_of[slot].bitcast(F32),
                                        ALU.subtract).then_inc(split_lo, 1)

            for n in range(FIRST + AHEAD):
                split(n, n)

            with pool.Fori(0, B - 1) as b:
                for c in range(CH):
                    split(4 * b + c + 4, 2 + c % 2)
            for c in range(CH - AHEAD):
                split(4 * (B - 1) + c + 4, 2 + c % 2)

        @block.scalar
        def _(act):
            def split(n, slot):
                act.wait_ge(raw_in, 16 * n + 16)
                nc.scalar.copy(hi_of[slot], raw[:]).then_inc(split_hi, 1)

            for n in range(FIRST + AHEAD):
                split(n, n)
            act.wait_ge(small_in, 48)
            act.wait_ge(zeroed, 2)

            def place_query(b, h):
                p, m = h % HG, h // HG
                rows = slice(DH * p, DH * p + DH)
                nc.scalar.copy(qb_hi[rows, p, :], q_t[rows, m, :]).then_inc(qb_hi_set, 1)

            def batch(b, last):
                for c in range(CH):
                    for m in range(KC):
                        act.wait_ge(projected, 32 * b + 8 * c + m + 1)
                        nc.scalar.activation(k_hi[:, m, c * BANK:(c + 1) * BANK], s_ps[:, m, :], ACT.Identity,
                                             bias=bias_k[:, m:m + 1]).then_inc(khi_out, 1)
                    for j in range(KV):
                        act.wait_ge(projected, 32 * b + 8 * c + KC + j + 1)
                        nc.scalar.copy(v[:, KV * c + j, :], s_ps[:, j, :]).then_inc(v_out, 1)
                    if not (last and c >= CH - AHEAD):
                        split(4 * b + c + 4, 2 + c % 2)
                    if c == 0:
                        act.wait_ge(q_in, 16 * b + 16)
                        for h in range(HG):
                            place_query(b, h)
                for h in range(H + 1):
                    if h < H:
                        act.wait_ge(negated, H * b + h + 1)
                        nc.scalar.activation(probs[:, h % 2, :], s_ps[:].rearrange("p c n -> p (c n)"), ACT.Exp,
                                             bias=neg_max[:, h % 2:h % 2 + 1],
                                             accum_out=sums[:, h:h + 1]).then_inc(exped, 1)
                    if h >= HG and h % HG == 0:
                        act.wait_ge(inv_turned, KC * b + h // HG)
                        nc.scalar.copy(inv_t[:], t_ps[:, 1, :L]).then_inc(inv_out, 1)
                    if 1 <= h <= H - HG:
                        place_query(b, h + 3)

            with act.Fori(0, B - 1) as b:
                batch(b, False)
            batch(B - 1, True)

        @block.vector
        def _(dve):
            dve.wait_ge(small_in, 48)

            def place_query(b, h):
                p, m = h % HG, h // HG
                rows = slice(DH * p, DH * p + DH)
                dve.wait_ge(qb_hi_set, H * b + h + 1)
                dve.tensor_tensor(qb_lo[rows, p, :], q_t[rows, m, :], qb_hi[rows, p, :].bitcast(F32),
                                  ALU.subtract).then_inc(qb_lo_set, 1)

            def widen_inverse(b, g):
                dve.wait_ge(exped, H * b + HG * g + HG)
                dve.reciprocal(inv[:], sums[:, HG * g:HG * g + HG]).then_inc(inv_chain, 1)
                dve.wait_ge(inv_chain, KC * b + g + 1)
                dve.tensor_copy(inv_wide[:], inv[:].unsqueeze(2).to_broadcast([P, HG, DH])).then_inc(inv_ready, 1)

            def empty_pt(b, h):
                for i in range(CH):
                    dve.wait_ge(turned, 64 * b + 4 * h + i + 1)
                    dve.tensor_copy(pt[:, PT_SLOT[i]], t_ps[:, PT_SLOT[i], :].rearrange("p (j l) -> p j l", j=KV))\
                       .then_inc(pt_out, 1)

            def finish_group(b, g):
                dve.wait_ge(pv_done, H * b + HG * g + HG)
                dve.wait_ge(inv_out, KC * b + g + 1)
                dve.tensor_tensor(out_t[:, g, :], o_ps[:, :L], inv_t[:], ALU.mult).then_inc(scaled, 1)
                dve.wait_ge(scaled, KC * b + g + 1)
                dve.tensor_scalar(out_t[:, g, :], out_t[:, g, :], bias_v[:, g:g + 1], None, ALU.add)\
                   .then_inc(out_ready, 1)

            def batch(b):
                for c in range(CH):
                    for m in range(KC):
                        dve.wait_ge(khi_out, 16 * b + 4 * c + m + 1)
                        part = slice(c * BANK, (c + 1) * BANK)
                        dve.scalar_tensor_tensor(out=k_lo[:, m, part], in0=s_ps[:, m, :], scalar=bias_k[:, m:m + 1],
                                                 in1=k_hi[:, m, part].bitcast(F32), op0=ALU.add,
                                                 op1=ALU.subtract).then_inc(klo_out, 1)
                    if c == 0:
                        dve.wait_ge(q_in, 16 * b + 16)
                        for h in range(HG):
                            place_query(b, h)
                for h in range(H + 1):
                    if h < H:
                        for i in range(CH):
                            dve.wait_ge(scored, 64 * b + 4 * h + i + 1)
                            dve.tensor_reduce(mx[:, h % 2, i:i + 1], s_ps[:, i, :], AX.X, ALU.max).then_inc(maxed, 1)
                        dve.wait_ge(maxed, 64 * b + 4 * h + 4)
                        dve.tensor_reduce(neg_max[:, h % 2:h % 2 + 1], mx[:, h % 2, :], AX.X, ALU.max,
                                          negate=True).then_inc(negated, 1)
                    if h >= HG and h % HG == 0:
                        widen_inverse(b, h // HG - 1)
                    if h >= 1:
                        empty_pt(b, h - 1)
                    if h >= HG and h % HG == 0:
                        finish_group(b, h // HG - 1)
                    if 1 <= h <= H - HG:
                        place_query(b, h + 3)

            with dve.Fori(0, B - 1) as b:
                batch(b)
            batch(B - 1)

        @block.tensor
        def _(pe):
            pe.wait_ge(small_in, 48)

            def three(out, w_hi, w_lo, x_hi, x_lo, first, final):
                pe.matmul(out, w_hi, x_hi, start=first, stop=False)
                pe.matmul(out, w_lo, x_hi, start=False, stop=False)
                return pe.matmul(out, w_hi, x_lo, start=False, stop=final)

            def project(b):
                for c in range(CH):
                    pe.wait_ge(split_lo, 4 * b + c + FIRST + 1)
                    s = c % 2
                    for m in range(KC):
                        if c >= 1:
                            pe.wait_ge(v_out, 16 * b + 4 * (c - 1) + m + 1)
                        part = slice(m * P, (m + 1) * P)
                        for k in range(KC):
                            mm = three(s_ps[:, m, :], wk_hi[:, k, part], wk_lo[:, k, part], c_hi[:, s, k, :],
                                       c_lo[:, s, k, :], k == 0, k == KC - 1)
                        mm.then_inc(projected, 1)
                    for j in range(KV):
                        pe.wait_ge(klo_out, 16 * b + 4 * c + j + 1)
                        part = slice(j * P, (j + 1) * P)
                        for k in range(KC):
                            mm = three(s_ps[:, j, :], c_hi[:, s, k, part], c_lo[:, s, k, part], wv_hi[:, k, :],
                                       wv_lo[:, k, :], k == 0, k == KC - 1)
                        mm.then_inc(projected, 1)

            def scores(b, h):
                p, m = h % HG, h // HG
                pe.wait_ge(qb_lo_set, H * b + h + 1)
                if h == 0:
                    pe.wait_ge(v_out, 16 * b + 16)
                    pe.wait_ge(klo_out, 16 * b + 16)
                else:
                    pe.wait_ge(exped, H * b + h)
                for i in range(CH):
                    part = slice(i * BANK, (i + 1) * BANK)
                    three(s_ps[:, i, :], qb_hi[:, p, :], qb_lo[:, p, :], k_hi[:, m, part], k_lo[:, m, part],
                          True, True).then_inc(scored, 1)

            def turn(b, h, i):
                for j in range(KV):
                    col = i * BANK + j * P
                    mm = pe.transpose(t_ps[:, PT_SLOT[i], j * L:(j + 1) * L], probs[:, h % 2, col:col + P], ident[:])
                mm.then_inc(turned, 1)

            def weigh(b, h, i):
                p = h % HG
                pe.wait_ge(pt_out, 64 * b + 4 * h + i + 1)
                for j in range(KV):
                    mm = pe.matmul(o_ps[DH * p:DH * p + DH, :L], v[:, KV * i + j, DH * h:DH * h + DH],
                                   pt[:, PT_SLOT[i], j, :], start=(i == 0 and j == 0),
                                   stop=(i == CH - 1 and j == KV - 1), tile_position=(0, DH * p))
                if i == CH - 1:
                    mm.then_inc(pv_done, 1)

            def values(b, h):
                pe.wait_ge(exped, H * b + h + 1)
                turn(b, h, 0)
                if h >= HG and h % HG == 0:
                    pe.wait_ge(inv_out, KC * b + h // HG)
                turn(b, h, 1)
                turn(b, h, 2)
                if h >= HG and h % HG == 0:
                    pe.wait_ge(scaled, KC * b + h // HG)
                weigh(b, h, 0)
                turn(b, h, 3)
                for i in range(1, CH):
                    weigh(b, h, i)
                if h % HG == HG - 1:
                    pe.wait_ge(inv_ready, KC * b + h // HG + 1)
                    pe.transpose(t_ps[:, 1, :L], inv_wide[:].rearrange("p h d -> p (h d)"), ident[:])\
                      .then_inc(inv_turned, 1)

            def batch(b):
                project(b)
                scores(b, 0)
                for h in range(1, H):
                    scores(b, h)
                    values(b, h - 1)
                values(b, H - 1)

            with pe.Fori(0, B - 1) as b:
                batch(b)
            batch(B - 1)


DIN = 2 * D
DT = DIN // P
N, DTR, TW = 16, 64, 4
XD = DTR + 2 * N
G, BG = 2, B // 2


def mixer_in(nc, a_scratch, x, wo_t, bo, w_in, b_in, w_conv, b_conv, w_x, ident_dram, xres, u, gate, xd):
    with ExitStack() as ctx:
        st = Stage(nc, ctx, "m")
        at = st.sb("at", [P, B, KC, L])
        wo = st.sb("wo", [P, KC, D])
        bo_all = st.sb("bo", [P, D])
        wi = st.sb("wi", [P, KC, 2 * DIN])
        bi = st.sb("bi", [P, 2 * DT])
        wc = st.sb("wc", [P, DT, TW])
        bc = st.sb("bc", [P, DT])
        wx = st.sb("wx", [P, DT, XD])
        ident = st.sb("ident", [P, P])
        xn = st.sb("xn", [P, 2, D])
        xn_t = st.sb("xnT", [P, KC, T])
        PADDED = L + TW - 1
        xc = st.sb("xc", [P, 2, B, PADDED])
        acc = st.sb("acc", [P, 2, B, L])
        stats, mv, rstd = st.sb("stats", [P, B, 6]), st.sb("mv", [P, B, 2]), st.sb("rstd", [P, B])
        op = st.ps("op", [P, 2, BANK])
        tp = st.ps("tp", [P, 2, BANK])
        ip = st.ps("ip", [P, 4, BANK])
        (w_in_s, x_in, biased, o_made, added, chain, var_ready, root_ready, normed, turned, copied, i_made,
         i_out, taps, conv_done, u_done, padded, xd_made, xd_out) = st.sems(
            "w_in", "x_in", "biased", "o_made", "added", "chain", "var_ready", "root_ready", "normed", "turned",
            "copied", "i_made", "i_out", "taps", "conv_done", "u_done", "padded", "xd_made", "xd_out")
        block = ctx.enter_context(nc.Block())

        @block.sync
        def _(sp):
            sp.dma_start(xres[:], x.rearrange("b l d -> l b d")).then_inc(x_in, 16)
            sp.dma_start(bo_all[:], bo.partition_broadcast(P)).then_inc(x_in, 16)
            sp.dma_start(wo[:], wo_t).then_inc(w_in_s, 16)
            sp.dma_start(at[:], a_scratch.rearrange("b p m l -> p b m l")).then_inc(w_in_s, 16)
            for dst, src in ((ident, ident_dram), (wi, w_in), (bi, b_in), (wc, w_conv), (bc, b_conv), (wx, w_x)):
                sp.dma_start(dst[:], src).then_inc(w_in_s, 16)

        @block.gpsimd
        def _(pool):
            nc.gpsimd.memset(xc[:, :, :, 0:TW - 1], 0.0).then_inc(padded, 1)
            pool.wait_ge(x_in, 32)
            for b in range(B):
                nc.gpsimd.tensor_tensor(xres[:, b, :], xres[:, b, :], bo_all[:], ALU.add).then_inc(biased, 1)

        @block.scalar
        def _(act):
            for b in range(B):
                act.wait_ge(var_ready, b + 1)
                nc.scalar.activation(rstd[:, b:b + 1], rstd[:, b:b + 1], ACT.Sqrt).then_inc(root_ready, 1)
            act.wait_ge(w_in_s, 128)
            act.wait_ge(padded, 1)
            for c in range(2 * DT):
                for g in range(G):
                    n = G * c + g
                    act.wait_ge(i_made, n + 1)
                    if c < DT:
                        if c >= 2 and g == 0:
                            act.wait_ge(conv_done, c - 1)
                        nc.scalar.activation(xc[:, c % 2, BG * g:BG * g + BG, TW - 1:],
                                             ip[:, n % 4, :].rearrange("p (b l) -> p b l", l=L), ACT.Identity,
                                             bias=bi[:, c:c + 1]).then_inc(i_out, 1)
                    else:
                        nc.scalar.activation(gate[:, c - DT, g * BANK:(g + 1) * BANK], ip[:, n % 4, :], ACT.Silu,
                                             bias=bi[:, c:c + 1]).then_inc(i_out, 1)
                if 1 <= c <= DT:
                    act.wait_ge(conv_done, c)
                    nc.scalar.activation(u[:, c - 1, :], acc[:, (c - 1) % 2].rearrange("p b l -> p (b l)"), ACT.Silu,
                                         bias=bc[:, c - 1:c]).then_inc(u_done, 1)

        @block.vector
        def _(dve):
            def finish_norm(b):
                dve.wait_ge(turned, b + 1)
                dve.tensor_copy(xn_t[:, :, b * L:(b + 1) * L],
                                tp[:, b % 2, :].rearrange("p (k l) -> p k l", k=KC)).then_inc(copied, 1)

            for b in range(B):
                dve.wait_ge(o_made, b + 1)
                dve.wait_ge(biased, b + 1)
                dve.tensor_tensor(xres[:, b, :], xres[:, b, :], op[:, b % 2, :], ALU.add).then_inc(added, 1)
                dve.wait_ge(added, b + 1)
                if b >= 2:
                    dve.wait_ge(turned, b - 1)
                layer_norm_steps(dve, xres[:, b, :], xn[:, b % 2, :], stats[:, b, :], mv[:, b, :],
                                 rstd[:, b:b + 1], root_ready, var_ready, chain, normed, b, 3 * b)
                if b >= 1:
                    finish_norm(b - 1)
            finish_norm(B - 1)
            dve.wait_ge(w_in_s, 128)
            for c in range(DT):
                dve.wait_ge(i_out, G * c + G)
                if c >= 2:
                    dve.wait_ge(u_done, c - 1)
                s = c % 2
                dve.tensor_scalar(acc[:, s], xc[:, s, :, TW - 1:TW - 1 + L], wc[:, c, TW - 1:TW], None,
                                  ALU.mult).then_inc(taps, 1)
                for k in range(TW - 1):
                    dve.wait_ge(taps, 3 * c + k + 1)
                    dve.scalar_tensor_tensor(out=acc[:, s], in0=xc[:, s, :, k:k + L], scalar=wc[:, c, k:k + 1],
                                             in1=acc[:, s], op0=ALU.mult, op1=ALU.add)\
                       .then_inc(conv_done if k == TW - 2 else taps, 1)
            for g in range(G):
                dve.wait_ge(xd_made, g + 1)
                dve.tensor_copy(xd[0:XD, g * BANK:(g + 1) * BANK], op[0:XD, g, :]).then_inc(xd_out, 1)

        @block.tensor
        def _(pe):
            pe.wait_ge(w_in_s, 128)

            def turn(b):
                pe.wait_ge(normed, b + 1)
                if b >= 2:
                    pe.wait_ge(copied, b - 1)
                for k in range(KC):
                    mm = pe.transpose(tp[:, b % 2, k * L:(k + 1) * L], xn[:, b % 2, k * P:(k + 1) * P], ident[:])
                mm.then_inc(turned, 1)

            for b in range(B):
                if b >= 2:
                    pe.wait_ge(added, b - 1)
                for k in range(KC):
                    mm = pe.matmul(op[:, b % 2, :], at[:, b, k, :], wo[:, k, :], start=(k == 0), stop=(k == KC - 1))
                mm.then_inc(o_made, 1)
                if b >= 1:
                    turn(b - 1)
            turn(B - 1)
            pe.wait_ge(copied, B)
            for c in range(2 * DT):
                for g in range(G):
                    n = G * c + g
                    if n >= 4:
                        pe.wait_ge(i_out, n - 3)
                    for k in range(KC):
                        mm = pe.matmul(ip[:, n % 4, :], wi[:, k, c * P:(c + 1) * P],
                                       xn_t[:, k, g * BANK:(g + 1) * BANK], start=(k == 0), stop=(k == KC - 1))
                    mm.then_inc(i_made, 1)
            pe.wait_ge(u_done, DT)
            for g in range(G):
                for c in range(DT):
                    mm = pe.matmul(op[0:XD, g, :], wx[:, c, :], u[:, c, g * BANK:(g + 1) * BANK],
                                   start=(c == 0), stop=(c == DT - 1))
                mm.then_inc(xd_made, 1)


def mixer_scan(nc, w_dt, a_log, d_skip, ident_dram, u, gate, xd):
    with ExitStack() as ctx:
        st = Stage(nc, ctx, "s")
        wd = st.sb("wd", [P, DIN])
        a_neg = st.sb("a_neg", [P, DT, N])
        dsk = st.sb("dsk", [P, DT])
        ident = st.sb("ident", [P, P])
        bc = st.sb("bc", [P, 2 * N, BANK])
        delta = st.sb("delta", [P, DT, BANK])
        du = st.sb("du", [P, 2, BANK])
        decay = st.sb("decay", [P, 2, BG, L + 1])
        drive = st.sb("drive", [P, 2, BG, L + 1])
        state = st.sb("state", [P, 2, BG, L + 1])
        seen = st.sb("seen", [P, 2, BG, L])
        skip = st.sb("skip", [P, 2, BANK])
        ps = st.ps("ps", [P, 8, BANK])
        (w_in, a_ready, zeroed, spread, odd_out, even_out, d_made, abs_out, exp_out, log_out, delta_out, du_out, decayed,
         driven, scanned, weighed, summed, skipped, y_out) = st.sems(
            "w_in", "a_ready", "zeroed", "spread", "odd_out", "even_out", "d_made", "abs_out", "exp_out", "log_out", "delta_out",
            "du_out", "decayed", "driven", "scanned", "weighed", "summed", "skipped", "y_out")
        block = ctx.enter_context(nc.Block())
        flat = lambda t: t.rearrange("p b l -> p (b l)")
        SPREAD_BANKS = 4
        UN = 2
        STEPS = UN * N

        @block.sync
        def _(sp):
            for dst, src in ((wd[0:DTR, :], w_dt), (a_neg[:], a_log), (dsk[:], d_skip), (ident[:], ident_dram)):
                sp.dma_start(dst, src).then_inc(w_in, 16)

        @block.gpsimd
        def _(pool):
            nc.gpsimd.memset(decay[:], 0.0).then_inc(zeroed, 1)
            nc.gpsimd.memset(drive[:], 0.0).then_inc(zeroed, 1)
            pool.wait_ge(zeroed, 2)

            def step(g, pair, s):
                n = s % N
                if n == 0:
                    pool.wait_ge(du_out, DT * g + UN * pair + s // N + 1)
                done = N * DT * g + STEPS * pair + s
                pool.wait_ge(scanned, done + 1)
                nc.gpsimd.tensor_tensor(drive[:, s % 2, :, 1:], du[:, s // N].rearrange("p (b l) -> p b l", l=L),
                                        bc[:, n, :].rearrange("p (b l) -> p b l", l=L), ALU.mult).then_inc(driven, 1)

            for g in range(G):
                pool.wait_ge(even_out, N * (g + 1))
                pool.wait_ge(odd_out, N * (g + 1))
                with pool.Fori(0, DT // UN) as pair:
                    for s in range(STEPS):
                        step(g, pair, s)

        @block.scalar
        def _(act):
            act.wait_ge(w_in, 64)
            nc.scalar.activation(a_neg[:], a_neg[:], ACT.Exp).then_inc(a_ready, 1)
            act.wait_ge(zeroed, 2)
            act.wait_ge(a_ready, 2)
            for g in range(G):
                for r in range(1, 2 * N, 2):
                    act.wait_ge(spread, 2 * N * g + r + 1)
                    nc.scalar.copy(bc[:, r, :], ps[:, r % SPREAD_BANKS, :]).then_inc(odd_out, 1)
                for d in range(DT):
                    act.wait_ge(d_made, DT * g + d + 1)
                    nc.scalar.activation(delta[:, d, :], ps[:, d, :], ACT.Abs).then_inc(abs_out, 1)
                for d in range(DT):
                    act.wait_ge(abs_out, DT * g + d + 1)
                    nc.scalar.activation(delta[:, d, :], delta[:, d, :], ACT.Exp, scale=-1.0).then_inc(exp_out, 1)
                for d in range(DT):
                    act.wait_ge(exp_out, DT * g + d + 1)
                    nc.scalar.activation(delta[:, d, :], delta[:, d, :], ACT.Ln, bias=1.0).then_inc(log_out, 1)
                act.wait_ge(delta_out, DT * g + DT)
                with act.Fori(0, DT // UN) as pair:
                    for s in range(STEPS):
                        n, d = s % N, UN * pair + s // N
                        act.wait_ge(scanned, N * DT * g + STEPS * pair + s + 1)
                        nc.scalar.activation(decay[:, s % 2, :, 1:],
                                             delta[:, d, :].rearrange("p (b l) -> p b l", l=L), ACT.Exp,
                                             scale=a_neg[:, d, n:n + 1]).then_inc(decayed, 1)

        @block.vector
        def _(dve):
            dve.wait_ge(a_ready, 1)
            dve.tensor_scalar(a_neg[:], a_neg[:], -1.0, None, ALU.mult).then_inc(a_ready, 1)
            dve.memset(state[:, 0, :, 0:1], 0.0).then_inc(scanned, 2)
            for g in range(G):
                for r in range(0, 2 * N, 2):
                    dve.wait_ge(spread, 2 * N * g + r + 1)
                    dve.tensor_copy(bc[:, r, :], ps[:, r % SPREAD_BANKS, :]).then_inc(even_out, 1)
                for d in range(DT):
                    dve.wait_ge(log_out, DT * g + d + 1)
                    dve.scalar_tensor_tensor(out=delta[:, d, :], in0=ps[:, d, :], scalar=0.0, in1=delta[:, d, :],
                                             op0=ALU.max, op1=ALU.add).then_inc(delta_out, 1)
                dve.wait_ge(delta_out, DT * g + DT)
                cols = slice(g * BANK, (g + 1) * BANK)
                with dve.Fori(0, DT // UN) as pair:
                    before = N * DT * g + STEPS * pair

                    def make_du(i):
                        d = UN * pair + i
                        dve.tensor_tensor(du[:, i, :], delta[:, d, :], u[:, d, cols], ALU.mult).then_inc(du_out, 1)

                    def weigh(s):
                        dve.wait_ge(scanned, before + s + 3)
                        dve.wait_ge(summed, before + s + 1)
                        dve.tensor_tensor(seen[:, s % 2], state[:, s % 2, :, 1:],
                                          bc[:, N + s % N, :].rearrange("p (b l) -> p b l", l=L), ALU.mult)\
                           .then_inc(weighed, 1)

                    def finish(i):
                        d = UN * pair + i
                        dve.wait_ge(summed, before + N * i + N + 2)
                        dve.scalar_tensor_tensor(out=skip[:, i, :], in0=u[:, d, cols], scalar=dsk[:, bass.ds(d, 1)],
                                                 in1=ps[:, i, :], op0=ALU.mult, op1=ALU.add).then_inc(skipped, 1)
                        dve.wait_ge(skipped, DT * g + UN * pair + i + 1)
                        dve.tensor_tensor(u[:, d, cols], skip[:, i, :], gate[:, d, cols], ALU.mult).then_inc(y_out, 1)

                    make_du(0)
                    make_du(1)
                    for s in range(STEPS):
                        dve.wait_ge(decayed, before + s + 1)
                        dve.wait_ge(driven, before + s + 1)
                        if s >= 2:
                            dve.wait_ge(weighed, before + s - 1)
                        dve.tensor_tensor_scan(flat(state[:, s % 2]), flat(decay[:, s % 2]), flat(drive[:, s % 2]),
                                               0.0, ALU.mult, ALU.add).then_inc(scanned, 1)
                        if s >= 1:
                            weigh(s - 1)
                        if s == N + 2:
                            finish(0)
                    weigh(STEPS - 1)
                    finish(1)

        @block.tensor
        def _(pe):
            pe.wait_ge(w_in, 64)
            pe.transpose(ps[:, 7, :P], ident[:], ident[:]).then_inc(summed, 2)
            for g in range(G):
                cols = slice(g * BANK, (g + 1) * BANK)
                if g >= 1:
                    pe.wait_ge(y_out, DT * g)
                for r in range(2 * N):
                    if r >= SPREAD_BANKS:
                        pe.wait_ge(odd_out if r % 2 else even_out, N * g + (r - SPREAD_BANKS) // 2 + 1)
                    row = DTR + r
                    pe.matmul(ps[:, r % SPREAD_BANKS, :], ident[0:XD, row:row + 1].to_broadcast([XD, P]),
                              xd[0:XD, cols], start=True, stop=True).then_inc(spread, 1)
                pe.wait_ge(even_out, N * (g + 1))
                pe.wait_ge(odd_out, N * (g + 1))
                for d in range(DT):
                    pe.matmul(ps[:, d, :], wd[0:DTR, d * P:(d + 1) * P], xd[0:DTR, cols],
                              start=True, stop=True).then_inc(d_made, 1)
                pe.wait_ge(delta_out, DT * (g + 1))
                with pe.Fori(0, DT // UN) as pair:
                    for s in range(STEPS):
                        i, n = s // N, s % N
                        pe.wait_ge(weighed, N * DT * g + STEPS * pair + s + 1)
                        pe.matmul(ps[:, i, :], ident[:], flat(seen[:, s % 2]), start=(n == 0), stop=(n == N - 1))\
                          .then_inc(summed, 1)


E = 8
HID = D // 4
K3 = 3


def experts(nc, w, ident_dram, iota, xres, u, out):
    with ExitStack() as ctx:
        st = Stage(nc, ctx, "e")
        ident = st.sb("ident", [P, P])
        ones = st.sb("ones", [P, P])
        wo = st.sb("w_out", [P, DT, D])
        xn = st.sb("xn", [P, 2, D])
        PADDED = L + K3 - 1
        xf_t = st.sb("xfT", [P, KC, B, PADDED])
        x1_t = st.sb("x1T", [P, KC, T])
        h_t = st.sb("hT", [P, KC, T])
        rms = st.sb("rms", [P, G, BANK])
        ff_t = st.sb("ffT", [P, T])
        pw, ow = st.sb("pw", [P, KC, D]), st.sb("ow", [P, KC, D])
        dw, dwb, pwb = st.sb("dw", [P, KC, K3]), st.sb("dwb", [P, KC]), st.sb("pwb", [P, KC])
        rw, rb = st.sb("rw", [P, KC, E]), st.sb("rb", [P, E])
        owb, nw, fdb = st.sb("owb", [P, KC]), st.sb("nw", [P, KC]), st.sb("fdb", [P, 1])
        fd, fu, fub = st.sb("fd", [P, KC, HID]), st.sb("fu", [HID, D]), st.sb("fub", [P, D])
        ew, eb = st.sb("ew", [P, 2, KC, D]), st.sb("eb", [P, 2, D])
        pre, act_e = st.sb("pre", [P, 2, D]), st.sb("act_e", [P, 2, D])
        stats, mv, rstd = st.sb("stats", [P, B, 6]), st.sb("mv", [P, B, 2]), st.sb("rstd", [P, B])
        logits, top = st.sb("logits", [P, B, E]), st.sb("top", [P, B, E])
        index = st.sb("index", [P, B, E], U32)
        chosen = st.sb("chosen", [P, B, E])
        numbers = st.sb("numbers", [P, E])
        share = st.sb("share", [P, 4, B])
        route, second = st.sb("route", [P, B, E]), st.sb("second", [P, B, E])
        uu = u.rearrange("p c t -> p (c t)")
        conv = uu[:, 0:KC * T].rearrange("p (k t) -> p k t", k=KC)
        comb = uu[:, KC * T:2 * KC * T].rearrange("p (b d) -> p b d", b=B)
        comb_t, hp_t = conv, comb.rearrange("p b d -> p (b d)").rearrange("p (k t) -> p k t", k=KC)
        ps = st.ps("ps", [P, 6, BANK])
        tp = st.ps("tp", [P, 2, BANK])
        (w_in, eb_in0, eb_in1, made, added, chain, var_ready, root_ready, normed, turned, copied, padded, taps,
         conv_out, silu_out, x1_out, lg_out, dstep, astep, routed, ex_made, pre_out, act_out, comb_out, zeroed,
         m_made, hp_out, sq_out, ss_made, rms_out, h_out, fd_made, ff_out, f_made, fin_out, biased, stored) = st.sems(
            "w_in", "eb_in0", "eb_in1", "made", "added", "chain", "var_ready", "root_ready", "normed", "turned",
            "copied", "padded", "taps", "conv_out", "silu_out", "x1_out", "lg_out", "dstep", "astep", "routed",
            "ex_made", "pre_out", "act_out", "comb_out", "zeroed", "m_made", "hp_out", "sq_out", "ss_made",
            "rms_out", "h_out", "fd_made", "ff_out", "f_made", "fin_out", "biased", "stored")
        eb_in = [eb_in0, eb_in1]
        block = ctx.enter_context(nc.Block())
        sq_of = lambda n: h_t[:, n // G, (n % G) * BANK:(n % G + 1) * BANK]
        NT = KC * G
        tile_of = lambda n: (n // G, slice((n % G) * BANK, (n % G + 1) * BANK))

        @block.sync
        def _(sp):
            loads = ((ident, ident_dram), (wo, w["w_out"]), (dw, w["dw"]), (dwb, w["dwb"]), (pw, w["pw"]),
                     (pwb, w["pwb"]), (rw, w["rw"]), (ow, w["ow"]), (owb, w["owb"]), (nw, w["nw"]), (fd, w["fd"]),
                     (fdb, w["fdb"]), (fu, w["fu"]), (numbers, iota.partition_broadcast(P)),
                     (rb, w["rb"].partition_broadcast(P)), (fub, w["fub"].partition_broadcast(P)))
            assert len(loads) == 16
            for dst, src in loads:
                sp.dma_start(dst[:], src).then_inc(w_in, 16)

            def load_expert(e, s):
                sp.dma_start(ew[:, s], w["ew"][e]).then_inc(eb_in[s], 16)
                sp.dma_start(eb[:, s, :], w["eb"][e].partition_broadcast(P)).then_inc(eb_in[s], 16)

            load_expert(0, 0)
            load_expert(1, 1)
            with sp.Fori(0, E // 2 - 1) as pair:
                for s in range(2):
                    sp.wait_ge(pre_out, 2 * B * pair + B * s + B)
                    load_expert(2 * pair + 2 + s, s)
            for b in range(B):
                sp.wait_ge(fin_out, b + 1)
                sp.dma_start(out[b], xres[:, b, :]).then_inc(stored, 16)
            sp.wait_ge(stored, 16 * B)

        @block.gpsimd
        def _(pool):
            nc.gpsimd.memset(xf_t[:, :, :, 0:K3 - 1], 0.0).then_inc(padded, 1)
            nc.gpsimd.memset(ones[:], 1.0).then_inc(padded, 1)
            pool.wait_ge(w_in, 256)
            pool.wait_ge(normed, B)
            for b in range(B):
                nc.gpsimd.tensor_tensor(xres[:, b, :], xres[:, b, :], fub[:], ALU.add).then_inc(biased, 1)
            pool.wait_ge(made, B)
            nc.gpsimd.memset(comb[:], 0.0).then_inc(zeroed, 1)

        @block.scalar
        def _(act):
            for b in range(B):
                act.wait_ge(var_ready, b + 1)
                nc.scalar.activation(rstd[:, b:b + 1], rstd[:, b:b + 1], ACT.Sqrt).then_inc(root_ready, 1)
            for n in range(NT):
                k, cols = tile_of(n)
                act.wait_ge(made, B + n + 1)
                nc.scalar.activation(h_t[:, k, cols], ps[:, n % 4, :], ACT.Silu, bias=pwb[:, k:k + 1])\
                   .then_inc(silu_out, 1)
            act.wait_ge(dstep, 2)
            nc.scalar.activation(share[:, 1, :], share[:, 0, :], ACT.Exp).then_inc(astep, 1)

            def silu(pair, s, b):
                n = B * s + b
                act.wait_ge(pre_out, 2 * B * pair + n + 1)
                nc.scalar.activation(act_e[:, n % 2, :], pre[:, n % 2, :], ACT.Silu).then_inc(act_out, 1)

            with act.Fori(0, E // 2) as pair:
                for s in range(2):
                    for b in range(B):
                        silu(pair, s, b)
            for g in range(G):
                act.wait_ge(ss_made, g + 1)
                nc.scalar.activation(rms[:, g, :], ps[:, 4 + g, :], ACT.Sqrt, scale=1.0 / D).then_inc(astep, 1)
            for g in range(G):
                act.wait_ge(fd_made, g + 1)
                nc.scalar.activation(ff_t[:, g * BANK:(g + 1) * BANK], ps[:, g, :], ACT.Gelu, bias=fdb[:, 0:1])\
                   .then_inc(ff_out, 1)

        @block.vector
        def _(dve):
            def finish_norm(b):
                dve.wait_ge(turned, b + 1)
                dve.tensor_copy(xf_t[:, :, b, K3 - 1:],
                                tp[:, b % 2, :].rearrange("p (k l) -> p k l", k=KC)).then_inc(copied, 1)

            dve.wait_ge(w_in, 256)
            for b in range(B):
                dve.wait_ge(made, b + 1)
                dve.tensor_tensor(xres[:, b, :], xres[:, b, :], ps[:, b % 4, :], ALU.add).then_inc(added, 1)
                dve.wait_ge(added, b + 1)
                if b >= 2:
                    dve.wait_ge(turned, b - 1)
                layer_norm_steps(dve, xres[:, b, :], xn[:, b % 2, :], stats[:, b, :], mv[:, b, :],
                                 rstd[:, b:b + 1], root_ready, var_ready, chain, normed, b, 3 * b)
                if b >= 1:
                    finish_norm(b - 1)
            finish_norm(B - 1)
            dve.wait_ge(padded, 2)
            dve.wait_ge(copied, B)
            for k in range(KC):
                c = conv[:, k, :].rearrange("p (b l) -> p b l", l=L)
                dve.tensor_scalar(c, xf_t[:, k, :, K3 - 1:], dw[:, k, K3 - 1:K3], dwb[:, k:k + 1], ALU.mult,
                                  ALU.add).then_inc(taps, 1)
                for j in range(K3 - 1):
                    dve.wait_ge(taps, 2 * k + j + 1)
                    dve.scalar_tensor_tensor(out=c, in0=xf_t[:, k, :, j:j + L], scalar=dw[:, k, j:j + 1], in1=c,
                                             op0=ALU.mult, op1=ALU.add).then_inc(conv_out if j else taps, 1)
            for n in range(NT):
                k, cols = tile_of(n)
                g = n % G
                dve.wait_ge(silu_out, n + 1)
                dve.tensor_tensor(x1_t[:, k, cols].rearrange("p (b l) -> p b l", l=L),
                                  xf_t[:, k, BG * g:BG * g + BG, K3 - 1:],
                                  h_t[:, k, cols].rearrange("p (b l) -> p b l", l=L), ALU.add).then_inc(x1_out, 1)
            dve.wait_ge(made, B + NT + B)
            dve.tensor_tensor(logits[:], ps[:, 4, 0:B * E].rearrange("p (b e) -> p b e", e=E),
                              rb[:].unsqueeze(1).to_broadcast([P, B, E]), ALU.add).then_inc(lg_out, 1)
            dve.wait_ge(lg_out, 1)
            for b in range(B):
                dve.max(top[:, b, :], logits[:, b, :]).then_inc(lg_out, 1)
            for b in range(B):
                dve.wait_ge(lg_out, b + 2)
                dve.max_index(index[:, b, :], top[:, b, :], logits[:, b, :]).then_inc(lg_out, 1)
            dve.wait_ge(lg_out, 2 * B + 1)
            dve.tensor_copy(chosen[:], index[:]).then_inc(dstep, 1)
            dve.tensor_tensor(share[:, 0, :], top[:, :, 1], top[:, :, 0], ALU.subtract).then_inc(dstep, 1)
            dve.wait_ge(astep, 1)
            dve.tensor_scalar(share[:, 2, :], share[:, 1, :], 1.0, None, ALU.add).then_inc(dstep, 1)
            dve.wait_ge(dstep, 3)
            dve.reciprocal(share[:, 2, :], share[:, 2, :]).then_inc(dstep, 1)
            dve.wait_ge(dstep, 4)
            dve.tensor_tensor(share[:, 3, :], share[:, 1, :], share[:, 2, :], ALU.mult).then_inc(dstep, 1)
            wide = lambda a: a.unsqueeze(2).to_broadcast([P, B, E])
            every = numbers[:].unsqueeze(1).to_broadcast([P, B, E])
            dve.tensor_tensor(route[:], every, wide(chosen[:, :, 0]), ALU.is_equal).then_inc(dstep, 1)
            dve.tensor_tensor(second[:], every, wide(chosen[:, :, 1]), ALU.is_equal).then_inc(dstep, 1)
            dve.wait_ge(dstep, 7)
            dve.tensor_tensor(route[:], route[:], wide(share[:, 2, :]), ALU.mult).then_inc(dstep, 1)
            dve.tensor_tensor(second[:], second[:], wide(share[:, 3, :]), ALU.mult).then_inc(dstep, 1)
            dve.wait_ge(dstep, 9)
            dve.tensor_tensor(route[:], route[:], second[:], ALU.add).then_inc(routed, 1)
            dve.wait_ge(routed, 1)
            dve.wait_ge(zeroed, 1)

            def biased_expert(pair, s, b):
                n = B * s + b
                if b == 0:
                    dve.wait_ge(eb_in[s], 32 * pair + 32)
                dve.wait_ge(ex_made, 2 * B * pair + n + 1)
                dve.tensor_tensor(pre[:, n % 2, :], ps[:, n % 4, :], eb[:, s, :], ALU.add).then_inc(pre_out, 1)

            def accumulate(pair, s, b):
                n = B * s + b
                dve.wait_ge(act_out, 2 * B * pair + n + 1)
                e = 2 * pair + s
                dve.scalar_tensor_tensor(out=comb[:, b, :], in0=act_e[:, n % 2, :], scalar=route[:, b, bass.ds(e, 1)],
                                         in1=comb[:, b, :], op0=ALU.mult, op1=ALU.add).then_inc(comb_out, 1)

            with dve.Fori(0, E // 2) as pair:
                for n in range(2 * B + 1):
                    if n < 2 * B:
                        biased_expert(pair, n // B, n % B)
                    if n >= 1:
                        accumulate(pair, (n - 1) // B, (n - 1) % B)
            for b in range(B):
                dve.wait_ge(turned, B + b + 1)
                dve.tensor_copy(comb_t[:, :, b * L:(b + 1) * L],
                                tp[:, b % 2, :].rearrange("p (k l) -> p k l", k=KC)).then_inc(copied, 1)
            for n in range(NT):
                k, cols = tile_of(n)
                dve.wait_ge(m_made, n + 1)
                dve.scalar_tensor_tensor(out=hp_t[:, k, cols], in0=ps[:, n % 4, :], scalar=owb[:, k:k + 1],
                                         in1=x1_t[:, k, cols], op0=ALU.add, op1=ALU.add).then_inc(hp_out, 1)
                dve.wait_ge(hp_out, n + 1)
                dve.tensor_tensor(sq_of(n), hp_t[:, k, cols], hp_t[:, k, cols], ALU.mult).then_inc(sq_out, 1)
            for g in range(G):
                dve.wait_ge(astep, 2 + g)
                dve.reciprocal(rms[:, g, :], rms[:, g, :]).then_inc(rms_out, 1)
            for n in range(NT):
                k, cols = tile_of(n)
                if n < G:
                    dve.wait_ge(rms_out, n + 1)
                dve.scalar_tensor_tensor(out=h_t[:, k, cols], in0=hp_t[:, k, cols], scalar=nw[:, k:k + 1],
                                         in1=rms[:, n % G, :], op0=ALU.mult, op1=ALU.mult).then_inc(h_out, 1)
            for b in range(B):
                dve.wait_ge(f_made, b + 1)
                dve.wait_ge(biased, b + 1)
                dve.tensor_tensor(xres[:, b, :], xres[:, b, :], ps[:, 2 + b % 4, :], ALU.add).then_inc(fin_out, 1)

        @block.tensor
        def _(pe):
            pe.wait_ge(w_in, 256)

            def turn(src, b, count, ready, value):
                pe.wait_ge(ready, value)
                if count >= 2:
                    pe.wait_ge(copied, count - 1)
                for k in range(KC):
                    mm = pe.transpose(tp[:, b % 2, k * L:(k + 1) * L], src[:, k * P:(k + 1) * P], ident[:])
                mm.then_inc(turned, 1)

            for b in range(B):
                if b >= 4:
                    pe.wait_ge(added, b - 3)
                for c in range(DT):
                    mm = pe.matmul(ps[:, b % 4, :], u[:, c, b * L:(b + 1) * L], wo[:, c, :], start=(c == 0),
                                   stop=(c == DT - 1))
                mm.then_inc(made, 1)
                if b >= 1:
                    turn(xn[:, (b - 1) % 2, :], b - 1, b - 1, normed, b)
            turn(xn[:, (B - 1) % 2, :], B - 1, B - 1, normed, B)
            for n in range(NT):
                k, cols = tile_of(n)
                if n == 0:
                    pe.wait_ge(conv_out, KC)
                if n >= 4:
                    pe.wait_ge(silu_out, n - 3)
                for i in range(KC):
                    mm = pe.matmul(ps[:, n % 4, :], pw[:, i, k * P:(k + 1) * P], conv[:, i, cols], start=(i == 0),
                                   stop=(i == KC - 1))
                mm.then_inc(made, 1)
            pe.wait_ge(x1_out, NT)
            for b in range(B):
                for k in range(KC):
                    mm = pe.matmul(ps[:, 4, b * E:(b + 1) * E], x1_t[:, k, b * L:(b + 1) * L], rw[:, k, :],
                                   start=(k == 0), stop=(k == KC - 1))
                mm.then_inc(made, 1)

            def expert(pair, s, b):
                n = B * s + b
                if b == 0:
                    pe.wait_ge(eb_in[s], 32 * pair + 32)
                for k in range(KC):
                    mm = pe.matmul(ps[:, n % 4, :], x1_t[:, k, b * L:(b + 1) * L], ew[:, s, k, :], start=(k == 0),
                                   stop=(k == KC - 1))
                mm.then_inc(ex_made, 1)

            for n in range(4):
                expert(0, 0, n)
            with pe.Fori(0, E // 2 - 1) as pair:
                for n in range(4, 2 * B + 4):
                    pe.wait_ge(pre_out, 2 * B * pair + n - 3)
                    if n < 2 * B:
                        expert(pair, n // B, n % B)
                    else:
                        expert(pair + 1, 0, n - 2 * B)
            for n in range(4, 2 * B):
                pe.wait_ge(pre_out, 2 * B * (E // 2 - 1) + n - 3)
                expert(E // 2 - 1, n // B, n % B)
            for b in range(B):
                turn(comb[:, b, :], b, B + b, comb_out, (E - 1) * B + b + 1)
            pe.wait_ge(copied, 2 * B)
            for n in range(NT):
                k, cols = tile_of(n)
                if n >= 4:
                    pe.wait_ge(hp_out, n - 3)
                for i in range(KC):
                    mm = pe.matmul(ps[:, n % 4, :], ow[:, i, k * P:(k + 1) * P], comb_t[:, i, cols], start=(i == 0),
                                   stop=(i == KC - 1))
                mm.then_inc(m_made, 1)
            for g in range(G):
                for k in range(KC):
                    pe.wait_ge(sq_out, G * k + g + 1)
                    mm = pe.matmul(ps[:, 4 + g, :], ones[:], sq_of(G * k + g), start=(k == 0), stop=(k == KC - 1))
                mm.then_inc(ss_made, 1)
            pe.wait_ge(h_out, NT)
            for g in range(G):
                for k in range(KC):
                    mm = pe.matmul(ps[:, g, :], fd[:, k, :], h_t[:, k, g * BANK:(g + 1) * BANK], start=(k == 0),
                                   stop=(k == KC - 1))
                mm.then_inc(fd_made, 1)
            pe.wait_ge(ff_out, G)
            for b in range(B):
                if b >= 4:
                    pe.wait_ge(fin_out, b - 3)
                s = 2 + b % 4
                pe.matmul(ps[:, s, :], ff_t[:, b * L:(b + 1) * L], fu[:], start=True, stop=False)
                for k in range(KC):
                    mm = pe.matmul(ps[:, s, k * P:(k + 1) * P], h_t[:, k, b * L:(b + 1) * L], ident[:], start=False,
                                   stop=(k == KC - 1))
                mm.then_inc(f_made, 1)


def layer(nc, a, out):
    q_scratch = nc.dram_tensor("q_scratch", (B, P, KC, L), F32, kind="Internal").ap()
    a_scratch = nc.dram_tensor("a_scratch", (B, P, KC, L), F32, kind="Internal").ap()
    queries(nc, a["x"], a["wq"], a["bq"], a["ident"], q_scratch)
    attention(nc, a["ctx"], a["wk"], a["wv"], a["bk"], a["bv"], a["ident"], q_scratch, a_scratch)
    with ExitStack() as ctx:
        st = Stage(nc, ctx, "l")
        xres = st.sb("xres", [P, B, D])
        u = st.sb("u", [P, DT, T])
        with nc.sbuf_tensor("l_gate", [P, DT, T], F32) as gate, nc.sbuf_tensor("l_xd", [P, T], F32) as xd:
            mixer_in(nc, a_scratch, a["x"], a["wo"], a["bo"], a["w_in"], a["b_in"], a["w_conv"], a["b_conv"],
                     a["w_x"], a["ident"], xres, u, gate, xd)
            mixer_scan(nc, a["w_dt"], a["a_log"], a["d_skip"], a["ident"], u, gate, xd)
        experts(nc, a, a["ident"], a["iota"], xres, u, out)


def by_rows(w):
    import numpy as np
    return np.ascontiguousarray(np.asarray(w).reshape(-1, P, w.shape[-1]).transpose(1, 0, 2))


def by_channel(v):
    import numpy as np
    return np.ascontiguousarray(np.asarray(v).reshape(-1, P).T)


def layout(i):
    import numpy as np
    i = {n: np.asarray(v) for n, v in i.items()}
    x, f = "L0_xattn_", "L0_ffn_"
    m = {n: i["L0_attn_" + n] for n in ("w_in", "b_in", "w_conv", "b_conv", "w_x", "w_dt", "A_log", "D", "w_out")}
    return {
        "x": i["x"],
        "ctx": i["ctx_1024"].reshape(B, CH, BANK, KC, P).transpose(0, 1, 4, 3, 2),
        "wq": by_rows(i[x + "Wq"].T), "bq": by_channel(i[x + "bq"]),
        "wk": by_rows(i[x + "Wk"].T), "bk": by_channel(i[x + "bk"]),
        "wv": by_rows(i[x + "Wv"].T), "bv": by_channel(i[x + "bv"]),
        "wo": by_rows(i[x + "Wo"].T), "bo": i[x + "bo"],
        "ident": np.eye(P, dtype=np.float32), "iota": np.arange(E, dtype=np.float32),
        "w_in": by_rows(m["w_in"]), "b_in": by_channel(m["b_in"]),
        "w_conv": by_rows(m["w_conv"].T), "b_conv": by_channel(m["b_conv"]),
        "w_x": by_rows(m["w_x"]), "w_dt": m["w_dt"], "a_log": by_rows(m["A_log"]), "d_skip": by_channel(m["D"]),
        "w_out": by_rows(m["w_out"]),
        "dw": by_rows(i[f + "dw_kernel"].reshape(D, K3)), "dwb": by_channel(i[f + "dw_bias"]),
        "pw": by_rows(i[f + "pw_w"].T), "pwb": by_channel(i[f + "pw_b"]),
        "rw": by_rows(i[f + "router_w"].T), "rb": i[f + "router_b"],
        "ew": i[f + "expert_w"].transpose(0, 2, 1).reshape(E, KC, P, D).transpose(0, 2, 1, 3),
        "eb": i[f + "expert_b"], "ow": by_rows(i[f + "out_w"].T), "owb": by_channel(i[f + "out_b"]),
        "nw": by_channel(i[f + "norm_w"]), "fd": by_rows(i[f + "ff_down_w"].T), "fdb": by_channel(i[f + "ff_down_b"]),
        "fu": i[f + "ff_up_w"].T, "fub": i[f + "ff_up_b"],
    }


def kernel(**inputs):
    import numpy as np
    import concourse.bacc as bacc
    from concourse.bass_utils import run_bass_kernel_spmd

    nc = bacc.Bacc("TRN2", target_bir_lowering=False, num_devices=1)
    arrays = {f"in_{n}": np.ascontiguousarray(a) for n, a in layout(inputs).items()}
    drams = {n[3:]: nc.dram_tensor(n, a.shape, F32, kind="ExternalInput").ap() for n, a in arrays.items()}
    out = nc.dram_tensor("out", (B, L, D), F32, kind="ExternalOutput").ap()
    layer(nc, drams, out)
    got = run_bass_kernel_spmd(nc, [arrays], core_ids=[0])
    return got.results[0]["out"]
```

```python
from contextlib import ExitStack

import concourse.bass as bass
from concourse import mybir

F32 = mybir.dt.float32
F32R = mybir.dt.float32r
U32 = mybir.dt.uint32
ALU = mybir.AluOpType
ACT = mybir.ActivationFunctionType
AX = mybir.AxisListType

P = 128
BANK = 512
B, L, D = 8, 128, 512
KC = D // P
T = B * L
SKV = 2048
H, DH = 16, 32
HG = P // DH
CH = SKV // BANK
KV = BANK // P
EPS = 1e-5
RING = 4


class Stage:

    def __init__(self, nc, ctx, prefix):
        self.nc, self.ctx, self.prefix = nc, ctx, prefix

    def sb(self, name, shape, dt=F32):
        return self.ctx.enter_context(self.nc.sbuf_tensor(f"{self.prefix}_{name}", shape, dt))

    def ps(self, name, shape):
        return self.ctx.enter_context(self.nc.psum_tensor(f"{self.prefix}_{name}", shape, F32))

    def sems(self, *names):
        return [self.ctx.enter_context(self.nc.semaphore(f"{self.prefix}_{n}")) for n in names]


def layer_norm_steps(eng, x, out, stats, mv, rstd, root_ready, var_ready, chain, done, b, base):
    eng.bn_stats(stats, x).then_inc(chain, 1)
    eng.wait_ge(chain, base + 1)
    eng.bn_aggr(mv, stats).then_inc(chain, 1)
    eng.wait_ge(chain, base + 2)
    eng.tensor_scalar(rstd, mv[:, 1:2], EPS, None, ALU.add).then_inc(var_ready, 1)
    eng.wait_ge(root_ready, b + 1)
    eng.reciprocal(rstd, rstd).then_inc(chain, 1)
    eng.wait_ge(chain, base + 3)
    eng.tensor_scalar(out, x, mv[:, 0:1], rstd, ALU.subtract, ALU.mult).then_inc(done, 1)


def queries(nc, x, wq_t, bq, ident_dram, q_scratch):
    with ExitStack() as ctx:
        st = Stage(nc, ctx, "q")
        xt = st.sb("x", [P, B, D])
        xn = st.sb("xn", [P, 2, D])
        xn_t = st.sb("xnT", [P, KC, T])
        w = st.sb("wq", [P, KC, D])
        bias = st.sb("bq", [P, KC])
        q_t = st.sb("qT", [P, B, KC, L])
        q_hi, q_lo = st.sb("q_hi", [P, B, KC, L], F32R), st.sb("q_lo", [P, B, KC, L], F32R)
        ident = st.sb("ident", [P, P])
        stats = st.sb("stats", [P, B, 6])
        mv = st.sb("mv", [P, B, 2])
        rstd = st.sb("rstd", [P, B])
        tp = st.ps("tp", [P, 2, BANK])
        qp = st.ps("qp", [P, 4, BANK])
        x_in, w_in, chain, var_ready, root_ready, normed, turned, copied, q_made, q_out, hi_out, lo_out, stored = st.sems(
            "x_in", "w_in", "chain", "var_ready", "root_ready", "normed", "turned", "copied", "q_made",
            "q_out", "hi_out", "lo_out", "stored")
        block = ctx.enter_context(nc.Block())
        tile_of = lambda n: (slice(4 * (n % 2), 4 * (n % 2) + 4), n // 2)

        @block.sync
        def _(sp):
            sp.dma_start(xt[:], x.rearrange("b l d -> l b d")).then_inc(x_in, 16)
            sp.dma_start(ident[:], ident_dram).then_inc(w_in, 16)
            sp.dma_start(w[:], wq_t).then_inc(w_in, 16)
            sp.dma_start(bias[:], bq).then_inc(w_in, 16)
            sp.wait_ge(hi_out, 2 * KC)
            sp.wait_ge(lo_out, 2 * KC)
            for part, src in enumerate((q_hi, q_lo)):
                for m in range(KC):
                    sp.dma_start(q_scratch[:, part, m].rearrange("b p l -> p b l"), src[:, :, m, :].bitcast(F32)).then_inc(stored, 16)
            sp.wait_ge(stored, 32 * KC)

        @block.scalar
        def _(act):
            for b in range(B):
                act.wait_ge(var_ready, b + 1)
                nc.scalar.activation(rstd[:, b:b + 1], rstd[:, b:b + 1], ACT.Sqrt).then_inc(root_ready, 1)
            for n in range(2 * KC):
                bs, m = tile_of(n)
                act.wait_ge(q_out, n + 1)
                nc.scalar.copy(q_hi[:, bs, m, :], q_t[:, bs, m, :]).then_inc(hi_out, 1)

        @block.gpsimd
        def _(pool):
            for n in range(2 * KC):
                bs, m = tile_of(n)
                pool.wait_ge(hi_out, n + 1)
                nc.gpsimd.tensor_tensor(q_lo[:, bs, m, :], q_t[:, bs, m, :], q_hi[:, bs, m, :].bitcast(F32),
                                        ALU.subtract).then_inc(lo_out, 1)

        @block.vector
        def _(dve):
            dve.wait_ge(x_in, 16)
            for b in range(B):
                if b >= 2:
                    dve.wait_ge(turned, b - 1)
                layer_norm_steps(dve, xt[:, b, :], xn[:, b % 2, :], stats[:, b, :], mv[:, b, :],
                                 rstd[:, b:b + 1], root_ready, var_ready, chain, normed, b, 3 * b)
                dve.wait_ge(turned, b + 1)
                dve.tensor_copy(xn_t[:, :, b * L:(b + 1) * L],
                                tp[:, b % 2, :].rearrange("p (k l) -> p k l", k=KC)).then_inc(copied, 1)
            dve.wait_ge(w_in, 48)
            for n in range(2 * KC):
                bs, m = tile_of(n)
                dve.wait_ge(q_made, n + 1)
                dve.tensor_scalar(q_t[:, bs, m, :], qp[:, n % 4, :].rearrange("p (b l) -> p b l", l=L),
                                  bias[:, m:m + 1], float(DH) ** -0.5, ALU.add, ALU.mult).then_inc(q_out, 1)

        @block.tensor
        def _(pe):
            pe.wait_ge(w_in, 48)
            for b in range(B):
                pe.wait_ge(normed, b + 1)
                if b >= 2:
                    pe.wait_ge(copied, b - 1)
                for k in range(KC):
                    mm = pe.transpose(tp[:, b % 2, k * L:(k + 1) * L], xn[:, b % 2, k * P:(k + 1) * P], ident[:])
                mm.then_inc(turned, 1)
            pe.wait_ge(copied, B)
            for n in range(2 * KC):
                m, g = n // 2, n % 2
                if n >= 4:
                    pe.wait_ge(q_out, n - 3)
                for k in range(KC):
                    mm = pe.matmul(qp[:, n % 4, :], w[:, k, m * P:(m + 1) * P], xn_t[:, k, g * BANK:(g + 1) * BANK],
                                   start=(k == 0), stop=(k == KC - 1))
                mm.then_inc(q_made, 1)


def attention(nc, ctx_t, wk_t, wv_t, bk, bv, ident_dram, q_scratch, k_scratch, a_scratch):
    S_RING, T_RING, PT_RING = 5, 2, 3
    with ExitStack() as ctx:
        st = Stage(nc, ctx, "a")
        raw = st.sb("raw", [P, KC, BANK])
        wk_hi, wk_lo = st.sb("wk_hi", [P, KC, D], F32R), st.sb("wk_lo", [P, KC, D], F32R)
        wv_hi, wv_lo = st.sb("wv_hi", [P, KC, D], F32R), st.sb("wv_lo", [P, KC, D], F32R)
        c_hi, c_lo = st.sb("c_hi", [P, 2, KC, BANK], F32R), st.sb("c_lo", [P, 2, KC, BANK], F32R)
        k_hi, k_lo = st.sb("k_hi", [P, 2, KC, BANK], F32R), st.sb("k_lo", [P, 2, KC, BANK], F32R)
        v = st.sb("v", [P, SKV // P, D])
        stack = st.sb("stack", [P, RING, SKV], F32R)
        q_stack = st.sb("q_stack", [P, H, L], F32R)
        probs = st.sb("probs", [P, 2, SKV])
        pt = st.sb("pt", [P, PT_RING, KV, L])
        out_t = st.sb("out_t", [P, KC, L])
        ident = st.sb("ident", [P, P])
        bias_k = st.sb("bias_k", [P, KC])
        bias_v = st.sb("bias_v", [P, D])
        mx = st.sb("mx", [P, 2, CH])
        neg_max = st.sb("neg_max", [P, 2])
        sums = st.sb("sums", [P, H, CH])
        total = st.sb("total", [P, HG])
        inv = st.sb("inv", [P, HG])
        inv_wide = st.sb("inv_wide", [P, HG, DH])
        inv_t = st.sb("inv_t", [P, L])
        s_ps = st.ps("s", [P, S_RING, BANK])
        t_ps = st.ps("t", [P, T_RING, BANK])
        o_ps = st.ps("o", [P, BANK])
        (small_in, raw_in, split_hi, split_lo, projected, khi_out, klo_out, v_out, q_in, zeroed, scored, maxed,
         negated, exped, turned, pt_act, pt_dve, inv_chain, inv_ready, inv_turned, inv_out, out_ready, a_stored, first_out, first_in,
         q_rest_in) = st.sems(
            "small_in", "raw_in", "split_hi", "split_lo", "projected", "khi_out", "klo_out", "v_out", "q_in",
            "zeroed", "scored", "maxed", "negated", "exped", "turned", "pt_act", "pt_dve", "inv_chain", "inv_ready",
            "inv_turned", "inv_out", "out_ready", "a_stored", "first_out", "first_in",
            "q_rest_in")
        k_stored = st.sems("k_stored0", "k_stored1")
        stack_in = st.sems(*[f"stack_in{s}" for s in range(RING)])
        block = ctx.enter_context(nc.Block())
        AHEAD, FIRST = 2, 2
        hi_of = [wk_hi[:], wv_hi[:], c_hi[:, 0], c_hi[:, 1]]
        lo_of = [wk_lo[:], wv_lo[:], c_lo[:, 0], c_lo[:, 1]]
        bank_of = lambda h, i: (CH * h + i) % S_RING
        tile_bank = lambda j: bank_of(H, j)
        v_tile = lambda c, j: t_ps[:, j % T_RING, :] if c == CH - 1 else s_ps[:, tile_bank(j), :]
        t_of, pt_of = lambda h, i: (CH * h + i) % T_RING, lambda h, i: (CH * h + i) % PT_RING
        act_copies = lambda h: (0, 1) if h % 2 == 0 else (0, 1, 2)
        PAIR_ACT, PAIR_DVE = 5, 3
        quarter = lambda r: slice(DH * r, DH * r + DH)

        @block.sync
        def _(sp):
            sp.dma_start(ident[:], ident_dram).then_inc(small_in, 16)
            sp.dma_start(bias_k[:], bk).then_inc(small_in, 16)
            sp.dma_start(bias_v[:], bv.partition_broadcast(P)).then_inc(small_in, 16)
            for n, src in enumerate([wk_t, wv_t, ctx_t[0, 0], ctx_t[0, 1]]):
                if n >= 1:
                    sp.wait_ge(split_lo, n)
                sp.dma_start(raw[:], src).then_inc(raw_in, 16)

            def load_stack(h):
                for r, part in enumerate((0, 0, 1)):
                    sp.dma_start(stack[quarter(r), h % RING, :].bitcast(F32),
                                 k_scratch[part, h // HG, quarter(h % HG), :]).then_inc(stack_in[h % RING], 16)

            def load_queries(b, ms, sem):
                for r, part in enumerate((0, 1, 0)):
                    sp.dma_start(q_stack[quarter(r), HG * ms.start:HG * ms.stop, :].bitcast(F32),
                                 q_scratch[b, part, ms].rearrange("m (p d) l -> d (m p) l", d=DH)).then_inc(sem, 16)

            def project(b, final):
                sp.wait_ge(scored, CH * H * b)
                load_queries(b, slice(0, 1), q_in)
                for c in range(CH):
                    if not (final and c >= CH - AHEAD):
                        sp.wait_ge(split_lo, CH * b + c + 4)
                        src = ctx_t[b, c + AHEAD] if c + AHEAD < CH else ctx_t[b + 1, c + AHEAD - CH]
                        sp.dma_start(raw[:], src).then_inc(raw_in, 16)
                    cols = slice(c * BANK, (c + 1) * BANK)
                    sp.wait_ge(khi_out, CH * KC * b + KC * c + 1)
                    sp.wait_ge(klo_out, CH * KC * b + KC * c + 1)
                    for part, src in enumerate((k_hi, k_lo)):
                        sp.dma_start(k_scratch[part, 0, :, cols], src[:, c % 2, 0].bitcast(F32)).then_inc(first_out, 16)
                    sp.wait_ge(first_out, 128 * b + 32 * c + 32)
                    for r, part in enumerate((0, 0, 1)):
                        sp.dma_start(stack[quarter(r), :, cols].bitcast(F32),
                                     k_scratch[part, 0, :, cols].rearrange("(p d) n -> d p n", d=DH))\
                          .then_inc(first_in, 16)
                    sp.wait_ge(khi_out, CH * KC * b + KC * c + KC)
                    sp.wait_ge(klo_out, CH * KC * b + KC * c + KC)
                    for part, src in enumerate((k_hi, k_lo)):
                        sp.dma_start(k_scratch[part, 1:, :, cols].rearrange("m p n -> p m n"),
                                     src[:, c % 2, 1:].bitcast(F32)).then_inc(k_stored[c % 2], 16)

            def heads(b):
                for s in range(2):
                    sp.wait_ge(k_stored[s], 64 * b + 64)
                load_queries(b, slice(1, KC), q_rest_in)
                for h in range(RING, H):
                    sp.wait_ge(scored, CH * H * b + CH * (h - RING + 1))
                    load_stack(h)
                sp.wait_ge(out_ready, KC * b + KC)
                sp.dma_start(a_scratch[b], out_t[:]).then_inc(a_stored, 16)

            project(0, False)
            with sp.Fori(0, B - 2) as b:
                heads(b)
                project(b + 1, False)
            heads(B - 2)
            project(B - 1, True)
            heads(B - 1)
            sp.wait_ge(a_stored, 16 * B)

        @block.gpsimd
        def _(pool):
            def split(n, slot):
                pool.wait_ge(split_hi, n + 1)
                nc.gpsimd.tensor_tensor(lo_of[slot], raw[:], hi_of[slot].bitcast(F32),
                                        ALU.subtract).then_inc(split_lo, 1)

            for n in range(FIRST + AHEAD):
                split(n, n)
            with pool.Fori(0, B - 1) as b:
                for c in range(CH):
                    split(CH * b + c + 4, 2 + c % 2)
            for c in range(CH - AHEAD):
                split(CH * (B - 1) + c + 4, 2 + c % 2)

        @block.scalar
        def _(act):
            def split(n, slot):
                act.wait_ge(raw_in, 16 * n + 16)
                nc.scalar.copy(hi_of[slot], raw[:]).then_inc(split_hi, 1)

            for n in range(FIRST + AHEAD):
                split(n, n)
            act.wait_ge(small_in, 48)

            def round_k(b, c, m):
                if m == 0:
                    act.wait_ge(k_stored[c % 2], 64 * b + 32 * (c // 2))
                act.wait_ge(projected, 32 * b + 8 * c + m + 1)
                nc.scalar.activation(k_hi[:, c % 2, m, :], s_ps[:, tile_bank(m), :], ACT.Identity,
                                     bias=bias_k[:, m:m + 1]).then_inc(khi_out, 1)

            def project(b, final, started):
                for c in range(CH):
                    if not (started and c == 0):
                        for m in range(KC):
                            round_k(b, c, m)
                    if c < (CH - AHEAD if final else CH - 1):
                        split_ahead(b, c)

            def split_ahead(b, c):
                act.wait_ge(projected, 32 * b + 8 * c + 8)
                split(CH * b + c + 4, 2 + c % 2)

            def empty_pt(b, h, i):
                act.wait_ge(turned, CH * H * b + CH * h + i + 1)
                nc.scalar.copy(pt[:, pt_of(h, i)], t_ps[:, t_of(h, i), :].rearrange("p (j l) -> p j l", j=KV))\
                   .then_inc(pt_act, 1)

            def exponentials(b, h, i):
                if i == 0:
                    act.wait_ge(negated, H * b + h + 1)
                nc.scalar.activation(probs[:, h % 2, i * BANK:(i + 1) * BANK], s_ps[:, bank_of(h, i), :], ACT.Exp,
                                     bias=neg_max[:, h % 2:h % 2 + 1],
                                     accum_out=sums[:, h, i:i + 1]).then_inc(exped, 1)

            def heads(b, more):
                for h in range(H):
                    for i in range(CH - 1):
                        exponentials(b, h, i)
                    if h == H - 1 and more:
                        exponentials(b, h, CH - 1)
                        split_ahead(b, CH - 1)
                        round_k(b + 1, 0, 0)
                        round_k(b + 1, 0, 1)
                        empty_pt(b, h, 0)
                        round_k(b + 1, 0, 2)
                        empty_pt(b, h, 1)
                        round_k(b + 1, 0, 3)
                        empty_pt(b, h, 2)
                    else:
                        empty_pt(b, h, 0)
                        exponentials(b, h, CH - 1)
                        for i in act_copies(h)[1:]:
                            empty_pt(b, h, i)

            project(0, False, False)
            with act.Fori(0, B - 2) as b:
                heads(b, True)
                project(b + 1, False, True)
            heads(B - 2, True)
            project(B - 1, True, True)
            heads(B - 1, False)

        @block.vector
        def _(dve):
            dve.memset(stack[quarter(3), :, :].bitcast(F32), 0.0).then_inc(zeroed, 1)
            dve.memset(q_stack[quarter(3), :, :].bitcast(F32), 0.0).then_inc(zeroed, 1)
            dve.wait_ge(small_in, 48)

            def rest_of_k(b, c, m):
                dve.wait_ge(khi_out, CH * KC * b + KC * c + m + 1)
                dve.scalar_tensor_tensor(out=k_lo[:, c % 2, m, :], in0=s_ps[:, tile_bank(m), :], scalar=bias_k[:, m:m + 1],
                                         in1=k_hi[:, c % 2, m, :].bitcast(F32), op0=ALU.add,
                                         op1=ALU.subtract).then_inc(klo_out, 1)

            def maxima(b, h, i):
                dve.wait_ge(scored, CH * H * b + CH * h + i + 1)
                dve.tensor_reduce(mx[:, h % 2, i:i + 1], s_ps[:, bank_of(h, i), :], AX.X, ALU.max).then_inc(maxed, 1)

            def negate_max(b, h):
                dve.wait_ge(maxed, CH * H * b + CH * h + CH)
                dve.tensor_reduce(neg_max[:, h % 2:h % 2 + 1], mx[:, h % 2, :], AX.X, ALU.max,
                                  negate=True).then_inc(negated, 1)

            def project(b, started):
                for c in range(CH):
                    if not (started and c == 0):
                        for m in range(KC):
                            rest_of_k(b, c, m)
                    for j in range(KV):
                        if c == CH - 1 and j >= 2:
                            maxima(b, 0, 2 * j - 4)
                            maxima(b, 0, 2 * j - 3)
                        dve.wait_ge(projected, 32 * b + 8 * c + KC + j + 1)
                        dve.tensor_tensor(v[:, KV * c + j, :], v_tile(c, j), bias_v[:], ALU.add).then_inc(v_out, 1)
                negate_max(b, 0)

            def widen_inverse(b, g):
                dve.wait_ge(exped, 64 * b + 16 * g + 16)
                dve.tensor_reduce(total[:], sums[:, HG * g:HG * g + HG, :], AX.X, ALU.add).then_inc(inv_chain, 1)
                dve.wait_ge(inv_chain, 2 * KC * b + 2 * g + 1)
                dve.reciprocal(inv[:], total[:]).then_inc(inv_chain, 1)
                dve.wait_ge(inv_chain, 2 * KC * b + 2 * g + 2)
                dve.tensor_copy(inv_wide[:], inv[:].unsqueeze(2).to_broadcast([P, HG, DH])).then_inc(inv_ready, 1)

            def empty_pt(b, h, i):
                dve.wait_ge(turned, CH * H * b + CH * h + i + 1)
                dve.tensor_copy(pt[:, pt_of(h, i)], t_ps[:, t_of(h, i), :].rearrange("p (j l) -> p j l", j=KV))\
                   .then_inc(pt_dve, 1)

            def finish_group(b, g):
                if g == 0:
                    dve.wait_ge(a_stored, 16 * b)
                dve.wait_ge(inv_turned, KC * b + g + 1)
                dve.tensor_copy(inv_t[:], o_ps[:, L:2 * L]).then_inc(inv_out, 1)
                dve.wait_ge(inv_out, KC * b + g + 1)
                dve.tensor_tensor(out_t[:, g, :], o_ps[:, :L], inv_t[:], ALU.mult).then_inc(out_ready, 1)

            def heads(b, more):
                for h in range(1, H):
                    for i in range(CH):
                        if h >= 2:
                            if i == 0 and h % 2 == 0:
                                empty_pt(b, h - 2, 2)
                            if i == 1:
                                empty_pt(b, h - 2, 3)
                                if h > HG and h % HG == 1:
                                    widen_inverse(b, h // HG - 1)
                        maxima(b, h, i)
                    negate_max(b, h)
                    if h > HG and h % HG == 1:
                        finish_group(b, h // HG - 1)
                empty_pt(b, H - 2, 2)
                if more:
                    rest_of_k(b + 1, 0, 0)
                empty_pt(b, H - 2, 3)
                if more:
                    for m in range(1, KC):
                        rest_of_k(b + 1, 0, m)
                empty_pt(b, H - 1, 3)
                widen_inverse(b, KC - 1)
                finish_group(b, KC - 1)

            project(0, False)
            with dve.Fori(0, B - 1) as b:
                heads(b, True)
                project(b + 1, True)
            heads(B - 1, False)

        @block.tensor
        def _(pe):
            pe.wait_ge(small_in, 48)

            def three(out, w_hi, w_lo, x_hi, x_lo, first, final):
                pe.matmul(out, w_hi, x_hi, start=first, stop=False)
                pe.matmul(out, w_lo, x_hi, start=False, stop=False)
                return pe.matmul(out, w_hi, x_lo, start=False, stop=final)

            def project_k(b, c, m):
                if m == 0:
                    pe.wait_ge(split_lo, CH * b + c + FIRST + 1)
                if c >= 1:
                    pe.wait_ge(v_out, 16 * b + 4 * (c - 1) + m + 1)
                part = slice(m * P, (m + 1) * P)
                for k in range(KC):
                    mm = three(s_ps[:, tile_bank(m), :], wk_hi[:, k, part], wk_lo[:, k, part], c_hi[:, c % 2, k, :],
                               c_lo[:, c % 2, k, :], k == 0, k == KC - 1)
                mm.then_inc(projected, 1)

            def project_v(b, c, j):
                if c < CH - 1:
                    pe.wait_ge(klo_out, 16 * b + 4 * c + j + 1)
                elif j >= T_RING:
                    pe.wait_ge(v_out, 16 * b + 4 * c + j - T_RING + 1)
                part = slice(j * P, (j + 1) * P)
                for k in range(KC):
                    mm = three(v_tile(c, j), c_hi[:, c % 2, k, part], c_lo[:, c % 2, k, part], wv_hi[:, k, :],
                               wv_lo[:, k, :], k == 0, k == KC - 1)
                mm.then_inc(projected, 1)

            def project(b, started):
                for c in range(CH):
                    if not (started and c == 0):
                        for m in range(KC):
                            project_k(b, c, m)
                    for j in range(KV):
                        if c == CH - 1 and j == 2:
                            for i in range(CH):
                                scores(b, 0, i)
                        project_v(b, c, j)
                        if started and c == 0 and j < 2:
                            last_values(b - 1, j)

            def scores(b, h, i):
                bank, item = bank_of(h, i), CH * h + i
                if i == 0:
                    if h < RING:
                        pe.wait_ge(first_in, 192 * b + 192)
                    else:
                        pe.wait_ge(stack_in[h % RING], (H // RING - 1) * 48 * b + 48 * (h // RING))
                        if h == HG:
                            pe.wait_ge(q_rest_in, 48 * b + 48)
                    if h == 0:
                        pe.wait_ge(zeroed, 2)
                        pe.wait_ge(q_in, 48 * b + 48)
                if item >= S_RING:
                    pe.wait_ge(exped, 64 * b + item - S_RING + 1)
                elif bank in [tile_bank(j) for j in range(KV)]:
                    j = [tile_bank(j) for j in range(KV)].index(bank)
                    pe.wait_ge(klo_out, 16 * b + 12 + j + 1)
                pe.matmul(s_ps[:, bank, :], q_stack[:, h, :], stack[:, h % RING, i * BANK:(i + 1) * BANK], start=True,
                          stop=True).then_inc(scored, 1)

            def pt_ready(b, h, i):
                if i in act_copies(h):
                    pe.wait_ge(pt_act, PAIR_ACT * (H // 2 * b + h // 2) + len(act_copies(0)) * (h % 2) + i + 1)
                else:
                    place = i - 1 if h % 2 == 0 else PAIR_DVE
                    pe.wait_ge(pt_dve, PAIR_DVE * (H // 2 * b + h // 2) + place)

            def turn(b, h, i):
                pe.wait_ge(exped, 64 * b + 4 * h + i + 1)
                n = CH * h + i
                if n < T_RING:
                    pe.wait_ge(v_out, 16 * b + 14 + n + 1)
                else:
                    pt_ready(b, (n - T_RING) // CH, (n - T_RING) % CH)
                for j in range(KV):
                    col = i * BANK + j * P
                    mm = pe.transpose(t_ps[:, t_of(h, i), j * L:(j + 1) * L], probs[:, h % 2, col:col + P], ident[:])
                mm.then_inc(turned, 1)

            def weigh(b, h, i):
                p = h % HG
                pt_ready(b, h, i)
                if i == 0 and h >= HG and p == 0:
                    pe.wait_ge(out_ready, KC * b + h // HG)
                for j in range(KV):
                    mm = pe.matmul(o_ps[DH * p:DH * p + DH, :L], v[:, KV * i + j, DH * h:DH * h + DH],
                                   pt[:, pt_of(h, i), j, :], start=(i == 0 and j == 0),
                                   stop=(i == CH - 1 and j == KV - 1), tile_position=(0, DH * p))
                if i == CH - 1 and p == HG - 1:
                    pe.wait_ge(inv_ready, KC * b + h // HG + 1)
                    pe.transpose(o_ps[:, L:2 * L], inv_wide[:].rearrange("p h d -> p (h d)"), ident[:])\
                      .then_inc(inv_turned, 1)

            def last_values(b, half):
                if half == 0:
                    weigh(b, H - 1, 0)
                    turn(b, H - 1, 3)
                    weigh(b, H - 1, 1)
                else:
                    weigh(b, H - 1, 2)
                    weigh(b, H - 1, 3)

            def heads(b, more):
                for h in range(H):
                    def ahead(i):
                        if h + 1 < H:
                            scores(b, h + 1, i)
                        elif more:
                            pe.wait_ge(exped, 64 * b + CH * H + i - S_RING + 1)
                            project_k(b + 1, 0, i)
                    ahead(0)
                    if h >= 1:
                        weigh(b, h - 1, 0)
                        turn(b, h - 1, 3)
                        weigh(b, h - 1, 1)
                    ahead(1)
                    turn(b, h, 0)
                    ahead(2)
                    if h >= 1:
                        weigh(b, h - 1, 2)
                    turn(b, h, 1)
                    ahead(3)
                    if h >= 1:
                        weigh(b, h - 1, 3)
                    turn(b, h, 2)

            project(0, False)
            with pe.Fori(0, B - 1) as b:
                heads(b, True)
                project(b + 1, True)
            heads(B - 1, False)
            for half in range(2):
                last_values(B - 1, half)


DIN = 2 * D
DT = DIN // P
N, DTR, TW = 16, 64, 4
XD = DTR + 2 * N
G, BG = 2, B // 2


def mixer_in(nc, a_scratch, x, wo_t, bo, w_in, b_in, w_conv, b_conv, w_x, ident_dram, xres, u, gate, xd):
    with ExitStack() as ctx:
        st = Stage(nc, ctx, "m")
        at = st.sb("at", [P, B, KC, L])
        wo = st.sb("wo", [P, KC, D])
        bo_all = st.sb("bo", [P, D])
        wi = st.sb("wi", [P, KC, 2 * DIN])
        bi = st.sb("bi", [P, 2 * DT])
        wc = st.sb("wc", [P, DT, TW])
        bc = st.sb("bc", [P, DT])
        wx = st.sb("wx", [P, DT, XD])
        ident = st.sb("ident", [P, P])
        xn = st.sb("xn", [P, 2, D])
        xn_t = st.sb("xnT", [P, KC, T])
        PADDED = L + TW - 1
        xc = st.sb("xc", [P, 2, B, PADDED])
        acc = st.sb("acc", [P, 2, B, L])
        stats, mv, rstd = st.sb("stats", [P, B, 6]), st.sb("mv", [P, B, 2]), st.sb("rstd", [P, B])
        op = st.ps("op", [P, 2, BANK])
        tp = st.ps("tp", [P, 2, BANK])
        ip = st.ps("ip", [P, 4, BANK])
        (w_in_s, x_in, biased, o_made, added, chain, var_ready, root_ready, normed, turned, copied, i_made,
         i_out, taps, conv_done, u_done, padded, xd_made, xd_out) = st.sems(
            "w_in", "x_in", "biased", "o_made", "added", "chain", "var_ready", "root_ready", "normed", "turned",
            "copied", "i_made", "i_out", "taps", "conv_done", "u_done", "padded", "xd_made", "xd_out")
        block = ctx.enter_context(nc.Block())

        @block.sync
        def _(sp):
            sp.dma_start(xres[:], x.rearrange("b l d -> l b d")).then_inc(x_in, 16)
            sp.dma_start(bo_all[:], bo.partition_broadcast(P)).then_inc(x_in, 16)
            sp.dma_start(wo[:], wo_t).then_inc(w_in_s, 16)
            sp.dma_start(at[:], a_scratch.rearrange("b p m l -> p b m l")).then_inc(w_in_s, 16)
            for dst, src in ((ident, ident_dram), (wi, w_in), (bi, b_in), (wc, w_conv), (bc, b_conv), (wx, w_x)):
                sp.dma_start(dst[:], src).then_inc(w_in_s, 16)

        @block.gpsimd
        def _(pool):
            nc.gpsimd.memset(xc[:, :, :, 0:TW - 1], 0.0).then_inc(padded, 1)
            pool.wait_ge(x_in, 32)
            for b in range(B):
                nc.gpsimd.tensor_tensor(xres[:, b, :], xres[:, b, :], bo_all[:], ALU.add).then_inc(biased, 1)

        @block.scalar
        def _(act):
            for b in range(B):
                act.wait_ge(var_ready, b + 1)
                nc.scalar.activation(rstd[:, b:b + 1], rstd[:, b:b + 1], ACT.Sqrt).then_inc(root_ready, 1)
            act.wait_ge(w_in_s, 128)
            act.wait_ge(padded, 1)
            for c in range(2 * DT):
                for g in range(G):
                    n = G * c + g
                    act.wait_ge(i_made, n + 1)
                    if c < DT:
                        if c >= 2 and g == 0:
                            act.wait_ge(conv_done, c - 1)
                        nc.scalar.activation(xc[:, c % 2, BG * g:BG * g + BG, TW - 1:],
                                             ip[:, n % 4, :].rearrange("p (b l) -> p b l", l=L), ACT.Identity,
                                             bias=bi[:, c:c + 1]).then_inc(i_out, 1)
                    else:
                        nc.scalar.activation(gate[:, c - DT, g * BANK:(g + 1) * BANK], ip[:, n % 4, :], ACT.Silu,
                                             bias=bi[:, c:c + 1]).then_inc(i_out, 1)
                if 1 <= c <= DT:
                    act.wait_ge(conv_done, c)
                    nc.scalar.activation(u[:, c - 1, :], acc[:, (c - 1) % 2].rearrange("p b l -> p (b l)"), ACT.Silu,
                                         bias=bc[:, c - 1:c]).then_inc(u_done, 1)

        @block.vector
        def _(dve):
            def finish_norm(b):
                dve.wait_ge(turned, b + 1)
                dve.tensor_copy(xn_t[:, :, b * L:(b + 1) * L],
                                tp[:, b % 2, :].rearrange("p (k l) -> p k l", k=KC)).then_inc(copied, 1)

            for b in range(B):
                dve.wait_ge(o_made, b + 1)
                dve.wait_ge(biased, b + 1)
                dve.tensor_tensor(xres[:, b, :], xres[:, b, :], op[:, b % 2, :], ALU.add).then_inc(added, 1)
                dve.wait_ge(added, b + 1)
                if b >= 2:
                    dve.wait_ge(turned, b - 1)
                layer_norm_steps(dve, xres[:, b, :], xn[:, b % 2, :], stats[:, b, :], mv[:, b, :],
                                 rstd[:, b:b + 1], root_ready, var_ready, chain, normed, b, 3 * b)
                if b >= 1:
                    finish_norm(b - 1)
            finish_norm(B - 1)
            dve.wait_ge(w_in_s, 128)
            for c in range(DT):
                dve.wait_ge(i_out, G * c + G)
                if c >= 2:
                    dve.wait_ge(u_done, c - 1)
                s = c % 2
                dve.tensor_scalar(acc[:, s], xc[:, s, :, TW - 1:TW - 1 + L], wc[:, c, TW - 1:TW], None,
                                  ALU.mult).then_inc(taps, 1)
                for k in range(TW - 1):
                    dve.wait_ge(taps, 3 * c + k + 1)
                    dve.scalar_tensor_tensor(out=acc[:, s], in0=xc[:, s, :, k:k + L], scalar=wc[:, c, k:k + 1],
                                             in1=acc[:, s], op0=ALU.mult, op1=ALU.add)\
                       .then_inc(conv_done if k == TW - 2 else taps, 1)
            for g in range(G):
                dve.wait_ge(xd_made, g + 1)
                dve.tensor_copy(xd[0:XD, g * BANK:(g + 1) * BANK], op[0:XD, g, :]).then_inc(xd_out, 1)

        @block.tensor
        def _(pe):
            pe.wait_ge(w_in_s, 128)

            def turn(b):
                pe.wait_ge(normed, b + 1)
                if b >= 2:
                    pe.wait_ge(copied, b - 1)
                for k in range(KC):
                    mm = pe.transpose(tp[:, b % 2, k * L:(k + 1) * L], xn[:, b % 2, k * P:(k + 1) * P], ident[:])
                mm.then_inc(turned, 1)

            for b in range(B):
                if b >= 2:
                    pe.wait_ge(added, b - 1)
                for k in range(KC):
                    mm = pe.matmul(op[:, b % 2, :], at[:, b, k, :], wo[:, k, :], start=(k == 0), stop=(k == KC - 1))
                mm.then_inc(o_made, 1)
                if b >= 1:
                    turn(b - 1)
            turn(B - 1)
            pe.wait_ge(copied, B)
            for c in range(2 * DT):
                for g in range(G):
                    n = G * c + g
                    if n >= 4:
                        pe.wait_ge(i_out, n - 3)
                    for k in range(KC):
                        mm = pe.matmul(ip[:, n % 4, :], wi[:, k, c * P:(c + 1) * P],
                                       xn_t[:, k, g * BANK:(g + 1) * BANK], start=(k == 0), stop=(k == KC - 1))
                    mm.then_inc(i_made, 1)
            pe.wait_ge(u_done, DT)
            for g in range(G):
                for c in range(DT):
                    mm = pe.matmul(op[0:XD, g, :], wx[:, c, :], u[:, c, g * BANK:(g + 1) * BANK],
                                   start=(c == 0), stop=(c == DT - 1))
                mm.then_inc(xd_made, 1)


def mixer_scan(nc, w_dt, a_log, d_skip, ident_dram, u, gate, xd):
    with ExitStack() as ctx:
        st = Stage(nc, ctx, "s")
        wd = st.sb("wd", [P, DIN])
        a_neg = st.sb("a_neg", [P, DT, N])
        dsk = st.sb("dsk", [P, DT])
        ident = st.sb("ident", [P, P])
        bc = st.sb("bc", [P, 2 * N, BANK])
        delta = st.sb("delta", [P, DT, BANK])
        du = st.sb("du", [P, 2, BANK])
        decay = st.sb("decay", [P, 2, BG, L + 1])
        drive = st.sb("drive", [P, 2, BG, L + 1])
        state = st.sb("state", [P, 2, BG, L + 1])
        seen = st.sb("seen", [P, 2, BG, L])
        skip = st.sb("skip", [P, 2, BANK])
        ps = st.ps("ps", [P, 8, BANK])
        (w_in, a_ready, zeroed, spread, odd_out, even_out, d_made, abs_out, exp_out, log_out, delta_out, du_out, decayed,
         driven, scanned, weighed, summed, skipped, y_out) = st.sems(
            "w_in", "a_ready", "zeroed", "spread", "odd_out", "even_out", "d_made", "abs_out", "exp_out", "log_out", "delta_out",
            "du_out", "decayed", "driven", "scanned", "weighed", "summed", "skipped", "y_out")
        block = ctx.enter_context(nc.Block())
        flat = lambda t: t.rearrange("p b l -> p (b l)")
        SPREAD_BANKS = 4
        UN = 2
        STEPS = UN * N

        @block.sync
        def _(sp):
            for dst, src in ((wd[0:DTR, :], w_dt), (a_neg[:], a_log), (dsk[:], d_skip), (ident[:], ident_dram)):
                sp.dma_start(dst, src).then_inc(w_in, 16)

        @block.gpsimd
        def _(pool):
            nc.gpsimd.memset(decay[:], 0.0).then_inc(zeroed, 1)
            nc.gpsimd.memset(drive[:], 0.0).then_inc(zeroed, 1)
            pool.wait_ge(zeroed, 2)

            def step(g, pair, s):
                n = s % N
                if n == 0:
                    pool.wait_ge(du_out, DT * g + UN * pair + s // N + 1)
                done = N * DT * g + STEPS * pair + s
                pool.wait_ge(scanned, done + 1)
                nc.gpsimd.tensor_tensor(drive[:, s % 2, :, 1:], du[:, s // N].rearrange("p (b l) -> p b l", l=L),
                                        bc[:, n, :].rearrange("p (b l) -> p b l", l=L), ALU.mult).then_inc(driven, 1)

            for g in range(G):
                pool.wait_ge(even_out, N * (g + 1))
                pool.wait_ge(odd_out, N * (g + 1))
                with pool.Fori(0, DT // UN) as pair:
                    for s in range(STEPS):
                        step(g, pair, s)

        @block.scalar
        def _(act):
            act.wait_ge(w_in, 64)
            nc.scalar.activation(a_neg[:], a_neg[:], ACT.Exp).then_inc(a_ready, 1)
            act.wait_ge(zeroed, 2)
            act.wait_ge(a_ready, 2)
            for g in range(G):
                for r in range(1, 2 * N, 2):
                    act.wait_ge(spread, 2 * N * g + r + 1)
                    nc.scalar.copy(bc[:, r, :], ps[:, r % SPREAD_BANKS, :]).then_inc(odd_out, 1)
                for d in range(DT):
                    act.wait_ge(d_made, DT * g + d + 1)
                    nc.scalar.activation(delta[:, d, :], ps[:, d, :], ACT.Abs).then_inc(abs_out, 1)
                for d in range(DT):
                    act.wait_ge(abs_out, DT * g + d + 1)
                    nc.scalar.activation(delta[:, d, :], delta[:, d, :], ACT.Exp, scale=-1.0).then_inc(exp_out, 1)
                for d in range(DT):
                    act.wait_ge(exp_out, DT * g + d + 1)
                    nc.scalar.activation(delta[:, d, :], delta[:, d, :], ACT.Ln, bias=1.0).then_inc(log_out, 1)
                act.wait_ge(delta_out, DT * g + DT)
                with act.Fori(0, DT // UN) as pair:
                    for s in range(STEPS):
                        n, d = s % N, UN * pair + s // N
                        act.wait_ge(scanned, N * DT * g + STEPS * pair + s + 1)
                        nc.scalar.activation(decay[:, s % 2, :, 1:],
                                             delta[:, d, :].rearrange("p (b l) -> p b l", l=L), ACT.Exp,
                                             scale=a_neg[:, d, n:n + 1]).then_inc(decayed, 1)

        @block.vector
        def _(dve):
            dve.wait_ge(a_ready, 1)
            dve.tensor_scalar(a_neg[:], a_neg[:], -1.0, None, ALU.mult).then_inc(a_ready, 1)
            dve.memset(state[:, 0, :, 0:1], 0.0).then_inc(scanned, 2)
            for g in range(G):
                for r in range(0, 2 * N, 2):
                    dve.wait_ge(spread, 2 * N * g + r + 1)
                    dve.tensor_copy(bc[:, r, :], ps[:, r % SPREAD_BANKS, :]).then_inc(even_out, 1)
                for d in range(DT):
                    dve.wait_ge(log_out, DT * g + d + 1)
                    dve.scalar_tensor_tensor(out=delta[:, d, :], in0=ps[:, d, :], scalar=0.0, in1=delta[:, d, :],
                                             op0=ALU.max, op1=ALU.add).then_inc(delta_out, 1)
                dve.wait_ge(delta_out, DT * g + DT)
                cols = slice(g * BANK, (g + 1) * BANK)
                with dve.Fori(0, DT // UN) as pair:
                    before = N * DT * g + STEPS * pair

                    def make_du(i):
                        d = UN * pair + i
                        dve.tensor_tensor(du[:, i, :], delta[:, d, :], u[:, d, cols], ALU.mult).then_inc(du_out, 1)

                    def weigh(s):
                        dve.wait_ge(scanned, before + s + 3)
                        dve.wait_ge(summed, before + s + 1)
                        dve.tensor_tensor(seen[:, s % 2], state[:, s % 2, :, 1:],
                                          bc[:, N + s % N, :].rearrange("p (b l) -> p b l", l=L), ALU.mult)\
                           .then_inc(weighed, 1)

                    def finish(i):
                        d = UN * pair + i
                        dve.wait_ge(summed, before + N * i + N + 2)
                        dve.scalar_tensor_tensor(out=skip[:, i, :], in0=u[:, d, cols], scalar=dsk[:, bass.ds(d, 1)],
                                                 in1=ps[:, i, :], op0=ALU.mult, op1=ALU.add).then_inc(skipped, 1)
                        dve.wait_ge(skipped, DT * g + UN * pair + i + 1)
                        dve.tensor_tensor(u[:, d, cols], skip[:, i, :], gate[:, d, cols], ALU.mult).then_inc(y_out, 1)

                    make_du(0)
                    make_du(1)
                    for s in range(STEPS):
                        dve.wait_ge(decayed, before + s + 1)
                        dve.wait_ge(driven, before + s + 1)
                        if s >= 2:
                            dve.wait_ge(weighed, before + s - 1)
                        dve.tensor_tensor_scan(flat(state[:, s % 2]), flat(decay[:, s % 2]), flat(drive[:, s % 2]),
                                               0.0, ALU.mult, ALU.add).then_inc(scanned, 1)
                        if s >= 1:
                            weigh(s - 1)
                        if s == N + 2:
                            finish(0)
                    weigh(STEPS - 1)
                    finish(1)

        @block.tensor
        def _(pe):
            pe.wait_ge(w_in, 64)
            pe.transpose(ps[:, 7, :P], ident[:], ident[:]).then_inc(summed, 2)
            for g in range(G):
                cols = slice(g * BANK, (g + 1) * BANK)
                if g >= 1:
                    pe.wait_ge(y_out, DT * g)
                for r in range(2 * N):
                    if r >= SPREAD_BANKS:
                        pe.wait_ge(odd_out if r % 2 else even_out, N * g + (r - SPREAD_BANKS) // 2 + 1)
                    row = DTR + r
                    pe.matmul(ps[:, r % SPREAD_BANKS, :], ident[0:XD, row:row + 1].to_broadcast([XD, P]),
                              xd[0:XD, cols], start=True, stop=True).then_inc(spread, 1)
                pe.wait_ge(even_out, N * (g + 1))
                pe.wait_ge(odd_out, N * (g + 1))
                for d in range(DT):
                    pe.matmul(ps[:, d, :], wd[0:DTR, d * P:(d + 1) * P], xd[0:DTR, cols],
                              start=True, stop=True).then_inc(d_made, 1)
                pe.wait_ge(delta_out, DT * (g + 1))
                with pe.Fori(0, DT // UN) as pair:
                    for s in range(STEPS):
                        i, n = s // N, s % N
                        pe.wait_ge(weighed, N * DT * g + STEPS * pair + s + 1)
                        pe.matmul(ps[:, i, :], ident[:], flat(seen[:, s % 2]), start=(n == 0), stop=(n == N - 1))\
                          .then_inc(summed, 1)


E = 8
HID = D // 4
K3 = 3


def experts(nc, w, ident_dram, iota, xres, u, out):
    with ExitStack() as ctx:
        st = Stage(nc, ctx, "e")
        ident = st.sb("ident", [P, P])
        ones = st.sb("ones", [P, P])
        wo = st.sb("w_out", [P, DT, D])
        xn = st.sb("xn", [P, 2, D])
        PADDED = L + K3 - 1
        xf_t = st.sb("xfT", [P, KC, B, PADDED])
        x1_t = st.sb("x1T", [P, KC, T])
        h_t = st.sb("hT", [P, KC, T])
        rms = st.sb("rms", [P, G, BANK])
        ff_t = st.sb("ffT", [P, T])
        pw, ow = st.sb("pw", [P, KC, D]), st.sb("ow", [P, KC, D])
        dw, dwb, pwb = st.sb("dw", [P, KC, K3]), st.sb("dwb", [P, KC]), st.sb("pwb", [P, KC])
        rw, rb = st.sb("rw", [P, KC, E]), st.sb("rb", [P, E])
        owb, nw, fdb = st.sb("owb", [P, KC]), st.sb("nw", [P, KC]), st.sb("fdb", [P, 1])
        fd, fu, fub = st.sb("fd", [P, KC, HID]), st.sb("fu", [HID, D]), st.sb("fub", [P, D])
        ew, eb = st.sb("ew", [P, 2, KC, D]), st.sb("eb", [P, 2, D])
        pre, act_e = st.sb("pre", [P, 2, D]), st.sb("act_e", [P, 2, D])
        stats, mv, rstd = st.sb("stats", [P, B, 6]), st.sb("mv", [P, B, 2]), st.sb("rstd", [P, B])
        logits, top = st.sb("logits", [P, B, E]), st.sb("top", [P, B, E])
        index = st.sb("index", [P, B, E], U32)
        chosen = st.sb("chosen", [P, B, E])
        numbers = st.sb("numbers", [P, E])
        share = st.sb("share", [P, 4, B])
        route, second = st.sb("route", [P, B, E]), st.sb("second", [P, B, E])
        uu = u.rearrange("p c t -> p (c t)")
        conv = uu[:, 0:KC * T].rearrange("p (k t) -> p k t", k=KC)
        comb = uu[:, KC * T:2 * KC * T].rearrange("p (b d) -> p b d", b=B)
        comb_t, hp_t = conv, comb.rearrange("p b d -> p (b d)").rearrange("p (k t) -> p k t", k=KC)
        ps = st.ps("ps", [P, 6, BANK])
        tp = st.ps("tp", [P, 2, BANK])
        (w_in, eb_in0, eb_in1, made, added, chain, var_ready, root_ready, normed, turned, copied, padded, taps,
         conv_out, silu_out, x1_out, lg_out, dstep, astep, routed, ex_made, pre_out, act_out, comb_out, zeroed,
         m_made, hp_out, sq_out, ss_made, rms_out, h_out, fd_made, ff_out, f_made, fin_out, biased, stored) = st.sems(
            "w_in", "eb_in0", "eb_in1", "made", "added", "chain", "var_ready", "root_ready", "normed", "turned",
            "copied", "padded", "taps", "conv_out", "silu_out", "x1_out", "lg_out", "dstep", "astep", "routed",
            "ex_made", "pre_out", "act_out", "comb_out", "zeroed", "m_made", "hp_out", "sq_out", "ss_made",
            "rms_out", "h_out", "fd_made", "ff_out", "f_made", "fin_out", "biased", "stored")
        eb_in = [eb_in0, eb_in1]
        block = ctx.enter_context(nc.Block())
        sq_of = lambda n: h_t[:, n // G, (n % G) * BANK:(n % G + 1) * BANK]
        NT = KC * G
        tile_of = lambda n: (n // G, slice((n % G) * BANK, (n % G + 1) * BANK))

        @block.sync
        def _(sp):
            loads = ((ident, ident_dram), (wo, w["w_out"]), (dw, w["dw"]), (dwb, w["dwb"]), (pw, w["pw"]),
                     (pwb, w["pwb"]), (rw, w["rw"]), (ow, w["ow"]), (owb, w["owb"]), (nw, w["nw"]), (fd, w["fd"]),
                     (fdb, w["fdb"]), (fu, w["fu"]), (numbers, iota.partition_broadcast(P)),
                     (rb, w["rb"].partition_broadcast(P)), (fub, w["fub"].partition_broadcast(P)))
            assert len(loads) == 16
            for dst, src in loads:
                sp.dma_start(dst[:], src).then_inc(w_in, 16)

            def load_expert(e, s):
                sp.dma_start(ew[:, s], w["ew"][e]).then_inc(eb_in[s], 16)
                sp.dma_start(eb[:, s, :], w["eb"][e].partition_broadcast(P)).then_inc(eb_in[s], 16)

            load_expert(0, 0)
            load_expert(1, 1)
            with sp.Fori(0, E // 2 - 1) as pair:
                for s in range(2):
                    sp.wait_ge(pre_out, 2 * B * pair + B * s + B)
                    load_expert(2 * pair + 2 + s, s)
            for b in range(B):
                sp.wait_ge(fin_out, b + 1)
                sp.dma_start(out[b], xres[:, b, :]).then_inc(stored, 16)
            sp.wait_ge(stored, 16 * B)

        @block.gpsimd
        def _(pool):
            nc.gpsimd.memset(xf_t[:, :, :, 0:K3 - 1], 0.0).then_inc(padded, 1)
            nc.gpsimd.memset(ones[:], 1.0).then_inc(padded, 1)
            pool.wait_ge(w_in, 256)
            pool.wait_ge(normed, B)
            for b in range(B):
                nc.gpsimd.tensor_tensor(xres[:, b, :], xres[:, b, :], fub[:], ALU.add).then_inc(biased, 1)
            pool.wait_ge(made, B)
            nc.gpsimd.memset(comb[:], 0.0).then_inc(zeroed, 1)

        @block.scalar
        def _(act):
            for b in range(B):
                act.wait_ge(var_ready, b + 1)
                nc.scalar.activation(rstd[:, b:b + 1], rstd[:, b:b + 1], ACT.Sqrt).then_inc(root_ready, 1)
            for n in range(NT):
                k, cols = tile_of(n)
                act.wait_ge(made, B + n + 1)
                nc.scalar.activation(h_t[:, k, cols], ps[:, n % 4, :], ACT.Silu, bias=pwb[:, k:k + 1])\
                   .then_inc(silu_out, 1)
            act.wait_ge(dstep, 2)
            nc.scalar.activation(share[:, 1, :], share[:, 0, :], ACT.Exp).then_inc(astep, 1)

            def silu(pair, s, b):
                n = B * s + b
                act.wait_ge(pre_out, 2 * B * pair + n + 1)
                nc.scalar.activation(act_e[:, n % 2, :], pre[:, n % 2, :], ACT.Silu).then_inc(act_out, 1)

            with act.Fori(0, E // 2) as pair:
                for s in range(2):
                    for b in range(B):
                        silu(pair, s, b)
            for g in range(G):
                act.wait_ge(ss_made, g + 1)
                nc.scalar.activation(rms[:, g, :], ps[:, 4 + g, :], ACT.Sqrt, scale=1.0 / D).then_inc(astep, 1)
            for g in range(G):
                act.wait_ge(fd_made, g + 1)
                nc.scalar.activation(ff_t[:, g * BANK:(g + 1) * BANK], ps[:, g, :], ACT.Gelu, bias=fdb[:, 0:1])\
                   .then_inc(ff_out, 1)

        @block.vector
        def _(dve):
            def finish_norm(b):
                dve.wait_ge(turned, b + 1)
                dve.tensor_copy(xf_t[:, :, b, K3 - 1:],
                                tp[:, b % 2, :].rearrange("p (k l) -> p k l", k=KC)).then_inc(copied, 1)

            dve.wait_ge(w_in, 256)
            for b in range(B):
                dve.wait_ge(made, b + 1)
                dve.tensor_tensor(xres[:, b, :], xres[:, b, :], ps[:, b % 4, :], ALU.add).then_inc(added, 1)
                dve.wait_ge(added, b + 1)
                if b >= 2:
                    dve.wait_ge(turned, b - 1)
                layer_norm_steps(dve, xres[:, b, :], xn[:, b % 2, :], stats[:, b, :], mv[:, b, :],
                                 rstd[:, b:b + 1], root_ready, var_ready, chain, normed, b, 3 * b)
                if b >= 1:
                    finish_norm(b - 1)
            finish_norm(B - 1)
            dve.wait_ge(padded, 2)
            dve.wait_ge(copied, B)
            for k in range(KC):
                c = conv[:, k, :].rearrange("p (b l) -> p b l", l=L)
                dve.tensor_scalar(c, xf_t[:, k, :, K3 - 1:], dw[:, k, K3 - 1:K3], dwb[:, k:k + 1], ALU.mult,
                                  ALU.add).then_inc(taps, 1)
                for j in range(K3 - 1):
                    dve.wait_ge(taps, 2 * k + j + 1)
                    dve.scalar_tensor_tensor(out=c, in0=xf_t[:, k, :, j:j + L], scalar=dw[:, k, j:j + 1], in1=c,
                                             op0=ALU.mult, op1=ALU.add).then_inc(conv_out if j else taps, 1)
            for n in range(NT):
                k, cols = tile_of(n)
                g = n % G
                dve.wait_ge(silu_out, n + 1)
                dve.tensor_tensor(x1_t[:, k, cols].rearrange("p (b l) -> p b l", l=L),
                                  xf_t[:, k, BG * g:BG * g + BG, K3 - 1:],
                                  h_t[:, k, cols].rearrange("p (b l) -> p b l", l=L), ALU.add).then_inc(x1_out, 1)
            dve.wait_ge(made, B + NT + B)
            dve.tensor_tensor(logits[:], ps[:, 4, 0:B * E].rearrange("p (b e) -> p b e", e=E),
                              rb[:].unsqueeze(1).to_broadcast([P, B, E]), ALU.add).then_inc(lg_out, 1)
            dve.wait_ge(lg_out, 1)
            for b in range(B):
                dve.max(top[:, b, :], logits[:, b, :]).then_inc(lg_out, 1)
            for b in range(B):
                dve.wait_ge(lg_out, b + 2)
                dve.max_index(index[:, b, :], top[:, b, :], logits[:, b, :]).then_inc(lg_out, 1)
            dve.wait_ge(lg_out, 2 * B + 1)
            dve.tensor_copy(chosen[:], index[:]).then_inc(dstep, 1)
            dve.tensor_tensor(share[:, 0, :], top[:, :, 1], top[:, :, 0], ALU.subtract).then_inc(dstep, 1)
            dve.wait_ge(astep, 1)
            dve.tensor_scalar(share[:, 2, :], share[:, 1, :], 1.0, None, ALU.add).then_inc(dstep, 1)
            dve.wait_ge(dstep, 3)
            dve.reciprocal(share[:, 2, :], share[:, 2, :]).then_inc(dstep, 1)
            dve.wait_ge(dstep, 4)
            dve.tensor_tensor(share[:, 3, :], share[:, 1, :], share[:, 2, :], ALU.mult).then_inc(dstep, 1)
            wide = lambda a: a.unsqueeze(2).to_broadcast([P, B, E])
            every = numbers[:].unsqueeze(1).to_broadcast([P, B, E])
            dve.tensor_tensor(route[:], every, wide(chosen[:, :, 0]), ALU.is_equal).then_inc(dstep, 1)
            dve.tensor_tensor(second[:], every, wide(chosen[:, :, 1]), ALU.is_equal).then_inc(dstep, 1)
            dve.wait_ge(dstep, 7)
            dve.tensor_tensor(route[:], route[:], wide(share[:, 2, :]), ALU.mult).then_inc(dstep, 1)
            dve.tensor_tensor(second[:], second[:], wide(share[:, 3, :]), ALU.mult).then_inc(dstep, 1)
            dve.wait_ge(dstep, 9)
            dve.tensor_tensor(route[:], route[:], second[:], ALU.add).then_inc(routed, 1)
            dve.wait_ge(routed, 1)
            dve.wait_ge(zeroed, 1)

            def biased_expert(pair, s, b):
                n = B * s + b
                if b == 0:
                    dve.wait_ge(eb_in[s], 32 * pair + 32)
                dve.wait_ge(ex_made, 2 * B * pair + n + 1)
                dve.tensor_tensor(pre[:, n % 2, :], ps[:, n % 4, :], eb[:, s, :], ALU.add).then_inc(pre_out, 1)

            def accumulate(pair, s, b):
                n = B * s + b
                dve.wait_ge(act_out, 2 * B * pair + n + 1)
                e = 2 * pair + s
                dve.scalar_tensor_tensor(out=comb[:, b, :], in0=act_e[:, n % 2, :], scalar=route[:, b, bass.ds(e, 1)],
                                         in1=comb[:, b, :], op0=ALU.mult, op1=ALU.add).then_inc(comb_out, 1)

            with dve.Fori(0, E // 2) as pair:
                for n in range(2 * B + 1):
                    if n < 2 * B:
                        biased_expert(pair, n // B, n % B)
                    if n >= 1:
                        accumulate(pair, (n - 1) // B, (n - 1) % B)
            for b in range(B):
                dve.wait_ge(turned, B + b + 1)
                dve.tensor_copy(comb_t[:, :, b * L:(b + 1) * L],
                                tp[:, b % 2, :].rearrange("p (k l) -> p k l", k=KC)).then_inc(copied, 1)
            for n in range(NT):
                k, cols = tile_of(n)
                dve.wait_ge(m_made, n + 1)
                dve.scalar_tensor_tensor(out=hp_t[:, k, cols], in0=ps[:, n % 4, :], scalar=owb[:, k:k + 1],
                                         in1=x1_t[:, k, cols], op0=ALU.add, op1=ALU.add).then_inc(hp_out, 1)
                dve.wait_ge(hp_out, n + 1)
                dve.tensor_tensor(sq_of(n), hp_t[:, k, cols], hp_t[:, k, cols], ALU.mult).then_inc(sq_out, 1)
            for g in range(G):
                dve.wait_ge(astep, 2 + g)
                dve.reciprocal(rms[:, g, :], rms[:, g, :]).then_inc(rms_out, 1)
            for n in range(NT):
                k, cols = tile_of(n)
                if n < G:
                    dve.wait_ge(rms_out, n + 1)
                dve.scalar_tensor_tensor(out=h_t[:, k, cols], in0=hp_t[:, k, cols], scalar=nw[:, k:k + 1],
                                         in1=rms[:, n % G, :], op0=ALU.mult, op1=ALU.mult).then_inc(h_out, 1)
            for b in range(B):
                dve.wait_ge(f_made, b + 1)
                dve.wait_ge(biased, b + 1)
                dve.tensor_tensor(xres[:, b, :], xres[:, b, :], ps[:, 2 + b % 4, :], ALU.add).then_inc(fin_out, 1)

        @block.tensor
        def _(pe):
            pe.wait_ge(w_in, 256)

            def turn(src, b, count, ready, value):
                pe.wait_ge(ready, value)
                if count >= 2:
                    pe.wait_ge(copied, count - 1)
                for k in range(KC):
                    mm = pe.transpose(tp[:, b % 2, k * L:(k + 1) * L], src[:, k * P:(k + 1) * P], ident[:])
                mm.then_inc(turned, 1)

            for b in range(B):
                if b >= 4:
                    pe.wait_ge(added, b - 3)
                for c in range(DT):
                    mm = pe.matmul(ps[:, b % 4, :], u[:, c, b * L:(b + 1) * L], wo[:, c, :], start=(c == 0),
                                   stop=(c == DT - 1))
                mm.then_inc(made, 1)
                if b >= 1:
                    turn(xn[:, (b - 1) % 2, :], b - 1, b - 1, normed, b)
            turn(xn[:, (B - 1) % 2, :], B - 1, B - 1, normed, B)
            for n in range(NT):
                k, cols = tile_of(n)
                if n == 0:
                    pe.wait_ge(conv_out, KC)
                if n >= 4:
                    pe.wait_ge(silu_out, n - 3)
                for i in range(KC):
                    mm = pe.matmul(ps[:, n % 4, :], pw[:, i, k * P:(k + 1) * P], conv[:, i, cols], start=(i == 0),
                                   stop=(i == KC - 1))
                mm.then_inc(made, 1)
            pe.wait_ge(x1_out, NT)
            for b in range(B):
                for k in range(KC):
                    mm = pe.matmul(ps[:, 4, b * E:(b + 1) * E], x1_t[:, k, b * L:(b + 1) * L], rw[:, k, :],
                                   start=(k == 0), stop=(k == KC - 1))
                mm.then_inc(made, 1)

            def expert(pair, s, b):
                n = B * s + b
                if b == 0:
                    pe.wait_ge(eb_in[s], 32 * pair + 32)
                for k in range(KC):
                    mm = pe.matmul(ps[:, n % 4, :], x1_t[:, k, b * L:(b + 1) * L], ew[:, s, k, :], start=(k == 0),
                                   stop=(k == KC - 1))
                mm.then_inc(ex_made, 1)

            for n in range(4):
                expert(0, 0, n)
            with pe.Fori(0, E // 2 - 1) as pair:
                for n in range(4, 2 * B + 4):
                    pe.wait_ge(pre_out, 2 * B * pair + n - 3)
                    if n < 2 * B:
                        expert(pair, n // B, n % B)
                    else:
                        expert(pair + 1, 0, n - 2 * B)
            for n in range(4, 2 * B):
                pe.wait_ge(pre_out, 2 * B * (E // 2 - 1) + n - 3)
                expert(E // 2 - 1, n // B, n % B)
            for b in range(B):
                turn(comb[:, b, :], b, B + b, comb_out, (E - 1) * B + b + 1)
            pe.wait_ge(copied, 2 * B)
            for n in range(NT):
                k, cols = tile_of(n)
                if n >= 4:
                    pe.wait_ge(hp_out, n - 3)
                for i in range(KC):
                    mm = pe.matmul(ps[:, n % 4, :], ow[:, i, k * P:(k + 1) * P], comb_t[:, i, cols], start=(i == 0),
                                   stop=(i == KC - 1))
                mm.then_inc(m_made, 1)
            for g in range(G):
                for k in range(KC):
                    pe.wait_ge(sq_out, G * k + g + 1)
                    mm = pe.matmul(ps[:, 4 + g, :], ones[:], sq_of(G * k + g), start=(k == 0), stop=(k == KC - 1))
                mm.then_inc(ss_made, 1)
            pe.wait_ge(h_out, NT)
            for g in range(G):
                for k in range(KC):
                    mm = pe.matmul(ps[:, g, :], fd[:, k, :], h_t[:, k, g * BANK:(g + 1) * BANK], start=(k == 0),
                                   stop=(k == KC - 1))
                mm.then_inc(fd_made, 1)
            pe.wait_ge(ff_out, G)
            for b in range(B):
                if b >= 4:
                    pe.wait_ge(fin_out, b - 3)
                s = 2 + b % 4
                pe.matmul(ps[:, s, :], ff_t[:, b * L:(b + 1) * L], fu[:], start=True, stop=False)
                for k in range(KC):
                    mm = pe.matmul(ps[:, s, k * P:(k + 1) * P], h_t[:, k, b * L:(b + 1) * L], ident[:], start=False,
                                   stop=(k == KC - 1))
                mm.then_inc(f_made, 1)


def layer(nc, a, out):
    q_scratch = nc.dram_tensor("q_scratch", (B, 2, KC, P, L), F32, kind="Internal").ap()
    k_scratch = nc.dram_tensor("k_scratch", (2, KC, P, SKV), F32, kind="Internal").ap()
    a_scratch = nc.dram_tensor("a_scratch", (B, P, KC, L), F32, kind="Internal").ap()
    queries(nc, a["x"], a["wq"], a["bq"], a["ident"], q_scratch)
    attention(nc, a["ctx"], a["wk"], a["wv"], a["bk"], a["bv"], a["ident"], q_scratch, k_scratch, a_scratch)
    with ExitStack() as ctx:
        st = Stage(nc, ctx, "l")
        xres = st.sb("xres", [P, B, D])
        u = st.sb("u", [P, DT, T])
        with nc.sbuf_tensor("l_gate", [P, DT, T], F32) as gate, nc.sbuf_tensor("l_xd", [P, T], F32) as xd:
            mixer_in(nc, a_scratch, a["x"], a["wo"], a["bo"], a["w_in"], a["b_in"], a["w_conv"], a["b_conv"],
                     a["w_x"], a["ident"], xres, u, gate, xd)
            mixer_scan(nc, a["w_dt"], a["a_log"], a["d_skip"], a["ident"], u, gate, xd)
        experts(nc, a, a["ident"], a["iota"], xres, u, out)


def by_rows(w):
    import numpy as np
    return np.ascontiguousarray(np.asarray(w).reshape(-1, P, w.shape[-1]).transpose(1, 0, 2))


def by_channel(v):
    import numpy as np
    return np.ascontiguousarray(np.asarray(v).reshape(-1, P).T)


def layout(i):
    import numpy as np
    i = {n: np.asarray(v) for n, v in i.items()}
    x, f = "L0_xattn_", "L0_ffn_"
    m = {n: i["L0_attn_" + n] for n in ("w_in", "b_in", "w_conv", "b_conv", "w_x", "w_dt", "A_log", "D", "w_out")}
    return {
        "x": i["x"],
        "ctx": i["ctx_1024"].reshape(B, CH, BANK, KC, P).transpose(0, 1, 4, 3, 2),
        "wq": by_rows(i[x + "Wq"].T), "bq": by_channel(i[x + "bq"]),
        "wk": by_rows(i[x + "Wk"].T), "bk": by_channel(i[x + "bk"]),
        "wv": by_rows(i[x + "Wv"].T), "bv": i[x + "bv"],
        "wo": by_rows(i[x + "Wo"].T), "bo": i[x + "bo"],
        "ident": np.eye(P, dtype=np.float32), "iota": np.arange(E, dtype=np.float32),
        "w_in": by_rows(m["w_in"]), "b_in": by_channel(m["b_in"]),
        "w_conv": by_rows(m["w_conv"].T), "b_conv": by_channel(m["b_conv"]),
        "w_x": by_rows(m["w_x"]), "w_dt": m["w_dt"], "a_log": by_rows(m["A_log"]), "d_skip": by_channel(m["D"]),
        "w_out": by_rows(m["w_out"]),
        "dw": by_rows(i[f + "dw_kernel"].reshape(D, K3)), "dwb": by_channel(i[f + "dw_bias"]),
        "pw": by_rows(i[f + "pw_w"].T), "pwb": by_channel(i[f + "pw_b"]),
        "rw": by_rows(i[f + "router_w"].T), "rb": i[f + "router_b"],
        "ew": i[f + "expert_w"].transpose(0, 2, 1).reshape(E, KC, P, D).transpose(0, 2, 1, 3),
        "eb": i[f + "expert_b"], "ow": by_rows(i[f + "out_w"].T), "owb": by_channel(i[f + "out_b"]),
        "nw": by_channel(i[f + "norm_w"]), "fd": by_rows(i[f + "ff_down_w"].T), "fdb": by_channel(i[f + "ff_down_b"]),
        "fu": i[f + "ff_up_w"].T, "fub": i[f + "ff_up_b"],
    }


def kernel(**inputs):
    import numpy as np
    import concourse.bacc as bacc
    from concourse.bass_utils import run_bass_kernel_spmd

    nc = bacc.Bacc("TRN2", target_bir_lowering=False, num_devices=1)
    arrays = {f"in_{n}": np.ascontiguousarray(a) for n, a in layout(inputs).items()}
    drams = {n[3:]: nc.dram_tensor(n, a.shape, F32, kind="ExternalInput").ap() for n, a in arrays.items()}
    out = nc.dram_tensor("out", (B, L, D), F32, kind="ExternalOutput").ap()
    layer(nc, drams, out)
    got = run_bass_kernel_spmd(nc, [arrays], core_ids=[0])
    return got.results[0]["out"]
```

```python
from contextlib import ExitStack

import concourse.bass as bass
from concourse import mybir

F32 = mybir.dt.float32
F32R = mybir.dt.float32r
U32 = mybir.dt.uint32
ALU = mybir.AluOpType
ACT = mybir.ActivationFunctionType
AX = mybir.AxisListType

P = 128
BANK = 512
B, L, D = 8, 128, 512
KC = D // P
T = B * L
SKV = 2048
H, DH = 16, 32
HG = P // DH
CH = SKV // BANK
KV = BANK // P
EPS = 1e-5
RING = 4


class Stage:

    def __init__(self, nc, ctx, prefix):
        self.nc, self.ctx, self.prefix = nc, ctx, prefix

    def sb(self, name, shape, dt=F32):
        return self.ctx.enter_context(self.nc.sbuf_tensor(f"{self.prefix}_{name}", shape, dt))

    def ps(self, name, shape):
        return self.ctx.enter_context(self.nc.psum_tensor(f"{self.prefix}_{name}", shape, F32))

    def sems(self, *names):
        return [self.ctx.enter_context(self.nc.semaphore(f"{self.prefix}_{n}")) for n in names]


def layer_norm_steps(eng, x, out, stats, mv, rstd, root_ready, var_ready, chain, done, b, base):
    eng.bn_stats(stats, x).then_inc(chain, 1)
    eng.wait_ge(chain, base + 1)
    eng.bn_aggr(mv, stats).then_inc(chain, 1)
    eng.wait_ge(chain, base + 2)
    eng.tensor_scalar(rstd, mv[:, 1:2], EPS, None, ALU.add).then_inc(var_ready, 1)
    eng.wait_ge(root_ready, b + 1)
    eng.reciprocal(rstd, rstd).then_inc(chain, 1)
    eng.wait_ge(chain, base + 3)
    eng.tensor_scalar(out, x, mv[:, 0:1], rstd, ALU.subtract, ALU.mult).then_inc(done, 1)


def queries(nc, x, wq_t, bq, ident_dram, to_split, q_scratch):
    with ExitStack() as ctx:
        st = Stage(nc, ctx, "q")
        xt = st.sb("x", [P, B, D])
        xn = st.sb("xn", [P, 2, D])
        xn_t = st.sb("xnT", [P, KC, T])
        w = st.sb("wq", [P, KC, D])
        bias = st.sb("bq", [P, KC])
        q_t = st.sb("qT", [P, B, KC, L])
        q_hi, q_lo = st.sb("q_hi", [P, B, KC, L], F32R), st.sb("q_lo", [P, B, KC, L], F32R)
        whole = st.sb("whole", [P, len(to_split), KC, BANK])
        ident = st.sb("ident", [P, P])
        stats = st.sb("stats", [P, B, 6])
        mv = st.sb("mv", [P, B, 2])
        rstd = st.sb("rstd", [P, B])
        tp = st.ps("tp", [P, 2, BANK])
        qp = st.ps("qp", [P, 4, BANK])
        w_in, chain, var_ready, root_ready, normed, turned, copied, q_made, q_out, hi_out, lo_out, stored = st.sems(
            "w_in", "chain", "var_ready", "root_ready", "normed", "turned", "copied", "q_made",
            "q_out", "hi_out", "lo_out", "stored")
        x_in = st.sems("x_in0", "x_in1")
        ident_in, = st.sems("ident_in")
        whole_in = st.sems(*[f"whole_in{n}" for n in range(len(to_split))])
        split_hi, split_lo = st.sems("split_hi", "split_lo")
        block = ctx.enter_context(nc.Block())
        tile_of = lambda n: (slice(4 * (n // KC), 4 * (n // KC) + 4), n % KC)

        @block.sync
        def _(sp):
            def load_whole(n):
                sp.dma_start(whole[:, n], to_split[n][0]).then_inc(whole_in[n], 16)

            for half in range(2):
                bs = slice(B // 2 * half, B // 2 * (half + 1))
                sp.dma_start(xt[:, bs], x[bs].rearrange("b l d -> l b d")).then_inc(x_in[half], 16)
                if half == 0:
                    sp.dma_start(ident[:], ident_dram).then_inc(ident_in, 16)
            sp.dma_start(w[:], wq_t).then_inc(w_in, 16)
            sp.dma_start(bias[:], bq).then_inc(w_in, 16)
            for n in range(len(to_split)):
                load_whole(n)
            for half in range(2):
                for m in range(KC):
                    bs = slice(B // 2 * half, B // 2 * (half + 1))
                    for part, (src, out) in enumerate(((q_hi, hi_out), (q_lo, lo_out))):
                        sp.wait_ge(out, KC * half + m + 1)
                        sp.dma_start(q_scratch[bs, part, m].rearrange("b p l -> p b l"),
                                     src[:, bs, m, :].bitcast(F32)).then_inc(stored, 16)
            sp.wait_ge(stored, 64 * KC)

        @block.scalar
        def _(act):
            def split(n):
                act.wait_ge(whole_in[n], 16)
                nc.scalar.copy(to_split[n][1], whole[:, n]).then_inc(split_hi, 1)

            for b in range(B):
                act.wait_ge(var_ready, b + 1)
                nc.scalar.activation(rstd[:, b:b + 1], rstd[:, b:b + 1], ACT.Sqrt).then_inc(root_ready, 1)
                if b >= 4:
                    split(b - 4)
            for n in range(2 * KC):
                bs, m = tile_of(n)
                act.wait_ge(q_out, n + 1)
                nc.scalar.copy(q_hi[:, bs, m, :], q_t[:, bs, m, :]).then_inc(hi_out, 1)

        @block.gpsimd
        def _(pool):
            for n, (_, hi, lo) in enumerate(to_split):
                pool.wait_ge(split_hi, n + 1)
                nc.gpsimd.tensor_tensor(lo, whole[:, n], hi.bitcast(F32), ALU.subtract).then_inc(split_lo, 1)

        @block.vector
        def _(dve):
            def finish_norm(b):
                dve.wait_ge(turned, b + 1)
                dve.tensor_copy(xn_t[:, :, b * L:(b + 1) * L],
                                tp[:, b % 2, :].rearrange("p (k l) -> p k l", k=KC)).then_inc(copied, 1)

            def empty(n):
                bs, m = tile_of(n)
                dve.wait_ge(q_made, n + 1)
                dve.tensor_scalar(q_t[:, bs, m, :], qp[:, n % 4, :].rearrange("p (b l) -> p b l", l=L),
                                  bias[:, m:m + 1], float(DH) ** -0.5, ALU.add, ALU.mult).then_inc(q_out, 1)

            def rest(n):
                bs, m = tile_of(n)
                dve.wait_ge(hi_out, n + 1)
                dve.tensor_tensor(q_lo[:, bs, m, :], q_t[:, bs, m, :], q_hi[:, bs, m, :].bitcast(F32),
                                  ALU.subtract).then_inc(lo_out, 1)

            for b in range(B):
                if b % (B // 2) == 0:
                    dve.wait_ge(x_in[b // (B // 2)], 16)
                if b >= 2:
                    dve.wait_ge(turned, b - 1)
                layer_norm_steps(dve, xt[:, b, :], xn[:, b % 2, :], stats[:, b, :], mv[:, b, :],
                                 rstd[:, b:b + 1], root_ready, var_ready, chain, normed, b, 3 * b)
                if b >= 1:
                    finish_norm(b - 1)
            finish_norm(B - 1)
            dve.wait_ge(w_in, 32)
            for n in range(2 * KC):
                empty(n)
                if n >= 1:
                    rest(n - 1)
            rest(2 * KC - 1)

        @block.tensor
        def _(pe):
            pe.wait_ge(ident_in, 16)

            def project(n):
                g, m = n // KC, n % KC
                if n >= 4:
                    pe.wait_ge(q_out, n - 3)
                for k in range(KC):
                    mm = pe.matmul(qp[:, n % 4, :], w[:, k, m * P:(m + 1) * P], xn_t[:, k, g * BANK:(g + 1) * BANK],
                                   start=(k == 0), stop=(k == KC - 1))
                mm.then_inc(q_made, 1)

            for b in range(B):
                pe.wait_ge(normed, b + 1)
                if b >= 2:
                    pe.wait_ge(copied, b - 1)
                for k in range(KC):
                    mm = pe.transpose(tp[:, b % 2, k * L:(k + 1) * L], xn[:, b % 2, k * P:(k + 1) * P], ident[:])
                mm.then_inc(turned, 1)
                if b >= B // 2:
                    if b == B // 2:
                        pe.wait_ge(copied, B // 2)
                        pe.wait_ge(w_in, 32)
                    project(b - B // 2)
            pe.wait_ge(copied, B)
            for n in range(KC, 2 * KC):
                project(n)


def attention(nc, ctx_t, wk, wv, c_hi, c_lo, bk, bv, ident_dram, q_scratch, k_scratch, a_scratch):
    S_RING, T_RING, PT_RING = 5, 2, 4
    with ExitStack() as ctx:
        st = Stage(nc, ctx, "a")
        (wk_hi, wk_lo), (wv_hi, wv_lo) = wk, wv
        raw = st.sb("raw", [P, KC, BANK])
        k_hi, k_lo = st.sb("k_hi", [P, 2, KC, BANK], F32R), st.sb("k_lo", [P, 2, KC, BANK], F32R)
        v = st.sb("v", [P, SKV // P, D])
        stack = st.sb("stack", [P, RING, SKV], F32R)
        q_stack = st.sb("q_stack", [P, H, L], F32R)
        probs = st.sb("probs", [P, 2, SKV])
        pt = st.sb("pt", [P, PT_RING, KV, L])
        out_t = st.sb("out_t", [P, KC, L])
        ident = st.sb("ident", [P, P])
        bias_k = st.sb("bias_k", [P, KC])
        bias_v = st.sb("bias_v", [P, D])
        mx = st.sb("mx", [P, 2, CH])
        neg_max = st.sb("neg_max", [P, 2])
        sums = st.sb("sums", [P, H, CH])
        total = st.sb("total", [P, HG])
        inv = st.sb("inv", [P, HG])
        inv_wide = st.sb("inv_wide", [P, HG, DH])
        inv_t = st.sb("inv_t", [P, L])
        s_ps = st.ps("s", [P, S_RING, BANK])
        t_ps = st.ps("t", [P, T_RING, BANK])
        o_ps = st.ps("o", [P, BANK])
        (small_in, raw_in, split_hi, split_lo, projected, khi_out, klo_out, v_out, q_in, zeroed, scored, maxed,
         negated, exped, turned, pt_act, pt_dve, inv_chain, inv_ready, inv_turned, inv_out, out_ready, a_stored, first_out, first_in,
         q_rest_in) = st.sems(
            "small_in", "raw_in", "split_hi", "split_lo", "projected", "khi_out", "klo_out", "v_out", "q_in",
            "zeroed", "scored", "maxed", "negated", "exped", "turned", "pt_act", "pt_dve", "inv_chain", "inv_ready",
            "inv_turned", "inv_out", "out_ready", "a_stored", "first_out", "first_in",
            "q_rest_in")
        k_stored = st.sems("k_stored0", "k_stored1")
        stack_in = st.sems(*[f"stack_in{s}" for s in range(RING)])
        block = ctx.enter_context(nc.Block())
        AHEAD = 2
        bank_of = lambda h, i: (CH * h + i) % S_RING
        tile_bank = lambda j: bank_of(H, j)
        v_tile = lambda c, j: t_ps[:, j % T_RING, :] if c == CH - 1 else s_ps[:, tile_bank(j), :]
        t_of, pt_of = lambda h, i: (CH * h + i) % T_RING, lambda h, i: (CH * h + i) % PT_RING
        act_copies = lambda h: (0, 1) if h % 2 == 0 else (0, 1, 2)
        PAIR_ACT, PAIR_DVE = 5, 3
        quarter = lambda r: slice(DH * r, DH * r + DH)

        @block.sync
        def _(sp):
            sp.dma_start(ident[:], ident_dram).then_inc(small_in, 16)
            sp.dma_start(bias_k[:], bk).then_inc(small_in, 16)
            sp.dma_start(bias_v[:], bv.partition_broadcast(P)).then_inc(small_in, 16)

            def load_stack(h):
                for r, part in enumerate((0, 0, 1)):
                    sp.dma_start(stack[quarter(r), h % RING, :].bitcast(F32),
                                 k_scratch[part, h // HG, quarter(h % HG), :]).then_inc(stack_in[h % RING], 16)

            def load_queries(b, ms, sem):
                for r, part in enumerate((0, 1, 0)):
                    sp.dma_start(q_stack[quarter(r), HG * ms.start:HG * ms.stop, :].bitcast(F32),
                                 q_scratch[b, part, ms].rearrange("m (p d) l -> d (m p) l", d=DH)).then_inc(sem, 16)

            def project(b, first=False, final=False):
                if not first:
                    sp.wait_ge(scored, CH * H * b)
                load_queries(b, slice(0, 1), q_in)
                for c in range(CH):
                    if not (final and c >= CH - AHEAD):
                        if not (first and c == 0):
                            sp.wait_ge(split_lo, CH * b + c)
                        src = ctx_t[b, c + AHEAD] if c + AHEAD < CH else ctx_t[b + 1, c + AHEAD - CH]
                        sp.dma_start(raw[:], src).then_inc(raw_in, 16)
                    cols = slice(c * BANK, (c + 1) * BANK)
                    sp.wait_ge(khi_out, CH * KC * b + KC * c + 1)
                    sp.wait_ge(klo_out, CH * KC * b + KC * c + 1)
                    for part, src in enumerate((k_hi, k_lo)):
                        sp.dma_start(k_scratch[part, 0, :, cols], src[:, c % 2, 0].bitcast(F32)).then_inc(first_out, 16)
                    sp.wait_ge(first_out, 128 * b + 32 * c + 32)
                    for r, part in enumerate((0, 0, 1)):
                        sp.dma_start(stack[quarter(r), :, cols].bitcast(F32),
                                     k_scratch[part, 0, :, cols].rearrange("(p d) n -> d p n", d=DH))\
                          .then_inc(first_in, 16)
                    sp.wait_ge(khi_out, CH * KC * b + KC * c + KC)
                    sp.wait_ge(klo_out, CH * KC * b + KC * c + KC)
                    for part, src in enumerate((k_hi, k_lo)):
                        sp.dma_start(k_scratch[part, 1:, :, cols].rearrange("m p n -> p m n"),
                                     src[:, c % 2, 1:].bitcast(F32)).then_inc(k_stored[c % 2], 16)

            def heads(b):
                for s in range(2):
                    sp.wait_ge(k_stored[s], 64 * b + 64)
                load_queries(b, slice(1, KC), q_rest_in)
                for h in range(RING, H):
                    sp.wait_ge(scored, CH * H * b + CH * (h - RING + 1))
                    load_stack(h)
                sp.wait_ge(out_ready, KC * b + KC)
                sp.dma_start(a_scratch[b], out_t[:]).then_inc(a_stored, 16)

            project(0, first=True)
            with sp.Fori(0, B - 2) as b:
                heads(b)
                project(b + 1)
            heads(B - 2)
            project(B - 1, final=True)
            heads(B - 1)
            sp.wait_ge(a_stored, 16 * B)

        @block.gpsimd
        def _(pool):
            def split(b, c):
                pool.wait_ge(split_hi, CH * b + c + 1)
                nc.gpsimd.tensor_tensor(c_lo[:, c % 2], raw[:], c_hi[:, c % 2].bitcast(F32),
                                        ALU.subtract).then_inc(split_lo, 1)

            with pool.Fori(0, B - 1) as b:
                for c in range(CH):
                    split(b, c)
            for c in range(CH - AHEAD):
                split(B - 1, c)

        @block.scalar
        def _(act):
            act.wait_ge(small_in, 48)

            def round_k(b, c, m, started=True):
                if m == 0 and (started or c >= 2):
                    act.wait_ge(k_stored[c % 2], 64 * b + 32 * (c // 2))
                act.wait_ge(projected, 32 * b + 8 * c + m + 1)
                nc.scalar.activation(k_hi[:, c % 2, m, :], s_ps[:, tile_bank(m), :], ACT.Identity,
                                     bias=bias_k[:, m:m + 1]).then_inc(khi_out, 1)

            def project(b, final, started):
                for c in range(CH):
                    if not (started and c == 0):
                        for m in range(KC):
                            round_k(b, c, m, started)
                    if c < (CH - AHEAD if final else CH - 1):
                        split_ahead(b, c)

            def split_ahead(b, c):
                act.wait_ge(projected, 32 * b + 8 * c + 8)
                act.wait_ge(raw_in, 16 * (CH * b + c) + 16)
                nc.scalar.copy(c_hi[:, c % 2], raw[:]).then_inc(split_hi, 1)

            def empty_pt(b, h, i):
                act.wait_ge(turned, CH * H * b + CH * h + i + 1)
                nc.scalar.copy(pt[:, pt_of(h, i)], t_ps[:, t_of(h, i), :].rearrange("p (j l) -> p j l", j=KV))\
                   .then_inc(pt_act, 1)

            def exponentials(b, h, i):
                if i == 0:
                    act.wait_ge(negated, H * b + h + 1)
                nc.scalar.activation(probs[:, h % 2, i * BANK:(i + 1) * BANK], s_ps[:, bank_of(h, i), :], ACT.Exp,
                                     bias=neg_max[:, h % 2:h % 2 + 1],
                                     accum_out=sums[:, h, i:i + 1]).then_inc(exped, 1)

            def heads(b, more):
                for h in range(H):
                    for i in range(CH - 1):
                        exponentials(b, h, i)
                    if h == H - 1 and more:
                        exponentials(b, h, CH - 1)
                        split_ahead(b, CH - 1)
                        round_k(b + 1, 0, 0)
                        round_k(b + 1, 0, 1)
                        empty_pt(b, h, 0)
                        round_k(b + 1, 0, 2)
                        empty_pt(b, h, 1)
                        round_k(b + 1, 0, 3)
                        empty_pt(b, h, 2)
                    else:
                        empty_pt(b, h, 0)
                        exponentials(b, h, CH - 1)
                        for i in act_copies(h)[1:]:
                            empty_pt(b, h, i)

            project(0, False, False)
            with act.Fori(0, B - 2) as b:
                heads(b, True)
                project(b + 1, False, True)
            heads(B - 2, True)
            project(B - 1, True, True)
            heads(B - 1, False)

        @block.vector
        def _(dve):
            dve.memset(stack[quarter(3), :, :].bitcast(F32), 0.0).then_inc(zeroed, 1)
            dve.memset(q_stack[quarter(3), :, :].bitcast(F32), 0.0).then_inc(zeroed, 1)
            dve.wait_ge(small_in, 48)

            def rest_of_k(b, c, m):
                dve.wait_ge(khi_out, CH * KC * b + KC * c + m + 1)
                dve.scalar_tensor_tensor(out=k_lo[:, c % 2, m, :], in0=s_ps[:, tile_bank(m), :], scalar=bias_k[:, m:m + 1],
                                         in1=k_hi[:, c % 2, m, :].bitcast(F32), op0=ALU.add,
                                         op1=ALU.subtract).then_inc(klo_out, 1)

            def maxima(b, h, i):
                dve.wait_ge(scored, CH * H * b + CH * h + i + 1)
                dve.tensor_reduce(mx[:, h % 2, i:i + 1], s_ps[:, bank_of(h, i), :], AX.X, ALU.max).then_inc(maxed, 1)

            def negate_max(b, h):
                dve.wait_ge(maxed, CH * H * b + CH * h + CH)
                dve.tensor_reduce(neg_max[:, h % 2:h % 2 + 1], mx[:, h % 2, :], AX.X, ALU.max,
                                  negate=True).then_inc(negated, 1)

            def project(b, started):
                for c in range(CH):
                    if not (started and c == 0):
                        for m in range(KC):
                            rest_of_k(b, c, m)
                    if started and c == 1:
                        dve.wait_ge(a_stored, 16 * b)
                    for j in range(KV):
                        if c == CH - 1 and j >= 2:
                            maxima(b, 0, 2 * j - 4)
                            maxima(b, 0, 2 * j - 3)
                        dve.wait_ge(projected, 32 * b + 8 * c + KC + j + 1)
                        dve.tensor_tensor(v[:, KV * c + j, :], v_tile(c, j), bias_v[:], ALU.add).then_inc(v_out, 1)
                negate_max(b, 0)

            def widen_inverse(b, g):
                dve.wait_ge(exped, 64 * b + 16 * g + 16)
                dve.tensor_reduce(total[:], sums[:, HG * g:HG * g + HG, :], AX.X, ALU.add).then_inc(inv_chain, 1)
                dve.wait_ge(inv_chain, 2 * KC * b + 2 * g + 1)
                dve.reciprocal(inv[:], total[:]).then_inc(inv_chain, 1)
                dve.wait_ge(inv_chain, 2 * KC * b + 2 * g + 2)
                dve.tensor_copy(inv_wide[:], inv[:].unsqueeze(2).to_broadcast([P, HG, DH])).then_inc(inv_ready, 1)

            def empty_pt(b, h, i):
                dve.wait_ge(turned, CH * H * b + CH * h + i + 1)
                dve.tensor_copy(pt[:, pt_of(h, i)], t_ps[:, t_of(h, i), :].rearrange("p (j l) -> p j l", j=KV))\
                   .then_inc(pt_dve, 1)

            def finish_group(b, g):
                dve.wait_ge(inv_turned, KC * b + g + 1)
                dve.tensor_copy(inv_t[:], o_ps[:, L:2 * L]).then_inc(inv_out, 1)
                dve.wait_ge(inv_out, KC * b + g + 1)
                dve.tensor_tensor(out_t[:, g, :], o_ps[:, :L], inv_t[:], ALU.mult).then_inc(out_ready, 1)

            def heads(b, more):
                for h in range(1, H):
                    for i in range(CH):
                        if h >= 2:
                            if i == 0 and h % 2 == 0:
                                empty_pt(b, h - 2, 2)
                            if i == 1:
                                empty_pt(b, h - 2, 3)
                                if h > HG and h % HG == 1:
                                    widen_inverse(b, h // HG - 1)
                        maxima(b, h, i)
                    negate_max(b, h)
                    if h > HG and h % HG == 1:
                        finish_group(b, h // HG - 1)
                empty_pt(b, H - 2, 2)
                if more:
                    rest_of_k(b + 1, 0, 0)
                empty_pt(b, H - 2, 3)
                if more:
                    for m in range(1, KC):
                        rest_of_k(b + 1, 0, m)
                empty_pt(b, H - 1, 3)
                widen_inverse(b, KC - 1)
                finish_group(b, KC - 1)

            project(0, False)
            with dve.Fori(0, B - 1) as b:
                heads(b, True)
                project(b + 1, True)
            heads(B - 1, False)

        @block.tensor
        def _(pe):
            def three(out, w_hi, w_lo, x_hi, x_lo, first, final):
                pe.matmul(out, w_hi, x_hi, start=first, stop=False)
                pe.matmul(out, w_lo, x_hi, start=False, stop=False)
                return pe.matmul(out, w_hi, x_lo, start=False, stop=final)

            def project_k(b, c, m, started):
                if m == 0 and (started or c >= AHEAD):
                    pe.wait_ge(split_lo, CH * b + c - AHEAD + 1)
                if c >= 1:
                    pe.wait_ge(v_out, 16 * b + 4 * (c - 1) + m + 1)
                part = slice(m * P, (m + 1) * P)
                for k in range(KC):
                    mm = three(s_ps[:, tile_bank(m), :], wk_hi[:, k, part], wk_lo[:, k, part], c_hi[:, c % 2, k, :],
                               c_lo[:, c % 2, k, :], k == 0, k == KC - 1)
                mm.then_inc(projected, 1)

            def project_v(b, c, j):
                if c < CH - 1:
                    pe.wait_ge(klo_out, 16 * b + 4 * c + j + 1)
                elif j >= T_RING:
                    pe.wait_ge(v_out, 16 * b + 4 * c + j - T_RING + 1)
                part = slice(j * P, (j + 1) * P)
                for k in range(KC):
                    mm = three(v_tile(c, j), c_hi[:, c % 2, k, part], c_lo[:, c % 2, k, part], wv_hi[:, k, :],
                               wv_lo[:, k, :], k == 0, k == KC - 1)
                mm.then_inc(projected, 1)

            def project(b, started):
                for c in range(CH):
                    if not (started and c == 0):
                        for m in range(KC):
                            project_k(b, c, m, started)
                    for j in range(KV):
                        if c == CH - 1 and j == 2:
                            for i in range(CH):
                                scores(b, 0, i)
                        project_v(b, c, j)
                        if started and c == 0 and j < 2:
                            last_values(b - 1, j)

            def scores(b, h, i):
                bank, item = bank_of(h, i), CH * h + i
                if i == 0:
                    if h < RING:
                        pe.wait_ge(first_in, 192 * b + 192)
                    else:
                        pe.wait_ge(stack_in[h % RING], (H // RING - 1) * 48 * b + 48 * (h // RING))
                        if h == HG:
                            pe.wait_ge(q_rest_in, 48 * b + 48)
                    if h == 0:
                        pe.wait_ge(small_in, 48)
                        pe.wait_ge(zeroed, 2)
                        pe.wait_ge(q_in, 48 * b + 48)
                if item >= S_RING:
                    pe.wait_ge(exped, 64 * b + item - S_RING + 1)
                elif bank in [tile_bank(j) for j in range(KV)]:
                    j = [tile_bank(j) for j in range(KV)].index(bank)
                    pe.wait_ge(klo_out, 16 * b + 12 + j + 1)
                pe.matmul(s_ps[:, bank, :], q_stack[:, h, :], stack[:, h % RING, i * BANK:(i + 1) * BANK], start=True,
                          stop=True).then_inc(scored, 1)

            def pt_ready(b, h, i):
                if i in act_copies(h):
                    pe.wait_ge(pt_act, PAIR_ACT * (H // 2 * b + h // 2) + len(act_copies(0)) * (h % 2) + i + 1)
                else:
                    place = i - 1 if h % 2 == 0 else PAIR_DVE
                    pe.wait_ge(pt_dve, PAIR_DVE * (H // 2 * b + h // 2) + place)

            def turn(b, h, i):
                pe.wait_ge(exped, 64 * b + 4 * h + i + 1)
                n = CH * h + i
                if n < T_RING:
                    pe.wait_ge(v_out, 16 * b + 14 + n + 1)
                else:
                    pt_ready(b, (n - T_RING) // CH, (n - T_RING) % CH)
                for j in range(KV):
                    col = i * BANK + j * P
                    mm = pe.transpose(t_ps[:, t_of(h, i), j * L:(j + 1) * L], probs[:, h % 2, col:col + P], ident[:])
                mm.then_inc(turned, 1)

            def weigh(b, h, i):
                p = h % HG
                pt_ready(b, h, i)
                if i == 0 and h >= HG and p == 0:
                    pe.wait_ge(out_ready, KC * b + h // HG)
                for j in range(KV):
                    mm = pe.matmul(o_ps[DH * p:DH * p + DH, :L], v[:, KV * i + j, DH * h:DH * h + DH],
                                   pt[:, pt_of(h, i), j, :], start=(i == 0 and j == 0),
                                   stop=(i == CH - 1 and j == KV - 1), tile_position=(0, DH * p))
                if i == CH - 1 and p == HG - 1:
                    pe.wait_ge(inv_ready, KC * b + h // HG + 1)
                    pe.transpose(o_ps[:, L:2 * L], inv_wide[:].rearrange("p h d -> p (h d)"), ident[:])\
                      .then_inc(inv_turned, 1)

            def last_values(b, half):
                if half == 0:
                    turn(b, H - 1, 3)
                    weigh(b, H - 1, 0)
                    weigh(b, H - 1, 1)
                else:
                    weigh(b, H - 1, 2)
                    weigh(b, H - 1, 3)

            def heads(b, more):
                for h in range(H):
                    def ahead(i):
                        if h + 1 < H:
                            scores(b, h + 1, i)
                        elif more:
                            pe.wait_ge(exped, 64 * b + CH * H + i - S_RING + 1)
                            project_k(b + 1, 0, i, True)
                    ahead(0)
                    if h >= 1:
                        turn(b, h - 1, 3)
                    for i in range(CH - 1):
                        ahead(i + 1)
                        if h >= 1:
                            weigh(b, h - 1, i)
                        turn(b, h, i)
                    if h >= 1:
                        weigh(b, h - 1, 3)

            project(0, False)
            with pe.Fori(0, B - 1) as b:
                heads(b, True)
                project(b + 1, True)
            heads(B - 1, False)
            for half in range(2):
                last_values(B - 1, half)


DIN = 2 * D
DT = DIN // P
N, DTR, TW = 16, 64, 4
XD = DTR + 2 * N
G, BG = 2, B // 2


def mixer_in(nc, a_scratch, x, wo_t, bo, w_in, b_in, w_conv, b_conv, w_x, ident_dram, xres, u, gate, xd):
    with ExitStack() as ctx:
        st = Stage(nc, ctx, "m")
        at = st.sb("at", [P, B, KC, L])
        wo = st.sb("wo", [P, KC, D])
        bo_all = st.sb("bo", [P, D])
        QUARTERS = 2 * DIN // BANK
        wi_raw = st.sb("wi_raw", [P, 2, KC, BANK])
        wi_hi, wi_lo = st.sb("wi_hi", [P, 2, KC, BANK], F32R), st.sb("wi_lo", [P, 2, KC, BANK], F32R)
        bi = st.sb("bi", [P, 2 * DT])
        wc = st.sb("wc", [P, DT, TW])
        bc = st.sb("bc", [P, DT])
        wx = st.sb("wx", [P, DT, XD])
        ident = st.sb("ident", [P, P])
        xn = st.sb("xn", [P, 2, D])
        xn_hi = st.sb("xn_hi", [P, B, KC, L], F32R)
        xn_lo = at[:].bitcast(F32R)
        PADDED = L + TW - 1
        xc = st.sb("xc", [P, 2, B, PADDED])
        acc = st.sb("acc", [P, 2, B, L])
        stats, mv, rstd = st.sb("stats", [P, B, 6]), st.sb("mv", [P, B, 2]), st.sb("rstd", [P, B])
        op = st.ps("op", [P, 2, BANK])
        tp = st.ps("tp", [P, 2, BANK])
        ip = st.ps("ip", [P, 4, BANK])
        (w_in_s, x_in, biased, o_made, added, chain, var_ready, root_ready, normed, turned, copied, i_made,
         i_out, taps, conv_done, u_done, padded, xd_made, xd_out, a_in, xn_rounded, wi_hi_out, wi_lo_out,
         at_late) = st.sems(
            "w_in", "x_in", "biased", "o_made", "added", "chain", "var_ready", "root_ready", "normed", "turned",
            "copied", "i_made", "i_out", "taps", "conv_done", "u_done", "padded", "xd_made", "xd_out",
            "a_in", "xn_rounded", "wi_hi_out", "wi_lo_out",
            "at_late")
        wi_in = st.sems("wi_in0", "wi_in1")
        block = ctx.enter_context(nc.Block())

        @block.sync
        def _(sp):
            sp.dma_start(wo[:], wo_t).then_inc(a_in, 16)
            for half in range(2):
                bs = slice(B // 2 * half, B // 2 * (half + 1))
                sp.dma_start(at[:, bs], a_scratch[bs].rearrange("b p m l -> p b m l"))\
                  .then_inc(at_late if half else a_in, 16)
                if half == 0:
                    sp.dma_start(ident[:], ident_dram).then_inc(a_in, 16)
            sp.dma_start(xres[:], x.rearrange("b l d -> l b d")).then_inc(x_in, 16)
            sp.dma_start(bo_all[:], bo.partition_broadcast(P)).then_inc(x_in, 16)
            for q in range(QUARTERS):
                if q == 2:
                    for dst, src in ((bi, b_in), (wc, w_conv), (bc, b_conv), (wx, w_x)):
                        sp.dma_start(dst[:], src).then_inc(w_in_s, 16)
                if q >= 2:
                    sp.wait_ge(wi_lo_out, q - 1)
                sp.dma_start(wi_raw[:, q % 2], w_in[:, :, q * BANK:(q + 1) * BANK]).then_inc(wi_in[q % 2], 16)

        @block.gpsimd
        def _(pool):
            nc.gpsimd.memset(xc[:, :, :, 0:TW - 1], 0.0).then_inc(padded, 1)
            pool.wait_ge(x_in, 32)
            for b in range(B):
                nc.gpsimd.tensor_tensor(xres[:, b, :], xres[:, b, :], bo_all[:], ALU.add).then_inc(biased, 1)
            for q in range(QUARTERS):
                pool.wait_ge(wi_hi_out, q + 1)
                nc.gpsimd.tensor_tensor(wi_lo[:, q % 2], wi_raw[:, q % 2], wi_hi[:, q % 2].bitcast(F32),
                                        ALU.subtract).then_inc(wi_lo_out, 1)

        @block.scalar
        def _(act):
            def round_w(q):
                act.wait_ge(wi_in[q % 2], 16 * (q // 2) + 16)
                if q >= 2:
                    act.wait_ge(i_made, G * KC * (q - 1))
                nc.scalar.copy(wi_hi[:, q % 2], wi_raw[:, q % 2]).then_inc(wi_hi_out, 1)

            def round_x(b):
                act.wait_ge(turned, b + 1)
                nc.scalar.copy(xn_hi[:, b], tp[:, b % 2, :].rearrange("p (k l) -> p k l", k=KC))\
                   .then_inc(xn_rounded, 1)

            for b in range(B):
                act.wait_ge(var_ready, b + 1)
                nc.scalar.activation(rstd[:, b:b + 1], rstd[:, b:b + 1], ACT.Sqrt).then_inc(root_ready, 1)
                if b >= 1:
                    round_x(b - 1)
                if b in (1, 4):
                    round_w(b // 3)
            round_x(B - 1)
            act.wait_ge(w_in_s, 64)
            act.wait_ge(padded, 1)
            for c in range(2 * DT):
                if c in (KC, 2 * KC):
                    round_w(c // KC + 1)
                for g in range(G):
                    n = G * c + g
                    act.wait_ge(i_made, n + 1)
                    if c < DT:
                        if c >= 2 and g == 0:
                            act.wait_ge(conv_done, c - 1)
                        nc.scalar.activation(xc[:, c % 2, BG * g:BG * g + BG, TW - 1:],
                                             ip[:, n % 4, :].rearrange("p (b l) -> p b l", l=L), ACT.Identity,
                                             bias=bi[:, c:c + 1]).then_inc(i_out, 1)
                    else:
                        nc.scalar.activation(gate[:, c - DT, g * BANK:(g + 1) * BANK], ip[:, n % 4, :], ACT.Silu,
                                             bias=bi[:, c:c + 1]).then_inc(i_out, 1)
                if 1 <= c <= DT:
                    act.wait_ge(conv_done, c)
                    nc.scalar.activation(u[:, c - 1, :], acc[:, (c - 1) % 2].rearrange("p b l -> p (b l)"), ACT.Silu,
                                         bias=bc[:, c - 1:c]).then_inc(u_done, 1)

        @block.vector
        def _(dve):
            def finish_norm(b):
                dve.wait_ge(xn_rounded, b + 1)
                dve.tensor_tensor(xn_lo[:, b], tp[:, b % 2, :].rearrange("p (k l) -> p k l", k=KC),
                                  xn_hi[:, b].bitcast(F32), ALU.subtract).then_inc(copied, 1)

            for b in range(B):
                dve.wait_ge(o_made, b + 1)
                dve.wait_ge(biased, b + 1)
                dve.tensor_tensor(xres[:, b, :], xres[:, b, :], op[:, b % 2, :], ALU.add).then_inc(added, 1)
                dve.wait_ge(added, b + 1)
                if b >= 2:
                    dve.wait_ge(turned, b - 1)
                layer_norm_steps(dve, xres[:, b, :], xn[:, b % 2, :], stats[:, b, :], mv[:, b, :],
                                 rstd[:, b:b + 1], root_ready, var_ready, chain, normed, b, 3 * b)
                if b >= 1:
                    finish_norm(b - 1)
            finish_norm(B - 1)
            dve.wait_ge(w_in_s, 64)
            for c in range(DT):
                dve.wait_ge(i_out, G * c + G)
                if c >= 2:
                    dve.wait_ge(u_done, c - 1)
                s = c % 2
                dve.tensor_scalar(acc[:, s], xc[:, s, :, TW - 1:TW - 1 + L], wc[:, c, TW - 1:TW], None,
                                  ALU.mult).then_inc(taps, 1)
                for k in range(TW - 1):
                    dve.wait_ge(taps, 3 * c + k + 1)
                    dve.scalar_tensor_tensor(out=acc[:, s], in0=xc[:, s, :, k:k + L], scalar=wc[:, c, k:k + 1],
                                             in1=acc[:, s], op0=ALU.mult, op1=ALU.add)\
                       .then_inc(conv_done if k == TW - 2 else taps, 1)
            for g in range(G):
                dve.wait_ge(xd_made, g + 1)
                dve.tensor_copy(xd[0:XD, g * BANK:(g + 1) * BANK], op[0:XD, g, :]).then_inc(xd_out, 1)

        @block.tensor
        def _(pe):
            pe.wait_ge(a_in, 48)

            def turn(b):
                pe.wait_ge(normed, b + 1)
                if b >= 2:
                    pe.wait_ge(copied, b - 1)
                for k in range(KC):
                    mm = pe.transpose(tp[:, b % 2, k * L:(k + 1) * L], xn[:, b % 2, k * P:(k + 1) * P], ident[:])
                mm.then_inc(turned, 1)

            for b in range(B):
                if b == B // 2:
                    pe.wait_ge(at_late, 16)
                if b >= 2:
                    pe.wait_ge(added, b - 1)
                for k in range(KC):
                    mm = pe.matmul(op[:, b % 2, :], at[:, b, k, :], wo[:, k, :], start=(k == 0), stop=(k == KC - 1))
                mm.then_inc(o_made, 1)
                if b >= 1:
                    turn(b - 1)
            turn(B - 1)
            pe.wait_ge(copied, B)

            def x_dbl():
                pe.wait_ge(w_in_s, 64)
                pe.wait_ge(u_done, DT)
                for g in range(G):
                    for c in range(DT):
                        mm = pe.matmul(op[0:XD, g, :], wx[:, c, :], u[:, c, g * BANK:(g + 1) * BANK],
                                       start=(c == 0), stop=(c == DT - 1))
                    mm.then_inc(xd_made, 1)

            for c in range(2 * DT):
                for g in range(G):
                    n = G * c + g
                    if n >= 4:
                        pe.wait_ge(i_out, n - 3)
                    if c % KC == 0 and g == 0:
                        pe.wait_ge(wi_lo_out, c // KC + 1)
                    q, cols = c // KC % 2, slice(c % KC * P, (c % KC + 1) * P)
                    for k in range(KC):
                        w_hi, w_lo = wi_hi[:, q, k, cols], wi_lo[:, q, k, cols]
                        x_hi, x_lo = (x[:, BG * g:BG * g + BG, k, :] for x in (xn_hi, xn_lo))
                        pe.matmul(ip[:, n % 4, :], w_hi, x_hi, start=(k == 0), stop=False)
                        pe.matmul(ip[:, n % 4, :], w_lo, x_hi, start=False, stop=False)
                        mm = pe.matmul(ip[:, n % 4, :], w_hi, x_lo, start=False, stop=(k == KC - 1))
                    mm.then_inc(i_made, 1)
                if c == 2 * DT - 4:
                    x_dbl()


def mixer_scan(nc, w_dt, a_log, d_skip, ident_dram, bc_scratch, u, gate, xd):
    with ExitStack() as ctx:
        st = Stage(nc, ctx, "s")
        RS = 4
        wd = st.sb("wd", [P, DIN])
        a_neg = st.sb("a_neg", [P, DT, N])
        dsk = st.sb("dsk", [P, DT])
        ident = st.sb("ident", [P, P])
        bc = st.sb("bc", [P, 2, N, BANK])
        delta = st.sb("delta", [P, DT, BANK])
        du = st.sb("du", [P, 2, BANK])
        decay = st.sb("decay", [P, RS, BG, L + 1])
        drive = st.sb("drive", [P, RS, BG, L + 1])
        state = st.sb("state", [P, RS, BG, L + 1])
        seen = st.sb("seen", [P, 2, BG, L])
        ps = st.ps("ps", [P, 8, BANK])
        (w_in, bc_out, a_ready, zeroed, d_made, abs_out, exp_out, log_out, delta_out, du_out, decayed, driven,
         scanned, weighed, summed, skipped, y_out) = st.sems(
            "w_in", "bc_out", "a_ready", "zeroed", "d_made", "abs_out", "exp_out", "log_out", "delta_out", "du_out",
            "decayed", "driven", "scanned", "weighed", "summed", "skipped", "y_out")
        row_in = st.sems(*[f"row_in{n}" for n in range(N)])
        block = ctx.enter_context(nc.Block())
        flat = lambda t: t.rearrange("p b l -> p (b l)")
        by_batch = lambda t: t.rearrange("p (b l) -> p b l", l=L)
        UN = 2
        STEPS, GROUP = UN * N, DT * N
        PAIRS = DT // UN

        @block.sync
        def _(sp):
            sp.dma_start(bc_scratch, xd[DTR:XD, :]).then_inc(bc_out, 16)
            for dst, src in ((wd[0:DTR, :], w_dt), (a_neg[:], a_log), (dsk[:], d_skip), (ident[:], ident_dram)):
                sp.dma_start(dst, src).then_inc(w_in, 16)
            sp.wait_ge(bc_out, 16)
            for g in range(G):
                for n in range(N):
                    if g >= 1:
                        sp.wait_ge(weighed, GROUP * g - N + n + 1)
                    rows = bc_scratch.rearrange("(r n) t -> r n t", n=N)[:, n, g * BANK:(g + 1) * BANK]
                    sp.dma_start(bc[:, :, n, :], rows.partition_broadcast(P)).then_inc(row_in[n], 16)

        @block.gpsimd
        def _(pool):
            nc.gpsimd.memset(decay[:], 0.0).then_inc(zeroed, 1)
            nc.gpsimd.memset(drive[:], 0.0).then_inc(zeroed, 1)
            pool.wait_ge(zeroed, 2)

            def step(g, pair, s):
                n = s % N
                if n == 0:
                    pool.wait_ge(du_out, DT * g + UN * pair + s // N + 1)
                if s < N:
                    pool.wait_ge(row_in[n], 16 * g + 16)
                pool.wait_ge(scanned, GROUP * g + STEPS * pair + s + 1)
                nc.gpsimd.tensor_tensor(drive[:, s % RS, :, 1:], by_batch(du[:, s // N]), by_batch(bc[:, 0, n, :]),
                                        ALU.mult).then_inc(driven, 1)

            for g in range(G):
                with pool.Fori(0, PAIRS) as pair:
                    for s in range(STEPS):
                        step(g, pair, s)

        @block.scalar
        def _(act):
            act.wait_ge(w_in, 64)
            nc.scalar.activation(a_neg[:], a_neg[:], ACT.Exp).then_inc(a_ready, 1)
            act.wait_ge(zeroed, 2)
            act.wait_ge(a_ready, 2)
            for g in range(G):
                for d in range(DT):
                    act.wait_ge(d_made, DT * g + d + 1)
                    nc.scalar.activation(delta[:, d, :], ps[:, d, :], ACT.Abs).then_inc(abs_out, 1)
                for d in range(DT):
                    act.wait_ge(abs_out, DT * g + d + 1)
                    nc.scalar.activation(delta[:, d, :], delta[:, d, :], ACT.Exp, scale=-1.0).then_inc(exp_out, 1)
                for d in range(DT):
                    act.wait_ge(exp_out, DT * g + d + 1)
                    nc.scalar.activation(delta[:, d, :], delta[:, d, :], ACT.Ln, bias=1.0).then_inc(log_out, 1)
                act.wait_ge(delta_out, DT * g + DT)
                with act.Fori(0, PAIRS) as pair:
                    for s in range(STEPS):
                        n, d = s % N, UN * pair + s // N
                        act.wait_ge(scanned, GROUP * g + STEPS * pair + s + 1)
                        nc.scalar.activation(decay[:, s % RS, :, 1:], by_batch(delta[:, d, :]), ACT.Exp,
                                             scale=a_neg[:, d, n:n + 1]).then_inc(decayed, 1)

        @block.vector
        def _(dve):
            dve.wait_ge(a_ready, 1)
            dve.tensor_scalar(a_neg[:], a_neg[:], -1.0, None, ALU.mult).then_inc(a_ready, 1)
            dve.memset(state[:, 0, :, 0:1], 0.0).then_inc(scanned, RS)
            for g in range(G):
                cols = slice(g * BANK, (g + 1) * BANK)
                for d in range(DT):
                    dve.wait_ge(log_out, DT * g + d + 1)
                    dve.scalar_tensor_tensor(out=delta[:, d, :], in0=ps[:, d, :], scalar=0.0, in1=delta[:, d, :],
                                             op0=ALU.max, op1=ALU.add).then_inc(delta_out, 1)
                dve.wait_ge(delta_out, DT * g + DT)

                def make_du(d, i):
                    dve.tensor_tensor(du[:, i, :], delta[:, d, :], u[:, d, cols], ALU.mult).then_inc(du_out, 1)

                def scan(before, s):
                    dve.wait_ge(decayed, before + s + 1)
                    dve.wait_ge(driven, before + s + 1)
                    if s >= 3:
                        dve.wait_ge(weighed, before + s - 2)
                    dve.tensor_tensor_scan(flat(state[:, s % RS]), flat(decay[:, s % RS]), flat(drive[:, s % RS]),
                                           0.0, ALU.mult, ALU.add).then_inc(scanned, 1)

                def weigh(before, s):
                    if s < N:
                        dve.wait_ge(row_in[s], 16 * g + 16)
                    dve.wait_ge(scanned, before + s + 1 + RS)
                    dve.wait_ge(summed, before + s + 1)
                    dve.tensor_tensor(seen[:, s % 2], state[:, s % RS, :, 1:], by_batch(bc[:, 1, s % N, :]),
                                      ALU.mult).then_inc(weighed, 1)

                def finish(before, d, i):
                    dve.wait_ge(summed, before + N * i + N + 2)
                    dve.scalar_tensor_tensor(out=u[:, d, cols], in0=u[:, d, cols], scalar=dsk[:, bass.ds(d, 1)],
                                             in1=ps[:, i, :], op0=ALU.mult, op1=ALU.add).then_inc(skipped, 1)
                    dve.wait_ge(skipped, DT * g + d + 1)
                    dve.tensor_tensor(u[:, d, cols], u[:, d, cols], gate[:, d, cols], ALU.mult).then_inc(y_out, 1)

                def body(pair, last):
                    before, d = GROUP * g + STEPS * pair, UN * pair
                    for s in range(2, STEPS if last else STEPS + 2):
                        scan(before, s)
                        weigh(before, s - 1)
                        if s == 6:
                            make_du(d + 1, 1)
                        if s == N + 2:
                            finish(before, d, 0)
                        if s == N + 6 and not last:
                            make_du(d + UN, 0)
                    if last:
                        weigh(before, STEPS - 1)
                    finish(before, d + 1, 1)

                make_du(0, 0)
                scan(GROUP * g, 0)
                scan(GROUP * g, 1)
                weigh(GROUP * g, 0)
                with dve.Fori(0, PAIRS - 1) as pair:
                    body(pair, False)
                body(PAIRS - 1, True)

        @block.tensor
        def _(pe):
            pe.wait_ge(w_in, 64)
            pe.transpose(ps[:, 7, :P], ident[:], ident[:]).then_inc(summed, 2)
            for g in range(G):
                cols = slice(g * BANK, (g + 1) * BANK)
                if g >= 1:
                    pe.wait_ge(y_out, DT * g)
                for d in range(DT):
                    pe.matmul(ps[:, d, :], wd[0:DTR, d * P:(d + 1) * P], xd[0:DTR, cols],
                              start=True, stop=True).then_inc(d_made, 1)
                pe.wait_ge(delta_out, DT * (g + 1))
                with pe.Fori(0, PAIRS) as pair:
                    for s in range(STEPS):
                        i, n = s // N, s % N
                        pe.wait_ge(weighed, GROUP * g + STEPS * pair + s + 1)
                        pe.matmul(ps[:, i, :], ident[:], flat(seen[:, s % 2]), start=(n == 0), stop=(n == N - 1))\
                          .then_inc(summed, 1)


E = 8
HID = D // 4
K3 = 3


def experts(nc, w, ident_dram, iota, xres, u, out):
    with ExitStack() as ctx:
        st = Stage(nc, ctx, "e")
        ident = st.sb("ident", [P, P])
        ones = st.sb("ones", [P, P])
        with ExitStack() as early:
            wo, pw = (Stage(nc, early, "e").sb(name, shape) for name, shape in (("w_out", [P, DT, D]),
                                                                               ("pw", [P, KC, D])))
        x1_lo = st.sb("x1_lo", [P, KC, T], F32R)
        x1_hi_low, x1_hi_high = (st.sb(f"x1_hi{half}", [P, KC // 2, T], F32R) for half in range(2))
        x1_hi = lambda k, cols: x1_hi_low[:, k, cols] if k < KC // 2 else x1_hi_high[:, k - KC // 2, cols]
        xn = st.sb("xn", [P, 2, D])
        PADDED = L + K3 - 1
        xf_t = st.sb("xfT", [P, KC, B, PADDED])
        x1_t = st.sb("x1T", [P, KC, T])
        h_t = st.sb("hT", [P, KC, T])
        rms = st.sb("rms", [P, G, BANK])
        ff_t = st.sb("ffT", [P, T])
        ow = st.sb("ow", [P, KC, D])
        dw, dwb, pwb = st.sb("dw", [P, KC, K3]), st.sb("dwb", [P, KC]), st.sb("pwb", [P, KC])
        rw, rb = st.sb("rw", [P, KC, E]), st.sb("rb", [P, E])
        owb, nw, fdb = st.sb("owb", [P, KC]), st.sb("nw", [P, KC]), st.sb("fdb", [P, 1])
        fd, fu = st.sb("fd", [P, KC, HID]), st.sb("fu", [HID, D])
        ew_raw, eb = st.sb("ew_raw", [P, KC, D]), st.sb("eb", [P, 2, D])
        ew_hi, ew_lo = st.sb("ew_hi", [P, 2, KC, D], F32R), st.sb("ew_lo", [P, 2, KC, D], F32R)
        pre, act_e = st.sb("pre", [P, 2, D]), st.sb("act_e", [P, 2, D])
        fub = act_e[:, 0, :]
        stats, mv, rstd = st.sb("stats", [P, B, 6]), st.sb("mv", [P, B, 2]), st.sb("rstd", [P, B])
        logits, top = st.sb("logits", [P, B, E]), st.sb("top", [P, B, E])
        index = st.sb("index", [P, B, E], U32)
        chosen = st.sb("chosen", [P, B, E])
        numbers = st.sb("numbers", [P, E])
        share = st.sb("share", [P, 4, B])
        route, second = st.sb("route", [P, B, E]), st.sb("second", [P, B, E])
        uu = u.rearrange("p c t -> p (c t)")
        conv = uu[:, 0:KC * T].rearrange("p (k t) -> p k t", k=KC)
        comb = uu[:, KC * T:2 * KC * T].rearrange("p (b d) -> p b d", b=B)
        comb_t, hp_t = conv, comb.rearrange("p b d -> p (b d)").rearrange("p (k t) -> p k t", k=KC)
        ps = st.ps("ps", [P, 6, BANK])
        tp = st.ps("tp", [P, 2, BANK])
        ew_in, ew_hi_out, ew_lo_out, x1_hi_out, x1_lo_out = st.sems("ew_in", "ew_hi_out", "ew_lo_out", "x1_hi_out",
                                                                    "x1_lo_out")
        (w_in, eb_in0, eb_in1, made, added, chain, var_ready, root_ready, normed, turned, copied, padded, taps,
         conv_out, silu_out, x1_out, lg_out, dstep, astep, routed, ex_made, pre_out, act_out, comb_out, zeroed,
         m_made, hp_out, sq_out, ss_made, rms_out, h_out, fd_made, ff_out, f_made, fin_out, biased, stored,
         first_in) = st.sems(
            "w_in", "eb_in0", "eb_in1", "made", "added", "chain", "var_ready", "root_ready", "normed", "turned",
            "copied", "padded", "taps", "conv_out", "silu_out", "x1_out", "lg_out", "dstep", "astep", "routed",
            "ex_made", "pre_out", "act_out", "comb_out", "zeroed", "m_made", "hp_out", "sq_out", "ss_made",
            "rms_out", "h_out", "fd_made", "ff_out", "f_made", "fin_out", "biased", "stored",
            "first_in")
        eb_in = [eb_in0, eb_in1]
        block = ctx.enter_context(nc.Block())
        sq_of = lambda n: h_t[:, n % KC, n // KC * BANK:(n // KC + 1) * BANK]
        NT = KC * G
        tile_of = lambda n: (n % KC, slice(n // KC * BANK, (n // KC + 1) * BANK))

        @block.sync
        def _(sp):
            sp.dma_start(wo[:], w["w_out"]).then_inc(first_in, 16)
            sp.dma_start(ident[:], ident_dram).then_inc(first_in, 16)
            sp.dma_start(ew_raw[:], w["ew"][0]).then_inc(ew_in, 16)
            loads = ((dw, w["dw"]), (dwb, w["dwb"]), (pw, w["pw"]),
                     (pwb, w["pwb"]), (rw, w["rw"]), (ow, w["ow"]), (owb, w["owb"]), (nw, w["nw"]), (fd, w["fd"]),
                     (fdb, w["fdb"]), (fu, w["fu"]), (numbers, iota.partition_broadcast(P)),
                     (rb, w["rb"].partition_broadcast(P)), (fub, w["fub"].partition_broadcast(P)))
            assert len(loads) == 14
            for dst, src in loads:
                sp.dma_start(dst[:] if dst is not fub else fub, src).then_inc(w_in, 16)

            def load_bias(e, s):
                sp.dma_start(eb[:, s, :], w["eb"][e].partition_broadcast(P)).then_inc(eb_in[s], 16)

            load_bias(0, 0)
            load_bias(1, 1)
            sp.wait_ge(ew_lo_out, 1)
            sp.dma_start(ew_raw[:], w["ew"][1]).then_inc(ew_in, 16)
            with sp.Fori(0, E // 2 - 1) as pair:
                for s in range(2):
                    sp.wait_ge(ew_lo_out, 2 * pair + s + 2)
                    sp.dma_start(ew_raw[:], w["ew"][2 * pair + 2 + s]).then_inc(ew_in, 16)
                    sp.wait_ge(pre_out, 2 * B * pair + B * s + B)
                    load_bias(2 * pair + 2 + s, s)
            for b in range(B):
                sp.wait_ge(fin_out, b + 1)
                sp.dma_start(out[b], xres[:, b, :]).then_inc(stored, 16)
            sp.wait_ge(stored, 16 * B)

        @block.gpsimd
        def _(pool):
            nc.gpsimd.memset(xf_t[:, :, :, 0:K3 - 1], 0.0).then_inc(padded, 1)
            nc.gpsimd.memset(ones[:], 1.0).then_inc(padded, 1)

            def rest_of_expert(e, s):
                pool.wait_ge(ew_hi_out, e + 1)
                nc.gpsimd.tensor_tensor(ew_lo[:, s], ew_raw[:], ew_hi[:, s].bitcast(F32), ALU.subtract)\
                    .then_inc(ew_lo_out, 1)

            for e in range(2):
                rest_of_expert(e, e)
            pool.wait_ge(w_in, 224)
            pool.wait_ge(normed, B)
            for b in range(B):
                nc.gpsimd.tensor_tensor(xres[:, b, :], xres[:, b, :], fub, ALU.add).then_inc(biased, 1)
            pool.wait_ge(made, B)
            nc.gpsimd.memset(comb[:], 0.0).then_inc(zeroed, 1)
            for n in range(NT):
                k, cols = tile_of(n)
                pool.wait_ge(x1_hi_out, n + 1)
                nc.gpsimd.tensor_tensor(x1_lo[:, k, cols], x1_t[:, k, cols], x1_hi(k, cols).bitcast(F32),
                                        ALU.subtract).then_inc(x1_lo_out, 1)
            with pool.Fori(0, E // 2 - 1) as pair:
                for s in range(2):
                    rest_of_expert(2 * pair + 2 + s, s)

        @block.scalar
        def _(act):
            def round_expert(e, s):
                act.wait_ge(ew_in, 16 * e + 16)
                nc.scalar.copy(ew_hi[:, s], ew_raw[:]).then_inc(ew_hi_out, 1)

            for b in range(B):
                act.wait_ge(var_ready, b + 1)
                nc.scalar.activation(rstd[:, b:b + 1], rstd[:, b:b + 1], ACT.Sqrt).then_inc(root_ready, 1)
                if b in (1, 4):
                    round_expert(b // 3, b // 3)
            act.wait_ge(w_in, 224)
            for n in range(NT):
                k, cols = tile_of(n)
                act.wait_ge(made, B + n + 1)
                nc.scalar.activation(h_t[:, k, cols], ps[:, n % 4, :], ACT.Silu, bias=pwb[:, k:k + 1])\
                   .then_inc(silu_out, 1)
            for n in range(NT):
                k, cols = tile_of(n)
                act.wait_ge(x1_out, n + 1)
                nc.scalar.copy(x1_hi(k, cols), x1_t[:, k, cols]).then_inc(x1_hi_out, 1)
            act.wait_ge(dstep, 2)
            nc.scalar.activation(share[:, 1, :], share[:, 0, :], ACT.Exp).then_inc(astep, 1)

            def silu(pair, s, b):
                n = B * s + b
                act.wait_ge(pre_out, 2 * B * pair + n + 1)
                nc.scalar.activation(act_e[:, n % 2, :], pre[:, n % 2, :], ACT.Silu).then_inc(act_out, 1)

            def silus(pair, last):
                for s in range(2):
                    for b in range(B):
                        silu(pair, s, b)
                        if b == 1 and s == 1 and not last:
                            round_expert(2 * pair + 2, 0)
                if not last:
                    round_expert(2 * pair + 3, 1)

            with act.Fori(0, E // 2 - 1) as pair:
                silus(pair, False)
            silus(E // 2 - 1, True)
            for g in range(G):
                act.wait_ge(ss_made, g + 1)
                nc.scalar.activation(rms[:, g, :], ps[:, 4 + g, :], ACT.Sqrt, scale=1.0 / D).then_inc(astep, 1)
            for g in range(G):
                act.wait_ge(fd_made, g + 1)
                nc.scalar.activation(ff_t[:, g * BANK:(g + 1) * BANK], ps[:, g, :], ACT.Gelu, bias=fdb[:, 0:1])\
                   .then_inc(ff_out, 1)

        @block.vector
        def _(dve):
            def finish_norm(b):
                dve.wait_ge(turned, b + 1)
                dve.tensor_copy(xf_t[:, :, b, K3 - 1:],
                                tp[:, b % 2, :].rearrange("p (k l) -> p k l", k=KC)).then_inc(copied, 1)

            def convolve(n):
                k, cols = tile_of(n)
                bs = slice(BG * (n // KC), BG * (n // KC) + BG)
                c = conv[:, k, cols].rearrange("p (b l) -> p b l", l=L)
                dve.tensor_scalar(c, xf_t[:, k, bs, K3 - 1:], dw[:, k, K3 - 1:K3], dwb[:, k:k + 1], ALU.mult,
                                  ALU.add).then_inc(taps, 1)
                for j in range(K3 - 1):
                    dve.wait_ge(taps, 2 * n + j + 1)
                    dve.scalar_tensor_tensor(out=c, in0=xf_t[:, k, bs, j:j + L], scalar=dw[:, k, j:j + 1], in1=c,
                                             op0=ALU.mult, op1=ALU.add).then_inc(conv_out if j else taps, 1)

            for b in range(B):
                dve.wait_ge(made, b + 1)
                dve.tensor_tensor(xres[:, b, :], xres[:, b, :], ps[:, b % 4, :], ALU.add).then_inc(added, 1)
                dve.wait_ge(added, b + 1)
                if b >= 2:
                    dve.wait_ge(turned, b - 1)
                layer_norm_steps(dve, xres[:, b, :], xn[:, b % 2, :], stats[:, b, :], mv[:, b, :],
                                 rstd[:, b:b + 1], root_ready, var_ready, chain, normed, b, 3 * b)
                if b >= 1:
                    finish_norm(b - 1)
                if b == BG:
                    dve.wait_ge(w_in, 224)
                    dve.wait_ge(padded, 2)
                    dve.wait_ge(copied, BG)
                if b >= BG:
                    convolve(b - BG)
            finish_norm(B - 1)
            dve.wait_ge(copied, B)
            for n in range(KC, NT):
                convolve(n)
            for n in range(NT):
                k, cols = tile_of(n)
                g = n // KC
                dve.wait_ge(silu_out, n + 1)
                dve.tensor_tensor(x1_t[:, k, cols].rearrange("p (b l) -> p b l", l=L),
                                  xf_t[:, k, BG * g:BG * g + BG, K3 - 1:],
                                  h_t[:, k, cols].rearrange("p (b l) -> p b l", l=L), ALU.add).then_inc(x1_out, 1)
            dve.wait_ge(made, B + NT + B)
            dve.tensor_tensor(logits[:], ps[:, 4, 0:B * E].rearrange("p (b e) -> p b e", e=E),
                              rb[:].unsqueeze(1).to_broadcast([P, B, E]), ALU.add).then_inc(lg_out, 1)
            dve.wait_ge(lg_out, 1)
            for b in range(B):
                dve.max(top[:, b, :], logits[:, b, :]).then_inc(lg_out, 1)
            for b in range(B):
                dve.wait_ge(lg_out, b + 2)
                dve.max_index(index[:, b, :], top[:, b, :], logits[:, b, :]).then_inc(lg_out, 1)
            dve.wait_ge(lg_out, 2 * B + 1)
            dve.tensor_copy(chosen[:], index[:]).then_inc(dstep, 1)
            dve.tensor_tensor(share[:, 0, :], top[:, :, 1], top[:, :, 0], ALU.subtract).then_inc(dstep, 1)
            dve.wait_ge(astep, 1)
            dve.tensor_scalar(share[:, 2, :], share[:, 1, :], 1.0, None, ALU.add).then_inc(dstep, 1)
            dve.wait_ge(dstep, 3)
            dve.reciprocal(share[:, 2, :], share[:, 2, :]).then_inc(dstep, 1)
            dve.wait_ge(dstep, 4)
            dve.tensor_tensor(share[:, 3, :], share[:, 1, :], share[:, 2, :], ALU.mult).then_inc(dstep, 1)
            wide = lambda a: a.unsqueeze(2).to_broadcast([P, B, E])
            every = numbers[:].unsqueeze(1).to_broadcast([P, B, E])
            dve.tensor_tensor(route[:], every, wide(chosen[:, :, 0]), ALU.is_equal).then_inc(dstep, 1)
            dve.tensor_tensor(second[:], every, wide(chosen[:, :, 1]), ALU.is_equal).then_inc(dstep, 1)
            dve.wait_ge(dstep, 7)
            dve.tensor_tensor(route[:], route[:], wide(share[:, 2, :]), ALU.mult).then_inc(dstep, 1)
            dve.tensor_tensor(second[:], second[:], wide(share[:, 3, :]), ALU.mult).then_inc(dstep, 1)
            dve.wait_ge(dstep, 9)
            dve.tensor_tensor(route[:], route[:], second[:], ALU.add).then_inc(routed, 1)
            dve.wait_ge(routed, 1)
            dve.wait_ge(zeroed, 1)

            def biased_expert(pair, s, b):
                n = B * s + b
                if b == 0:
                    dve.wait_ge(eb_in[s], 16 * pair + 16)
                dve.wait_ge(ex_made, 2 * B * pair + n + 1)
                dve.tensor_tensor(pre[:, n % 2, :], ps[:, n % 4, :], eb[:, s, :], ALU.add).then_inc(pre_out, 1)

            def accumulate(pair, s, b):
                n = B * s + b
                dve.wait_ge(act_out, 2 * B * pair + n + 1)
                e = 2 * pair + s
                dve.scalar_tensor_tensor(out=comb[:, b, :], in0=act_e[:, n % 2, :], scalar=route[:, b, bass.ds(e, 1)],
                                         in1=comb[:, b, :], op0=ALU.mult, op1=ALU.add).then_inc(comb_out, 1)

            with dve.Fori(0, E // 2) as pair:
                for n in range(2 * B + 1):
                    if n < 2 * B:
                        biased_expert(pair, n // B, n % B)
                    if n >= 1:
                        accumulate(pair, (n - 1) // B, (n - 1) % B)
            for b in range(B):
                dve.wait_ge(turned, B + b + 1)
                dve.tensor_copy(comb_t[:, :, b * L:(b + 1) * L],
                                tp[:, b % 2, :].rearrange("p (k l) -> p k l", k=KC)).then_inc(copied, 1)
            def scale_group(g):
                dve.wait_ge(astep, 2 + g)
                dve.reciprocal(rms[:, g, :], rms[:, g, :]).then_inc(rms_out, 1)
                dve.wait_ge(rms_out, g + 1)
                for n in range(KC * g, KC * g + KC):
                    k, cols = tile_of(n)
                    dve.scalar_tensor_tensor(out=h_t[:, k, cols], in0=hp_t[:, k, cols], scalar=nw[:, k:k + 1],
                                             in1=rms[:, g, :], op0=ALU.mult, op1=ALU.mult).then_inc(h_out, 1)

            for n in range(NT):
                k, cols = tile_of(n)
                dve.wait_ge(m_made, n + 1)
                dve.scalar_tensor_tensor(out=hp_t[:, k, cols], in0=ps[:, n % 4, :], scalar=owb[:, k:k + 1],
                                         in1=x1_t[:, k, cols], op0=ALU.add, op1=ALU.add).then_inc(hp_out, 1)
                dve.wait_ge(hp_out, n + 1)
                dve.tensor_tensor(sq_of(n), hp_t[:, k, cols], hp_t[:, k, cols], ALU.mult).then_inc(sq_out, 1)
                if n == KC + 1:
                    scale_group(0)
            scale_group(1)
            for b in range(B):
                dve.wait_ge(f_made, b + 1)
                dve.wait_ge(biased, b + 1)
                dve.tensor_tensor(xres[:, b, :], xres[:, b, :], ps[:, 2 + b % 4, :], ALU.add).then_inc(fin_out, 1)

        @block.tensor
        def _(pe):
            pe.wait_ge(first_in, 32)

            def turn(src, b, count, ready, value):
                pe.wait_ge(ready, value)
                if count >= 2:
                    pe.wait_ge(copied, count - 1)
                for k in range(KC):
                    mm = pe.transpose(tp[:, b % 2, k * L:(k + 1) * L], src[:, k * P:(k + 1) * P], ident[:])
                mm.then_inc(turned, 1)

            for b in range(B):
                if b >= 4:
                    pe.wait_ge(added, b - 3)
                for c in range(DT):
                    mm = pe.matmul(ps[:, b % 4, :], u[:, c, b * L:(b + 1) * L], wo[:, c, :], start=(c == 0),
                                   stop=(c == DT - 1))
                mm.then_inc(made, 1)
                if b >= 1:
                    turn(xn[:, (b - 1) % 2, :], b - 1, b - 1, normed, b)
            turn(xn[:, (B - 1) % 2, :], B - 1, B - 1, normed, B)
            for n in range(NT):
                k, cols = tile_of(n)
                if n % KC == 0:
                    pe.wait_ge(w_in, 224)
                    pe.wait_ge(conv_out, n + KC)
                if n >= 4:
                    pe.wait_ge(silu_out, n - 3)
                for i in range(KC):
                    mm = pe.matmul(ps[:, n % 4, :], pw[:, i, k * P:(k + 1) * P], conv[:, i, cols], start=(i == 0),
                                   stop=(i == KC - 1))
                mm.then_inc(made, 1)
            pe.wait_ge(x1_out, NT)
            for b in range(B):
                for k in range(KC):
                    mm = pe.matmul(ps[:, 4, b * E:(b + 1) * E], x1_t[:, k, b * L:(b + 1) * L], rw[:, k, :],
                                   start=(k == 0), stop=(k == KC - 1))
                mm.then_inc(made, 1)

            def expert(pair, s, b):
                n = B * s + b
                if b == 0:
                    pe.wait_ge(ew_lo_out, 2 * pair + s + 1)
                for k in range(KC):
                    tokens = slice(b * L, (b + 1) * L)
                    x_hi, x_lo = x1_hi(k, tokens), x1_lo[:, k, tokens]
                    w_hi, w_lo = ew_hi[:, s, k, :], ew_lo[:, s, k, :]
                    pe.matmul(ps[:, n % 4, :], x_hi, w_hi, start=(k == 0), stop=False)
                    pe.matmul(ps[:, n % 4, :], x_hi, w_lo, start=False, stop=False)
                    mm = pe.matmul(ps[:, n % 4, :], x_lo, w_hi, start=False, stop=(k == KC - 1))
                mm.then_inc(ex_made, 1)

            pe.wait_ge(x1_lo_out, NT)
            for n in range(4):
                expert(0, 0, n)
            with pe.Fori(0, E // 2 - 1) as pair:
                for n in range(4, 2 * B + 4):
                    pe.wait_ge(pre_out, 2 * B * pair + n - 3)
                    if n < 2 * B:
                        expert(pair, n // B, n % B)
                    else:
                        expert(pair + 1, 0, n - 2 * B)
            for n in range(4, 2 * B):
                pe.wait_ge(pre_out, 2 * B * (E // 2 - 1) + n - 3)
                expert(E // 2 - 1, n // B, n % B)
            for b in range(B):
                turn(comb[:, b, :], b, B + b, comb_out, (E - 1) * B + b + 1)
            pe.wait_ge(copied, 2 * B)

            def squares(g):
                for k in range(KC):
                    pe.wait_ge(sq_out, KC * g + k + 1)
                    mm = pe.matmul(ps[:, 4 + g, :], ones[:], sq_of(KC * g + k), start=(k == 0), stop=(k == KC - 1))
                mm.then_inc(ss_made, 1)

            for n in range(NT):
                k, cols = tile_of(n)
                if n >= 4:
                    pe.wait_ge(hp_out, n - 3)
                for i in range(KC):
                    mm = pe.matmul(ps[:, n % 4, :], ow[:, i, k * P:(k + 1) * P], comb_t[:, i, cols], start=(i == 0),
                                   stop=(i == KC - 1))
                mm.then_inc(m_made, 1)
                if n == KC:
                    squares(0)
            squares(1)

            def down(g):
                pe.wait_ge(h_out, KC * g + KC)
                for k in range(KC):
                    mm = pe.matmul(ps[:, g, :], fd[:, k, :], h_t[:, k, g * BANK:(g + 1) * BANK], start=(k == 0),
                                   stop=(k == KC - 1))
                mm.then_inc(fd_made, 1)

            down(0)
            for b in range(B):
                if b == 3:
                    down(1)
                if b in (0, BG):
                    pe.wait_ge(ff_out, b // BG + 1)
                if b >= 4:
                    pe.wait_ge(fin_out, b - 3)
                s = 2 + b % 4
                pe.matmul(ps[:, s, :], ff_t[:, b * L:(b + 1) * L], fu[:], start=True, stop=False)
                for k in range(KC):
                    mm = pe.matmul(ps[:, s, k * P:(k + 1) * P], h_t[:, k, b * L:(b + 1) * L], ident[:], start=False,
                                   stop=(k == KC - 1))
                mm.then_inc(f_made, 1)


def layer(nc, a, out):
    q_scratch = nc.dram_tensor("q_scratch", (B, 2, KC, P, L), F32, kind="Internal").ap()
    k_scratch = nc.dram_tensor("k_scratch", (2, KC, P, SKV), F32, kind="Internal").ap()
    bc_scratch = nc.dram_tensor("bc_scratch", (2 * N, T), F32, kind="Internal").ap()
    a_scratch = nc.dram_tensor("a_scratch", (B, P, KC, L), F32, kind="Internal").ap()
    with ExitStack() as ctx:
        st = Stage(nc, ctx, "p")
        wk, wv = ([st.sb(f"{name}_{part}", [P, KC, D], F32R) for part in ("hi", "lo")] for name in ("wk", "wv"))
        c_hi, c_lo = (st.sb(f"c_{part}", [P, 2, KC, BANK], F32R) for part in ("hi", "lo"))
        to_split = [(a["wk"], wk[0][:], wk[1][:]), (a["wv"], wv[0][:], wv[1][:])]
        to_split += [(a["ctx"][0, s], c_hi[:, s], c_lo[:, s]) for s in range(2)]
        queries(nc, a["x"], a["wq"], a["bq"], a["ident"], to_split, q_scratch)
        attention(nc, a["ctx"], wk, wv, c_hi, c_lo, a["bk"], a["bv"], a["ident"], q_scratch, k_scratch, a_scratch)
    with ExitStack() as ctx:
        st = Stage(nc, ctx, "l")
        xres = st.sb("xres", [P, B, D])
        u = st.sb("u", [P, DT, T])
        with nc.sbuf_tensor("l_gate", [P, DT, T], F32) as gate, nc.sbuf_tensor("l_xd", [P, T], F32) as xd:
            mixer_in(nc, a_scratch, a["x"], a["wo"], a["bo"], a["w_in"], a["b_in"], a["w_conv"], a["b_conv"],
                     a["w_x"], a["ident"], xres, u, gate, xd)
            mixer_scan(nc, a["w_dt"], a["a_log"], a["d_skip"], a["ident"], bc_scratch, u, gate, xd)
        experts(nc, a, a["ident"], a["iota"], xres, u, out)


def by_rows(w):
    import numpy as np
    return np.ascontiguousarray(np.asarray(w).reshape(-1, P, w.shape[-1]).transpose(1, 0, 2))


def by_channel(v):
    import numpy as np
    return np.ascontiguousarray(np.asarray(v).reshape(-1, P).T)


def layout(i):
    import numpy as np
    i = {n: np.asarray(v) for n, v in i.items()}
    x, f = "L0_xattn_", "L0_ffn_"
    m = {n: i["L0_attn_" + n] for n in ("w_in", "b_in", "w_conv", "b_conv", "w_x", "w_dt", "A_log", "D", "w_out")}
    return {
        "x": i["x"],
        "ctx": i["ctx_1024"].reshape(B, CH, BANK, KC, P).transpose(0, 1, 4, 3, 2),
        "wq": by_rows(i[x + "Wq"].T), "bq": by_channel(i[x + "bq"]),
        "wk": by_rows(i[x + "Wk"].T), "bk": by_channel(i[x + "bk"]),
        "wv": by_rows(i[x + "Wv"].T), "bv": i[x + "bv"],
        "wo": by_rows(i[x + "Wo"].T), "bo": i[x + "bo"],
        "ident": np.eye(P, dtype=np.float32), "iota": np.arange(E, dtype=np.float32),
        "w_in": by_rows(m["w_in"]), "b_in": by_channel(m["b_in"]),
        "w_conv": by_rows(m["w_conv"].T), "b_conv": by_channel(m["b_conv"]),
        "w_x": by_rows(m["w_x"]), "w_dt": m["w_dt"], "a_log": by_rows(m["A_log"]), "d_skip": by_channel(m["D"]),
        "w_out": by_rows(m["w_out"]),
        "dw": by_rows(i[f + "dw_kernel"].reshape(D, K3)), "dwb": by_channel(i[f + "dw_bias"]),
        "pw": by_rows(i[f + "pw_w"].T), "pwb": by_channel(i[f + "pw_b"]),
        "rw": by_rows(i[f + "router_w"].T), "rb": i[f + "router_b"],
        "ew": i[f + "expert_w"].transpose(0, 2, 1).reshape(E, KC, P, D).transpose(0, 2, 1, 3),
        "eb": i[f + "expert_b"], "ow": by_rows(i[f + "out_w"].T), "owb": by_channel(i[f + "out_b"]),
        "nw": by_channel(i[f + "norm_w"]), "fd": by_rows(i[f + "ff_down_w"].T), "fdb": by_channel(i[f + "ff_down_b"]),
        "fu": i[f + "ff_up_w"].T, "fub": i[f + "ff_up_b"],
    }


def kernel(**inputs):
    import numpy as np
    import concourse.bacc as bacc
    from concourse.bass_utils import run_bass_kernel_spmd

    nc = bacc.Bacc("TRN2", target_bir_lowering=False, num_devices=1)
    arrays = {f"in_{n}": np.ascontiguousarray(a) for n, a in layout(inputs).items()}
    drams = {n[3:]: nc.dram_tensor(n, a.shape, F32, kind="ExternalInput").ap() for n, a in arrays.items()}
    out = nc.dram_tensor("out", (B, L, D), F32, kind="ExternalOutput").ap()
    layer(nc, drams, out)
    got = run_bass_kernel_spmd(nc, [arrays], core_ids=[0])
    return got.results[0]["out"]
```
